# Optimizing a Trainium2 kernel written in Bass

```python
import numpy as np
import jax
import jax.numpy as jnp

def _softmax(x, axis=-1):
    return jax.nn.softmax(x, axis=axis)

def _gelu(x):
    return jax.nn.gelu(x, approximate=True)

def _silu(x):
    return jax.nn.silu(x)

def _sigmoid(x):
    return jax.nn.sigmoid(x)

def _layernorm(x, axis=-1, eps=1e-05):
    m = jnp.mean(x, axis=axis, keepdims=True)
    v = jnp.var(x, axis=axis, keepdims=True)
    return (x - m) / jnp.sqrt(v + eps)

def _scatter_add(tgt, idx, src, axis=0):
    return tgt.at[idx].add(src)

def _segment_sum(src, seg, n):
    return jax.ops.segment_sum(src, seg, n)
kernel_name = 'mk_perceiver_d2_seqx_r4_6a7776'

def setup_inputs(seed: int=0):
    np.random.seed(seed)
    _w = jnp.asarray

    def _rec_inputs():
        import jax
        import jax.numpy as jnp
        _rk = jax.random.key(seed)
        x = -0.0002928 + 1 * jax.random.normal(jax.random.fold_in(_rk, 1), (16, 64, 256), jnp.float32)
        _lenS = 64 - jax.random.randint(jax.random.fold_in(_rk, 7), (16,), 0, max(1, 64 // 4) + 1, jnp.int32)
        _lenS2 = 1024 - jax.random.randint(jax.random.fold_in(_rk, 8), (16,), 0, max(1, 1024 // 4) + 1, jnp.int32)
        _ctx_1024P = jax.random.normal(jax.random.fold_in(_rk, 11), (16, 16, 256), jnp.float32)
        _ctx_1024c = jax.random.dirichlet(jax.random.fold_in(_rk, 511), 0.3 * jnp.ones((16,), jnp.float32), (16, 1024))
        _ctx_1024t = jnp.einsum('bsk,bkd->bsd', _ctx_1024c, _ctx_1024P)
        _ctx_1024t = _ctx_1024t * jax.lax.rsqrt(jnp.mean(jnp.square(_ctx_1024t)) + 1e-12) * 0.953939
        ctx_1024 = -0.000292821 + 1.00034 * (_ctx_1024t + 0.3 * jax.random.normal(jax.random.fold_in(_rk, 611), (16, 1024, 256), jnp.float32))
        return (x, ctx_1024)
    x, ctx_1024 = _rec_inputs()

    def _L0_xattn_setup():
        import jax, jax.numpy as jnp
        import numpy as np
        B, S, D = (2, 512, 256)
        H, HD = (16, 64)
        key = jax.random.key(seed)
        ks = jax.random.split(key, 10)
        scale = 1.0 / np.sqrt(D)
        inputs_q = jax.random.normal(ks[0], (B, S, D), dtype=jnp.float32)
        inputs_kv = inputs_q
        Wq = jax.random.normal(ks[1], (D, H, HD), dtype=jnp.float32) * scale
        Wk = jax.random.normal(ks[2], (D, H, HD), dtype=jnp.float32) * scale
        Wv = jax.random.normal(ks[3], (D, H, HD), dtype=jnp.float32) * scale
        Wo = jax.random.normal(ks[4], (H, HD, D), dtype=jnp.float32) * scale
        bq = jnp.zeros((H, HD), dtype=jnp.float32)
        bk = jnp.zeros((H, HD), dtype=jnp.float32)
        bv = jnp.zeros((H, HD), dtype=jnp.float32)
        bo = jnp.zeros((D,), dtype=jnp.float32)
        return {'inputs_q': inputs_q, 'inputs_kv': inputs_kv, 'Wq': Wq, 'bq': bq, 'Wk': Wk, 'bk': bk, 'Wv': Wv, 'bv': bv, 'Wo': Wo, 'bo': bo}
    _L0_xattn_all = _L0_xattn_setup()
    _L0_xattn_in = {k: v for k, v in _L0_xattn_all.items() if k in ('Wq', 'bq', 'Wk', 'bk', 'Wv', 'bv', 'Wo', 'bo')}
    del _L0_xattn_all

    def _L0_attn_setup():
        import jax, jax.numpy as jnp
        import numpy as np
        import math
        B, S, E = (2, 512, 256)
        H, DC, DR = (16, 64, 128)
        HD = E // H

        def _linear_params(key, din, dout):
            k1, k2 = jax.random.split(key)
            bound = 1.0 / math.sqrt(din)
            w = jax.random.uniform(k1, (din, dout), minval=-bound, maxval=bound, dtype=jnp.float32)
            b = jax.random.uniform(k2, (dout,), minval=-bound, maxval=bound, dtype=jnp.float32)
            return (w, b)

        def _gelu(x):
            return jax.nn.gelu(x, approximate=False)

        def _rope_cos_sin(seq_len, d_rope):
            inv_freq = 1.0 / 10000.0 ** (jnp.arange(0, d_rope, 2, dtype=jnp.float32) / d_rope)
            t = jnp.arange(seq_len, dtype=jnp.float32)
            freqs = t[:, None] * inv_freq[None, :]
            emb = jnp.concatenate([freqs, freqs], axis=-1)
            return (jnp.cos(emb), jnp.sin(emb))

        def _apply_rope(x, cos, sin):
            d = x.shape[-1]
            x1, x2 = (x[..., :d // 2], x[..., d // 2:])
            rot = jnp.concatenate([-x2, x1], axis=-1)
            return x * cos + rot * sin
        key = jax.random.key(seed)
        ks = jax.random.split(key, 10)
        x = jax.random.normal(ks[0], (B, S, E), dtype=jnp.float32)
        wq, bq = _linear_params(ks[1], E, DC)
        wqc, bqc = _linear_params(ks[2], DC, E - DR)
        wqr, bqr = _linear_params(ks[3], E, DR)
        wkv, bkv = _linear_params(ks[4], E, DC)
        wkr, bkr = _linear_params(ks[5], E, DR)
        wkc, bkc = _linear_params(ks[6], DC, E - DR)
        wv, bv = _linear_params(ks[7], DC, E)
        wo, bo = _linear_params(ks[8], E, E)
        return dict(x=x, wq=wq, bq=bq, wqc=wqc, bqc=bqc, wqr=wqr, bqr=bqr, wkv=wkv, bkv=bkv, wkr=wkr, bkr=bkr, wkc=wkc, bkc=bkc, wv=wv, bv=bv, wo=wo, bo=bo)
    _L0_attn_all = _L0_attn_setup()
    _L0_attn_in = {k: v for k, v in _L0_attn_all.items() if k in ('wq', 'bq', 'wqc', 'bqc', 'wqr', 'bqr', 'wkv', 'bkv', 'wkr', 'bkr', 'wkc', 'bkc', 'wv', 'bv', 'wo', 'bo')}
    del _L0_attn_all

    def _L0_ffn_setup():
        import jax, jax.numpy as jnp
        import numpy as np
        INPUT_SIZE = 256
        OUTPUT_SIZE = 256
        key = jax.random.key(seed)
        kx, kt, kp, ktn, kpn = jax.random.split(key, 5)
        x = jax.random.normal(kx, (8, 512, INPUT_SIZE), dtype=jnp.float32)
        theta = jax.random.normal(kt, (INPUT_SIZE, OUTPUT_SIZE), dtype=jnp.float32) * 0.02
        phi = jax.random.normal(kp, (INPUT_SIZE, OUTPUT_SIZE), dtype=jnp.float32) * 0.02
        theta_noise = jax.random.normal(ktn, (INPUT_SIZE, OUTPUT_SIZE), dtype=jnp.float32) * 0.01
        phi_noise = jax.random.normal(kpn, (INPUT_SIZE, OUTPUT_SIZE), dtype=jnp.float32) * 0.01
        return {'x': x, 'theta': theta, 'phi': phi, 'theta_noise': theta_noise, 'phi_noise': phi_noise}
    _L0_ffn_all = _L0_ffn_setup()
    _L0_ffn_in = {k: v for k, v in _L0_ffn_all.items() if k in ('theta', 'phi', 'theta_noise', 'phi_noise')}
    del _L0_ffn_all

    def _L1_xattn_setup():
        import jax, jax.numpy as jnp
        import numpy as np
        DIM = 256
        HEAD_DIM = 64
        NUM_HEADS = 8
        INNER = HEAD_DIM * NUM_HEADS
        ROT_DIM = HEAD_DIM
        ROPE_BASE = 10000.0
        EPS = 1e-05

        def layer_norm(x, g, b):
            mu = jnp.mean(x, axis=-1, keepdims=True)
            var = jnp.var(x, axis=-1, keepdims=True)
            return (x - mu) * jax.lax.rsqrt(var + EPS) * g + b

        def rope_rotate_k(k):
            n = k.shape[1]
            half = ROT_DIM // 2
            inv_freq = 1.0 / ROPE_BASE ** (jnp.arange(0, ROT_DIM, 2, dtype=jnp.float32) / ROT_DIM)
            theta = jnp.arange(n, dtype=jnp.float32)[:, None] * inv_freq[None, :]
            angles = jnp.concatenate([theta, theta], axis=-1)
            cos = jnp.cos(angles)[None, :, None, :].astype(k.dtype)
            sin = jnp.sin(angles)[None, :, None, :].astype(k.dtype)
            k_rope, k_pass = (k[..., :ROT_DIM], k[..., ROT_DIM:])
            neg_half = jnp.concatenate([-k_rope[..., half:], k_rope[..., :half]], axis=-1)
            k_rope = k_rope * cos + neg_half * sin
            return jnp.concatenate([k_rope, k_pass], axis=-1)
        key = jax.random.key(seed)
        ks = jax.random.split(key, 5)
        b, n, m = (8, 2048, 64)
        s = 1.0 / np.sqrt(DIM)
        return {'x': jax.random.normal(ks[0], (b, n, DIM), jnp.float32), 'latents': jax.random.normal(ks[1], (b, m, DIM), jnp.float32), 'gamma_x': jnp.ones((DIM,), jnp.float32), 'beta_x': jnp.zeros((DIM,), jnp.float32), 'gamma_l': jnp.ones((DIM,), jnp.float32), 'beta_l': jnp.zeros((DIM,), jnp.float32), 'Wq': jax.random.normal(ks[2], (DIM, INNER), jnp.float32) * s, 'Wkv': jax.random.normal(ks[3], (DIM, 2 * INNER), jnp.float32) * s, 'Wo': jax.random.normal(ks[4], (INNER, DIM), jnp.float32) * (1.0 / np.sqrt(INNER))}
    _L1_xattn_all = _L1_xattn_setup()
    _L1_xattn_in = {k: v for k, v in _L1_xattn_all.items() if k in ('gamma_x', 'beta_x', 'gamma_l', 'beta_l', 'Wq', 'Wkv', 'Wo')}
    del _L1_xattn_all

    def _L1_attn_setup():
        import jax, jax.numpy as jnp
        import numpy as np
        import math
        INPUT_WIDTH = 256
        KEY_WIDTH = 64
        VALUE_WIDTH = 64
        NUM_HEADS = 16
        key = jax.random.key(seed)
        k_x, k_q, k_k, k_v, k_p = jax.random.split(key, 5)
        n, s = (2, 512)
        scale = 1.0 / math.sqrt(INPUT_WIDTH)
        X = jax.random.normal(k_x, (n, s, INPUT_WIDTH), dtype=jnp.float32)
        Wq = jax.random.uniform(k_q, (INPUT_WIDTH, NUM_HEADS * KEY_WIDTH), jnp.float32, -scale, scale)
        Wk = jax.random.uniform(k_k, (INPUT_WIDTH, NUM_HEADS * KEY_WIDTH), jnp.float32, -scale, scale)
        Wv = jax.random.uniform(k_v, (INPUT_WIDTH, NUM_HEADS * VALUE_WIDTH), jnp.float32, -scale, scale)
        p_scale = 1.0 / math.sqrt(NUM_HEADS * VALUE_WIDTH)
        Wpost = jax.random.uniform(k_p, (NUM_HEADS * VALUE_WIDTH, INPUT_WIDTH), jnp.float32, -p_scale, p_scale)
        return {'X': X, 'Wq': Wq, 'Wk': Wk, 'Wv': Wv, 'Wpost': Wpost}
    _L1_attn_all = _L1_attn_setup()
    _L1_attn_in = {k: v for k, v in _L1_attn_all.items() if k in ('Wq', 'Wk', 'Wv', 'Wpost')}
    del _L1_attn_all

    def _L1_ffn_setup():
        import math
        import jax, jax.numpy as jnp
        import numpy as np
        B, S, D, F, E = (8, 512, 256, 1024, 8)
        CAPACITY_FACTOR = 1.0
        key = jax.random.key(seed)
        k1, k2, k3, k4 = jax.random.split(key, 4)
        x = jax.random.normal(k1, (B, S, D), dtype=jnp.float32)
        Wr = jax.random.normal(k2, (D, E), dtype=jnp.float32) * (1.0 / math.sqrt(D))
        W1 = jax.random.normal(k3, (E, D, F), dtype=jnp.float32) * (1.0 / math.sqrt(D))
        W2 = jax.random.normal(k4, (E, F, D), dtype=jnp.float32) * (1.0 / math.sqrt(F))
        return {'x': x, 'Wr': Wr, 'W1': W1, 'W2': W2}
    _L1_ffn_all = _L1_ffn_setup()
    _L1_ffn_in = {k: v for k, v in _L1_ffn_all.items() if k in ('Wr', 'W1', 'W2')}
    del _L1_ffn_all
    return {'x': x, 'ctx_1024': ctx_1024, 'L0_xattn_Wq': _L0_xattn_in['Wq'], 'L0_xattn_bq': _L0_xattn_in['bq'], 'L0_xattn_Wk': _L0_xattn_in['Wk'], 'L0_xattn_bk': _L0_xattn_in['bk'], 'L0_xattn_Wv': _L0_xattn_in['Wv'], 'L0_xattn_bv': _L0_xattn_in['bv'], 'L0_xattn_Wo': _L0_xattn_in['Wo'], 'L0_xattn_bo': _L0_xattn_in['bo'], 'L0_attn_wq': _L0_attn_in['wq'], 'L0_attn_bq': _L0_attn_in['bq'], 'L0_attn_wqc': _L0_attn_in['wqc'], 'L0_attn_bqc': _L0_attn_in['bqc'], 'L0_attn_wqr': _L0_attn_in['wqr'], 'L0_attn_bqr': _L0_attn_in['bqr'], 'L0_attn_wkv': _L0_attn_in['wkv'], 'L0_attn_bkv': _L0_attn_in['bkv'], 'L0_attn_wkr': _L0_attn_in['wkr'], 'L0_attn_bkr': _L0_attn_in['bkr'], 'L0_attn_wkc': _L0_attn_in['wkc'], 'L0_attn_bkc': _L0_attn_in['bkc'], 'L0_attn_wv': _L0_attn_in['wv'], 'L0_attn_bv': _L0_attn_in['bv'], 'L0_attn_wo': _L0_attn_in['wo'], 'L0_attn_bo': _L0_attn_in['bo'], 'L0_ffn_theta': _L0_ffn_in['theta'], 'L0_ffn_phi': _L0_ffn_in['phi'], 'L0_ffn_theta_noise': _L0_ffn_in['theta_noise'], 'L0_ffn_phi_noise': _L0_ffn_in['phi_noise'], 'L1_xattn_gamma_x': _L1_xattn_in['gamma_x'], 'L1_xattn_beta_x': _L1_xattn_in['beta_x'], 'L1_xattn_gamma_l': _L1_xattn_in['gamma_l'], 'L1_xattn_beta_l': _L1_xattn_in['beta_l'], 'L1_xattn_Wq': _L1_xattn_in['Wq'], 'L1_xattn_Wkv': _L1_xattn_in['Wkv'], 'L1_xattn_Wo': _L1_xattn_in['Wo'], 'L1_attn_Wq': _L1_attn_in['Wq'], 'L1_attn_Wk': _L1_attn_in['Wk'], 'L1_attn_Wv': _L1_attn_in['Wv'], 'L1_attn_Wpost': _L1_attn_in['Wpost'], 'L1_ffn_Wr': _L1_ffn_in['Wr'], 'L1_ffn_W1': _L1_ffn_in['W1'], 'L1_ffn_W2': _L1_ffn_in['W2']}

def reference(x, ctx_1024, L0_xattn_Wq, L0_xattn_bq, L0_xattn_Wk, L0_xattn_bk, L0_xattn_Wv, L0_xattn_bv, L0_xattn_Wo, L0_xattn_bo, L0_attn_wq, L0_attn_bq, L0_attn_wqc, L0_attn_bqc, L0_attn_wqr, L0_attn_bqr, L0_attn_wkv, L0_attn_bkv, L0_attn_wkr, L0_attn_bkr, L0_attn_wkc, L0_attn_bkc, L0_attn_wv, L0_attn_bv, L0_attn_wo, L0_attn_bo, L0_ffn_theta, L0_ffn_phi, L0_ffn_theta_noise, L0_ffn_phi_noise, L1_xattn_gamma_x, L1_xattn_beta_x, L1_xattn_gamma_l, L1_xattn_beta_l, L1_xattn_Wq, L1_xattn_Wkv, L1_xattn_Wo, L1_attn_Wq, L1_attn_Wk, L1_attn_Wv, L1_attn_Wpost, L1_ffn_Wr, L1_ffn_W1, L1_ffn_W2):
    import jax
    import jax.numpy as jnp

    def _L0_xattn_ref(inputs_q, inputs_kv, Wq, bq, Wk, bk, Wv, bv, Wo, bo):
        import jax, jax.numpy as jnp
        import numpy as np
        B, S, D = (2, 512, 256)
        H, HD = (16, 64)
        q = jnp.einsum('bsd,dhe->bshe', inputs_q, Wq) + bq
        k = jnp.einsum('bsd,dhe->bshe', inputs_kv, Wk) + bk
        v = jnp.einsum('bsd,dhe->bshe', inputs_kv, Wv) + bv
        q = q / jnp.sqrt(jnp.asarray(HD, dtype=q.dtype))
        scores = jnp.einsum('bqhd,bkhd->bhqk', q, k)
        weights = jax.nn.softmax(scores, axis=-1)
        ctx = jnp.einsum('bhqk,bkhd->bqhd', weights, v)
        out = jnp.einsum('bqhd,hde->bqe', ctx, Wo) + bo
        return out

    def _L0_attn_ref(x, wq, bq, wqc, bqc, wqr, bqr, wkv, bkv, wkr, bkr, wkc, bkc, wv, bv, wo, bo):
        import jax, jax.numpy as jnp
        import numpy as np
        import math
        B, S, E = (2, 512, 256)
        H, DC, DR = (16, 64, 128)
        HD = E // H

        def _linear_params(key, din, dout):
            k1, k2 = jax.random.split(key)
            bound = 1.0 / math.sqrt(din)
            w = jax.random.uniform(k1, (din, dout), minval=-bound, maxval=bound, dtype=jnp.float32)
            b = jax.random.uniform(k2, (dout,), minval=-bound, maxval=bound, dtype=jnp.float32)
            return (w, b)

        def _gelu(x):
            return jax.nn.gelu(x, approximate=False)

        def _rope_cos_sin(seq_len, d_rope):
            inv_freq = 1.0 / 10000.0 ** (jnp.arange(0, d_rope, 2, dtype=jnp.float32) / d_rope)
            t = jnp.arange(seq_len, dtype=jnp.float32)
            freqs = t[:, None] * inv_freq[None, :]
            emb = jnp.concatenate([freqs, freqs], axis=-1)
            return (jnp.cos(emb), jnp.sin(emb))

        def _apply_rope(x, cos, sin):
            d = x.shape[-1]
            x1, x2 = (x[..., :d // 2], x[..., d // 2:])
            rot = jnp.concatenate([-x2, x1], axis=-1)
            return x * cos + rot * sin
        b, s, _ = x.shape
        cq = _gelu(x @ wq + bq)
        q_c = cq @ wqc + bqc
        q_r = x @ wqr + bqr
        ckv = _gelu(x @ wkv + bkv)
        k_r = x @ wkr + bkr
        k_c = ckv @ wkc + bkc
        v = (ckv @ wv + bv).reshape(b, s, H, HD).transpose(0, 2, 1, 3)
        cos, sin = _rope_cos_sin(s, DR)
        q_r = _apply_rope(q_r, cos, sin)
        k_r = _apply_rope(k_r, cos, sin)
        q = _gelu(jnp.concatenate([q_c, q_r], axis=-1)).reshape(b, s, H, HD).transpose(0, 2, 1, 3)
        k = _gelu(jnp.concatenate([k_c, k_r], axis=-1)).reshape(b, s, H, HD).transpose(0, 2, 1, 3)
        scale = 1.0 / math.sqrt(HD)
        scores = jnp.einsum('bhqd,bhkd->bhqk', q, k) * scale
        causal = jnp.triu(jnp.ones((s, s), dtype=bool), k=1)
        scores = jnp.where(causal[None, None], -jnp.inf, scores)
        attn = jax.nn.softmax(scores, axis=-1)
        out = jnp.einsum('bhqk,bhkd->bhqd', attn, v)
        out = out.transpose(0, 2, 1, 3).reshape(b, s, E)
        return out @ wo + bo

    def _L0_ffn_ref(x, theta, phi, theta_noise, phi_noise):
        import jax, jax.numpy as jnp
        import numpy as np
        INPUT_SIZE = 256
        OUTPUT_SIZE = 256
        real = jnp.einsum('bti,io->bto', x, jnp.cos(theta + theta_noise))
        imag = jnp.einsum('bti,io->bto', x, jnp.sin(phi + phi_noise))
        return jnp.sqrt(real * real + imag * imag)

    def _L1_xattn_ref(x, latents, gamma_x, beta_x, gamma_l, beta_l, Wq, Wkv, Wo):
        import jax, jax.numpy as jnp
        import numpy as np
        DIM = 256
        HEAD_DIM = 64
        NUM_HEADS = 8
        INNER = HEAD_DIM * NUM_HEADS
        ROT_DIM = HEAD_DIM
        ROPE_BASE = 10000.0
        EPS = 1e-05

        def layer_norm(x, g, b):
            mu = jnp.mean(x, axis=-1, keepdims=True)
            var = jnp.var(x, axis=-1, keepdims=True)
            return (x - mu) * jax.lax.rsqrt(var + EPS) * g + b

        def rope_rotate_k(k):
            n = k.shape[1]
            half = ROT_DIM // 2
            inv_freq = 1.0 / ROPE_BASE ** (jnp.arange(0, ROT_DIM, 2, dtype=jnp.float32) / ROT_DIM)
            theta = jnp.arange(n, dtype=jnp.float32)[:, None] * inv_freq[None, :]
            angles = jnp.concatenate([theta, theta], axis=-1)
            cos = jnp.cos(angles)[None, :, None, :].astype(k.dtype)
            sin = jnp.sin(angles)[None, :, None, :].astype(k.dtype)
            k_rope, k_pass = (k[..., :ROT_DIM], k[..., ROT_DIM:])
            neg_half = jnp.concatenate([-k_rope[..., half:], k_rope[..., :half]], axis=-1)
            k_rope = k_rope * cos + neg_half * sin
            return jnp.concatenate([k_rope, k_pass], axis=-1)
        b, n, _ = x.shape
        m = latents.shape[1]
        h, d = (NUM_HEADS, HEAD_DIM)
        scale = d ** (-0.5)
        xn = layer_norm(x, gamma_x, beta_x)
        ln = layer_norm(latents, gamma_l, beta_l)
        q = (ln @ Wq).reshape(b, m, h, d)
        kv_x = xn @ Wkv
        k_x, v_x = (kv_x[..., :INNER], kv_x[..., INNER:])
        kv_l = ln @ Wkv
        k_l, v_l = (kv_l[..., :INNER], kv_l[..., INNER:])
        k_x = k_x.reshape(b, n, h, d)
        v_x = v_x.reshape(b, n, h, d)
        k_x = rope_rotate_k(k_x)
        q = jnp.transpose(q, (0, 2, 1, 3)) * scale
        k_x = jnp.transpose(k_x, (0, 2, 1, 3))
        v_x = jnp.transpose(v_x, (0, 2, 1, 3))
        k_l = jnp.transpose(k_l.reshape(b, m, h, d), (0, 2, 1, 3))
        v_l = jnp.transpose(v_l.reshape(b, m, h, d), (0, 2, 1, 3))
        k = jnp.concatenate([k_x, k_l], axis=2)
        v = jnp.concatenate([v_x, v_l], axis=2)
        sim = jnp.einsum('bhid,bhjd->bhij', q, k)
        attn = jax.nn.softmax(sim, axis=-1)
        out = jnp.einsum('bhij,bhjd->bhid', attn, v)
        out = jnp.transpose(out, (0, 2, 1, 3)).reshape(b, m, INNER)
        return out @ Wo

    def _L1_attn_ref(X, Wq, Wk, Wv, Wpost):
        import jax, jax.numpy as jnp
        import numpy as np
        import math
        INPUT_WIDTH = 256
        KEY_WIDTH = 64
        VALUE_WIDTH = 64
        NUM_HEADS = 16
        n, s, _ = X.shape
        Q = (X @ Wq).reshape(n, s, NUM_HEADS, KEY_WIDTH)
        K = (X @ Wk).reshape(n, s, NUM_HEADS, KEY_WIDTH)
        V = (X @ Wv).reshape(n, s, NUM_HEADS, VALUE_WIDTH)
        inv_sqrt_d = 1.0 / math.sqrt(KEY_WIDTH)
        raw_attn = jnp.einsum('bshe,bthe->bsth', Q, K * inv_sqrt_d)
        attn = jax.nn.softmax(raw_attn, axis=2)
        A = jnp.einsum('bsth,bthe->bshe', attn, V).reshape(n, s, NUM_HEADS * VALUE_WIDTH)
        A = jax.nn.gelu(A, approximate=False)
        P = A @ Wpost
        return X + P

    def _L1_ffn_ref(x, Wr, W1, W2):
        import math
        import jax, jax.numpy as jnp
        import numpy as np
        B, S, D, F, E = (8, 512, 256, 1024, 8)
        CAPACITY_FACTOR = 1.0
        b, s, d = x.shape
        t = b * s
        cap = max(math.ceil(t * CAPACITY_FACTOR / E), 1)
        xf = x.reshape(t, d)
        probs = jax.nn.softmax(xf.astype(jnp.float32) @ Wr, axis=-1)
        eidx = jnp.argmax(probs, axis=-1)
        p_tok = jnp.take_along_axis(probs, eidx[:, None], axis=1)[:, 0]
        onehot = jax.nn.one_hot(eidx, E, dtype=jnp.int32)
        rank_all = jnp.cumsum(onehot, axis=0) - onehot
        rank = jnp.take_along_axis(rank_all, eidx[:, None], axis=1)[:, 0]
        keep = rank < cap
        slot = jnp.where(keep, rank, cap)
        dispatch = jnp.zeros((E, cap + 1), dtype=jnp.int32).at[eidx, slot].set(jnp.arange(t, dtype=jnp.int32))
        valid = jnp.zeros((E, cap + 1), dtype=bool).at[eidx, slot].set(keep)
        dispatch = dispatch[:, :cap]
        valid = valid[:, :cap]
        xe = xf[dispatch]
        h = jnp.maximum(jnp.einsum('ecd,edf->ecf', xe, W1), 0.0)
        ye = jnp.einsum('ecf,efd->ecd', h, W2)
        pe = p_tok[dispatch]
        ye = ye * (pe * valid.astype(ye.dtype))[:, :, None]
        y = jnp.zeros((t, d), dtype=x.dtype).at[dispatch.reshape(-1)].add(ye.reshape(E * cap, d).astype(x.dtype))
        return y.reshape(b, s, d)
    x = x + _L0_xattn_ref(_layernorm(x, axis=-1), ctx_1024, L0_xattn_Wq, L0_xattn_bq, L0_xattn_Wk, L0_xattn_bk, L0_xattn_Wv, L0_xattn_bv, L0_xattn_Wo, L0_xattn_bo)
    x = x + _L0_attn_ref(_layernorm(x, axis=-1), L0_attn_wq, L0_attn_bq, L0_attn_wqc, L0_attn_bqc, L0_attn_wqr, L0_attn_bqr, L0_attn_wkv, L0_attn_bkv, L0_attn_wkr, L0_attn_bkr, L0_attn_wkc, L0_attn_bkc, L0_attn_wv, L0_attn_bv, L0_attn_wo, L0_attn_bo)
    x = x + _L0_ffn_ref(_layernorm(x, axis=-1), L0_ffn_theta, L0_ffn_phi, L0_ffn_theta_noise, L0_ffn_phi_noise)
    x = x + _L1_xattn_ref(ctx_1024, _layernorm(x, axis=-1), L1_xattn_gamma_x, L1_xattn_beta_x, L1_xattn_gamma_l, L1_xattn_beta_l, L1_xattn_Wq, L1_xattn_Wkv, L1_xattn_Wo)
    x = x + _L1_attn_ref(_layernorm(x, axis=-1), L1_attn_Wq, L1_attn_Wk, L1_attn_Wv, L1_attn_Wpost)
    x = x + _L1_ffn_ref(_layernorm(x, axis=-1), L1_ffn_Wr, L1_ffn_W1, L1_ffn_W2)
    return x

_drawn_inputs = setup_inputs


def setup_inputs(seed=0):
    import zlib

    import numpy as np

    out = dict(_drawn_inputs(seed))
    spreads = {'L0_xattn_bq': (0.0, 0.1),
     'L0_xattn_bk': (0.0, 2.0),
     'L0_xattn_bv': (0.0, 0.1),
     'L0_xattn_bo': (0.0, 0.1),
     'L1_xattn_gamma_x': (1.0, 0.2),
     'L1_xattn_beta_x': (0.0, 0.1),
     'L1_xattn_gamma_l': (1.0, 0.6),
     'L1_xattn_beta_l': (0.0, 0.684)}
    factors = {'L0_attn_wq': 8.0,
     'L0_attn_bq': 157.818,
     'L0_attn_wqc': 8.0,
     'L0_attn_bqc': 195.629,
     'L0_attn_wqr': 8.0,
     'L0_attn_bqr': 64.0,
     'L0_attn_bkv': 8.0,
     'L0_attn_wkr': 8.0,
     'L0_attn_bkr': 175.711,
     'L0_attn_wkc': 8.0,
     'L0_attn_bkc': 30.478,
     'L0_ffn_theta': 8.0,
     'L0_ffn_theta_noise': 8.0,
     'L1_attn_Wq': 8.0,
     'L1_attn_Wk': 8.0}
    for name, (base, spread) in spreads.items():
        noise = np.random.default_rng([zlib.crc32(name.encode()), seed]).standard_normal(out[name].shape)
        drawn = base * np.exp(spread * noise) if base else spread * noise
        out[name] = jnp.asarray(drawn.astype(out[name].dtype))
    for name, factor in factors.items():
        out[name] = (out[name] * factor).astype(out[name].dtype)
    return out
```

```python
from contextlib import ExitStack, contextmanager

import numpy as np

import concourse.bass as bass
from concourse import mybir

F32 = mybir.dt.float32
ACT = mybir.ActivationFunctionType
ALU = mybir.AluOpType
AX = mybir.AxisListType

P = 128
B, S, D = 16, 64, 256
T = B * S // P
BT = P // S
KD = D // P
CTX = 1024
KC = CTX // P
BANK = 512
HALF = CTX // BANK
EPS = 1e-5
MASKED = -1.0e30


class Mark:

    def __init__(self, line):
        self.line, self.n, self.base, self.per, self.epoch = line, line.n, line.total, line.per, line.epoch

    def at(self, iteration):
        return (iteration * self.per + (self.base + self.n)) * self.line.step


class Line:

    def __init__(self, nc, ctx, name, step=1):
        self.name, self.sem = name, ctx.enter_context(nc.semaphore(name))
        self.step, self.total, self.epoch, self.i, self.per, self.n = step, 0, 0, None, 0, 0

    def __call__(self, instruction):
        instruction.then_inc(self.sem, self.step)
        self.n += 1
        return Mark(self)

    def start(self, per, i):
        self.total, self.n, self.per, self.i, self.epoch = self.total + self.n, 0, per, i, self.epoch + 1

    def stop(self, times):
        assert self.n == self.per, f"{self.name}: {self.n} counts in the loop, {self.per} declared"
        self.total, self.n, self.per, self.i = self.total + self.per * times, 0, 0, None
        self.epoch += 1

    def before(self):
        if self.i is None:
            return (self.total + self.n) * self.step
        return self.i * (self.per * self.step) + self.total * self.step


def wait(engine, *marks):
    for m in marks:
        if m is None:
            continue
        line = m.line
        if m.epoch == line.epoch and line.i is not None:
            engine.wait_ge(line.sem, line.i * (line.per * line.step) + (line.total + m.n) * line.step)
        elif m.epoch == line.epoch:
            engine.wait_ge(line.sem, (line.total + m.n) * line.step)
        else:
            engine.wait_ge(line.sem, line.total * line.step)


def wait_before(engine, *lines):
    for line in lines:
        engine.wait_ge(line.sem, line.before())



def program(nc, g, out):
    with ExitStack() as ctx:
        build(nc, ctx, g, out)


def build(nc, ctx, g, out):
    pe, dve, act, pool, sp = nc.tensor, nc.vector, nc.scalar, nc.gpsimd, nc.sync

    def sb(name, shape, stack=ctx, dt=F32):
        return stack.enter_context(nc.sbuf_tensor(name, shape, dt))

    PE, DVE, AC, PL = (Line(nc, ctx, n) for n in ("s_pe", "s_dve", "s_act", "s_pool"))
    engine_of = {PE: pe.engine, DVE: dve.engine, AC: act.engine, PL: pool.engine}

    @contextmanager
    def tiles(times, **per):
        lines = {"pe": PE, "dve": DVE, "act": AC, "pool": PL}
        with nc.Fori(0, times, engines=tuple(engine_of[lines[k]] for k in per)) as i:
            for k, n in per.items():
                lines[k].start(n, i)
            yield i
        for k in per:
            lines[k].stop(times)

    def meet(*engines):
        for e in engines or (pe, dve, act, pool, sp):
            wait_before(e, *(l for l in (PE, DVE, AC, PL) if l.total + l.n))

    x = sb("x", [P, T, D])
    xn = sb("xn", [P, T, D])
    ident = sb("ident", [P, P])
    ones = sb("ones", [P, P])
    big = sb("big", [P, 8192])
    ctx_buf = [sb(f"ctx_buf{b}", [P, KC, D]) for b in range(BT)]
    ctxT_buf = [sb(f"ctxT_buf{b}", [P, KD, CTX]) for b in range(BT)]
    st6 = sb("st6", [P, T, 6])
    mv = sb("mv", [P, T, 2])
    rstd = sb("rstd", [P, T])
    sd = sb("sd", [P, T])
    banks = [ctx.enter_context(nc.psum_tensor(f"bank{n}", [P, 2 * BANK], F32)) for n in range(4)]

    def bank(n):
        return banks[n // 2][:, (n % 2) * BANK:(n % 2 + 1) * BANK]

    def stream(name):
        return Line(nc, ctx, name, 16)

    d_x, d_w1, d_w2, d_w3, d_w4, d_w5, d_w6, d_out = (
        stream(n) for n in ("d_x", "d_w1", "d_w2", "d_w3", "d_w4", "d_w5", "d_w6", "d_out"))
    d_ctx = [stream(f"d_ctx{b}") for b in range(BT)]
    d_ctx4 = [stream(f"d_ctx4_{b}") for b in range(BT)]
    H1, M1 = 16, 8
    Wq1, WkT1, Wv1, Wo1 = (big[:, n * 2048:(n + 1) * 2048] for n in range(4))
    Wq1 = Wq1.rearrange("p (k n) -> p k n", k=KD)
    WkT1 = WkT1.rearrange("p (m d) -> p m d", m=M1)
    Wv1 = Wv1.rearrange("p (k n) -> p k n", k=KD)
    Wo1 = Wo1.rearrange("p (m d) -> p m d", m=M1)
    bq1, bk1, bv1 = (sb(n, [P, M1]) for n in ("bq1", "bk1", "bv1"))
    bo1 = sb("bo1", [P, D])

    def rows(name):
        return g[name].rearrange("(k p) n -> p k n", p=P)

    def everywhere(name):
        return g[name].partition_broadcast(P)

    d_x(sp.dma_start(x[:, :, :], g["x"].rearrange("(t p) d -> p t d", p=P)))
    d_w1(sp.dma_start(Wq1, rows("L0_xattn_Wq")))
    d_w1(sp.dma_start(WkT1, rows("L0_xattn_WkT")))
    for dst, name in ((bq1, "L0_xattn_bq"), (bk1, "L0_xattn_bk"), (bv1, "L0_xattn_bv")):
        d_w1(act.dma_start(dst[:, :], g[name]))
    d_w1(act.dma_start(bo1[:, :], everywhere("L0_xattn_bo")))
    ctx_rows = g["ctx_1024"].rearrange("(t b) (k p) d -> t b p k d", b=BT, p=P)
    ctxT_rows = g["ctx_T"].rearrange("(t b) (k p) c -> t b p k c", b=BT, p=P)

    def load_ctx(b, t):
        src = [rows_[bass.ds(t, 1), b].rearrange("a p k n -> (a p) k n") for rows_ in (ctxT_rows, ctx_rows)]
        d_ctx[b](sp.dma_start(ctxT_buf[b][:, :, :], src[0]))
        d_ctx[b](sp.dma_start(ctx_buf[b][:, :, :], src[1]))

    def load_ctx4(b, t):
        src = ctx_rows[bass.ds(t, 1), b].rearrange("a p k n -> (a p) k n")
        d_ctx4[b](sp.dma_start(ctx_buf[b][:, :, :], src))

    load_ctx(0, 0)
    d_w1(sp.dma_start(Wv1, rows("L0_xattn_Wv")))
    d_w1(sp.dma_start(Wo1, rows("L0_xattn_Wo")))
    load_ctx(1, 0)

    PL(pool.memset(ones[:, :], 1.0))
    m = PL(pool.memset(ident[:, :], 0.0))
    wait(pool, m)
    m_ident = PL(pool.affine_select(out=ident[:, :], in_=ident[:, :], compare_op=ALU.not_equal, fill=1.0, base=0,
                                    pattern=[[-1, P]], channel_multiplier=1))
    wait(pe, m_ident)
    PE(pe.matmul(bank(7)[:, 0:P], ones[:, :], ident[:, :], start=True, stop=True))

    def moments(src):
        with tiles(T, dve=1) as i:
            DVE(dve.bn_stats(st6[:, i, :], src[:, i, :]))
        wait_before(dve, DVE)
        for t in range(T):
            m = DVE(dve.bn_aggr(mv[:, t, :], st6[:, t, :]))
        wait(dve, m)
        m = DVE(dve.tensor_scalar(sd[:, :], mv[:, :, 1], EPS, None, ALU.add))
        wait(act, m)
        m = AC(act.activation(sd[:, :], sd[:, :], ACT.Sqrt))
        wait(dve, m)
        wait(dve, DVE(dve.reciprocal(rstd[:, :], sd[:, :])))

    def normed(dst, src, i):
        return DVE(dve.tensor_scalar(dst, src[:, bass.ds(i, 1), :].rearrange("p a d -> p (a d)"),
                                     mv[:, bass.ds(i, 1), 0], rstd[:, bass.ds(i, 1)], ALU.subtract, ALU.mult))

    mask = sb("mask", [P, 2, P])
    d_w2(act.dma_start(mask[:, :, :], g["masks"].rearrange("m p k -> p m k")))

    def transposed_tile(src, dst, into):
        for k in range(KD):
            m = pe.transpose(into[:, k * P:(k + 1) * P], src[:, k * P:(k + 1) * P], ident[:, :])
        m = PE(m)
        wait(dve, m)
        return DVE(dve.tensor_copy(dst[:, :, :], into[:, 0:D].rearrange("p (k n) -> p k n", k=KD)))

    def tile_softmax(m_scores, ps, sm, small, scale, which):
        wait(dve, m_scores)
        m = DVE(dve.scalar_tensor_tensor(sm[:, :, :], ps[:, :].rearrange("p (h k) -> p h k", h=8), scale,
                                         mask[:, which:which + 1, :].broadcast_to([P, 8, P]), ALU.mult, ALU.add))
        yield m
        wait(dve, m)
        m = DVE(dve.tensor_reduce(small[:, 0, :], sm[:, :, :], AX.X, ALU.max))
        wait(dve, m)
        m = DVE(dve.tensor_tensor(sm[:, :, :], sm[:, :, :], small[:, 0, :].unsqueeze(2).broadcast_to([P, 8, P]),
                                  ALU.subtract))
        wait(act, m)
        m = AC(act.activation(sm[:, :, :], sm[:, :, :], ACT.Exp))
        yield m
        wait(dve, m)
        m = DVE(dve.tensor_reduce(small[:, 0, :], sm[:, :, :], AX.X, ALU.add))
        wait(dve, m)
        m = DVE(dve.reciprocal(small[:, 1, :], small[:, 0, :]))
        yield m

    def tile_transposes(m_prob, ps, sm, smT):
        wait(pe, m_prob)
        marks = []
        for hf, (line, e) in enumerate(((DVE, dve), (AC, act))):
            for h in range(4 * hf, 4 * hf + 4):
                m = pe.transpose(ps[:, h * P:(h + 1) * P], sm[:, h, :], ident[:, :])
            m = PE(m)
            wait(e, m)
            dst = smT[:, 4 * hf:4 * hf + 4, :]
            src = ps[:, 4 * hf * P:4 * (hf + 1) * P].rearrange("p (h q) -> p h q", h=4)
            marks.append(line(e.tensor_copy(dst, src) if e is dve else e.activation(dst, src, ACT.Copy)))
        return marks

    def interleave(*bodies):
        left = list(bodies)
        while left:
            left = [b for b in left if next(b, "end") != "end"]

    U2 = 2

    HD2, DC = 16, 64
    w_qkv2 = sb("w_qkv2", [P, KD, P])
    b_qkv2 = sb("b_qkv2", [P, 1])
    w_c2 = sb("w_c2", [P, 2, P])
    w_r2 = sb("w_r2", [P, 4, KD, P])
    b_c2 = sb("b_c2", [P, 2])
    b_r2 = sb("b_r2", [P, 4])
    w_v2 = sb("w_v2", [P, D])
    b_v2 = sb("b_v2", [P, D])
    w_o2 = sb("w_o2", [P, KD, D])
    b_o2 = sb("b_o2", [P, D])
    rope2 = sb("rope2", [P, 2, P])
    head2 = sb("head2", [P, 8])
    HF = P // 2
    m = PL(pool.memset(w_c2[:, :, :], 0.0))
    m = PL(pool.memset(w_v2[:, :], 0.0))
    wait(act, m)
    d_w2(act.dma_start(w_qkv2[:, :, 0:DC], rows("L0_attn_wq")))
    d_w2(act.dma_start(w_qkv2[:, :, DC:2 * DC], rows("L0_attn_wkv")))
    d_w2(act.dma_start(b_qkv2[0:DC, :], g["L0_attn_bq"].unsqueeze(1)))
    d_w2(act.dma_start(b_qkv2[DC:2 * DC, :], g["L0_attn_bkv"].unsqueeze(1)))
    d_w2(act.dma_start(w_c2[0:DC, 0, :], g["L0_attn_wqc"]))
    d_w2(act.dma_start(w_c2[DC:2 * DC, 1, :], g["L0_attn_wkc"]))
    d_w2(act.dma_start(w_v2[DC:2 * DC, :], g["L0_attn_wv"]))
    d_w2(act.dma_start(w_o2[:, :, :], rows("L0_attn_wo")))
    for n, (w, v) in enumerate((("L0_attn_wqr", "L0_attn_bqr"), ("L0_attn_wkr", "L0_attn_bkr"))):
        d_w2(act.dma_start(b_c2[:, n:n + 1], g[("L0_attn_bqc", "L0_attn_bkc")[n]].unsqueeze(1)))
        d_w2(act.dma_start(w_r2[:, 2 * n, :, :], rows(w)))
        d_w2(act.dma_start(b_r2[:, 2 * n:2 * n + 1], g[v].unsqueeze(1)))
        for h in range(2):
            to, fro = slice(h * HF, (h + 1) * HF), slice((1 - h) * HF, (2 - h) * HF)
            d_w2(act.dma_start(w_r2[:, 2 * n + 1, :, to], rows(w)[:, :, fro]))
            d_w2(act.dma_start(b_r2[to, 2 * n + 1:2 * n + 2], g[v][fro].unsqueeze(1)))
    d_w2(act.dma_start(b_v2[:, :], everywhere("L0_attn_bv")))
    d_w2(act.dma_start(b_o2[:, :], everywhere("L0_attn_bo")))
    d_w2(act.dma_start(rope2[:, :, :], g["rope2"].rearrange("c p t -> p c t")))
    d_w2(act.dma_start(head2[:, :], g["head2"]))

    trig3 = sb("trig3", [P, 2, KD, D])
    noise3, turns3 = (xn[:, h * 4:h * 4 + 4, :].rearrange("p (n k) d -> p n k d", n=2) for h in range(2))
    for n, name in enumerate(("theta", "phi")):
        d_w3(act.dma_start(trig3[:, n, :, :], rows("L0_ffn_" + name)))
        d_w3(act.dma_start(noise3[:, n, :, :], rows(f"L0_ffn_{name}_noise")))
    wait_before(dve, d_w3)
    a3, t3 = trig3[:, :, :, :], turns3
    wait(dve, DVE(dve.tensor_tensor(a3, a3, noise3[:, :, :, :], ALU.add)))
    ROUND = 1.5 * 2.0 ** 23
    wait(dve, DVE(dve.tensor_scalar(t3, a3, 1.0 / (2.0 * np.pi), ROUND, ALU.mult, ALU.add)))
    wait(dve, DVE(dve.tensor_scalar(t3, t3, ROUND, None, ALU.subtract)))
    high = 6.28125
    for part in (high, 2.0 * np.pi - high):
        wait(dve, DVE(dve.scalar_tensor_tensor(a3, t3, -float(part), a3, ALU.mult, ALU.add)))
    PI = 3.1415925
    wait(dve, DVE(dve.tensor_scalar(a3, a3, -PI, PI, ALU.max, ALU.min)))
    c3 = trig3[:, 0, :, :]
    wait(dve, DVE(dve.scalar_tensor_tensor(c3, c3, -1.0, c3, ALU.mult, ALU.min)))
    m = DVE(dve.tensor_scalar(c3, c3, float(np.pi / 2), None, ALU.add))
    wait(act, m)
    AC(act.activation(a3, a3, ACT.Sin))

    H4, M4 = 8, 4
    w_q4 = sb("w_q4", [P, 2, KD, M4 * P])
    w_k4 = sb("w_k4", [P, KD, M4 * P])
    w_v4 = sb("w_v4", [P, KD, M4 * P])
    w_o4 = sb("w_o4", [P, M4, D])
    gb4 = sb("gb4", [P, 4, D])
    rope4 = sb("rope4", [P, 2, CTX])
    turn4 = sb("turn4", [P, 2])
    stats_c = sb("stats_c", [P, B * KC, 6])
    mean_c = sb("mean_c", [P, (B + BT) * KC])
    rstd_c = sb("rstd_c", [P, (B + BT) * KC])
    INNER = M4 * P
    d_w4(sp.dma_start(w_q4[:, 0, :, :], rows("L1_xattn_Wq")))
    d_w4(sp.dma_start(w_q4[:, 1, :, :], rows("L1_xattn_Wq_turned")))
    d_w4(sp.dma_start(w_k4[:, :, :], rows("L1_xattn_Wkv")[:, :, 0:INNER]))
    d_w4(sp.dma_start(w_v4[:, :, :], rows("L1_xattn_Wkv")[:, :, INNER:2 * INNER]))
    d_w4(sp.dma_start(w_o4[:, :, :], rows("L1_xattn_Wo")))
    for n, name in enumerate(("gamma_x", "beta_x", "gamma_l", "beta_l")):
        d_w4(sp.dma_start(gb4[:, n, :], everywhere("L1_xattn_" + name)))
    d_w4(sp.dma_start(rope4[:, :, :], g["rope4"].rearrange("c p t -> p c t")))
    d_w4(sp.dma_start(turn4[:, :], g["turn4"]))

    M5 = 8
    E, F, CAP = 8, 1024, 128
    Wq5, Wk5, Wv5, Wo5 = (big[:, n * 2048:(n + 1) * 2048] for n in range(4))
    Wq5, Wk5, Wv5 = (w.rearrange("p (k n) -> p k n", k=KD) for w in (Wq5, Wk5, Wv5))
    Wo5 = Wo5.rearrange("p (m d) -> p m d", m=M5)
    w_r6 = sb("w_r6", [P, KD, E])
    count6 = sb("count6", [P, 2 * E])
    d_w6(sp.dma_start(w_r6[:, :, :], rows("L1_ffn_Wr")))
    d_w6(sp.dma_start(count6[:, :], g["count6"]))
    w1_ring = [ctxT_buf[0][:, :, :], ctxT_buf[1][:, :, :]] + \
        [big[:, 4096 * n:4096 * n + 2048].rearrange("p (k f) -> p k f", k=KD) for n in range(2)]
    w2_ring = [ctx_buf[0][:, :, :], ctx_buf[1][:, :, :]] + \
        [big[:, 4096 * n + 2048:4096 * n + 4096].rearrange("p (f d) -> p f d", d=D) for n in range(2)]
    d_e = stream("d_e")

    def load_expert(n):
        d_e(sp.dma_start(w1_ring[n % 4], g["L1_ffn_W1"][n].rearrange("(k p) f -> p k f", p=P)))
        d_e(sp.dma_start(w2_ring[n % 4], g["L1_ffn_W2"][n].rearrange("(f p) d -> p f d", p=P)))

    wait_before(dve, d_x)
    moments(x)

    with ExitStack() as tmp:
        def tb(name, shape):
            return sb(name, shape, tmp)

        G = M1 // 2
        xs = tb("xs1", [P, D])
        xT = tb("xT1", [P, KD, P])
        q_bd = tb("q_bd1", [P, M1, BT, P])
        qp = [tb(f"qp1_{n}", [P, KD, 2 * P]) for n in range(2)]
        qbk = [tb(f"qbk1_{n}", [P, 2]) for n in range(2)]
        prob = [tb(f"prob1_{n}", [P, CTX]) for n in range(2)]
        probT = tb("probT1", [P, KC, 2 * P])
        u_sb = tb("u1", [P, KD, 2 * P])
        attn = tb("attn1", [P, M1, P])
        mx, nb, rs, ri = ([tb(f"{a}1_{n}", [P, 1]) for n in range(2)] for a in ("mx", "nb", "rs", "ri"))
        SCALE1 = 1.0 / 8.0
        DVE(dve.memset(q_bd[:, :, :, :], 0.0))
        QP, U, TP = bank(6), bank(7), (bank(4), bank(5))
        wait_before(pe, d_w1)
        wait_before(dve, d_w1)

        with tiles(T, pe=85, dve=152, act=40) as i:
            wait_before(dve, PE, DVE)
            wait_before(pe, DVE, AC)
            m = normed(xs[:, :], x, i)
            wait(pe, m)
            for k in range(KD):
                m = PE(pe.transpose(QP[:, k * P:(k + 1) * P], xs[:, k * P:(k + 1) * P], ident[:, :]))
            wait(dve, m)
            m_xT = DVE(dve.tensor_copy(xT[:, :, :], QP[:, 0:D].rearrange("p (k n) -> p k n", k=KD)))
            wait(pe, m_xT)
            for half in range(2):
                for mm in range(4):
                    for k in range(KD):
                        pair = half * 4 + mm
                        m = pe.matmul(bank(half)[:, mm * P:(mm + 1) * P], Wq1[:, k, pair * P:(pair + 1) * P],
                                      xT[:, k, :], start=k == 0, stop=k == KD - 1)
                m = PE(m)
                wait(dve, m)
                for h in range(2):
                    r = slice(h * S, (h + 1) * S)
                    ps = bank(half)[r, :].rearrange("p (m b q) -> p m b q", m=4, b=BT)
                    bias = bq1[r, half * 4:(half + 1) * 4].unsqueeze(2).unsqueeze(3).broadcast_to([S, 4, BT, S])
                    m_q = DVE(dve.tensor_tensor(q_bd[r, half * 4:(half + 1) * 4, :, r], ps, bias, ALU.add))

            m_stats = {}
            steps = [(b, s) for b in range(BT) for s in range(G)]
            m_qp, m_qbk, m_S, m_exp, m_T, m_PT, m_PV, m_u, m_OB, m_at, m_P = ({} for _ in range(11))

            def project(n):
                b, s = steps[n]
                wait(pe, m_q, m_qbk.get(n - 1))
                for pr in range(2):
                    for k in range(KD):
                        m = pe.matmul(QP[:, (k * 2 + pr) * P:(k * 2 + pr + 1) * P],
                                      WkT1[:, 2 * s + pr, k * P:(k + 1) * P], q_bd[:, 2 * s + pr, b, :],
                                      start=True, stop=True)
                m = PE(m)
                wait(act, m, m_S.get((n - 2, 1)))
                m_qp[n] = AC(act.activation(qp[n % 2][:, :, :], QP.rearrange("p (k n) -> p k n", k=KD), ACT.Copy))

            def scores(n, pr):
                b, s = steps[n]
                wait(pe, m_qp[n], m_exp.get((n - 1, pr)))
                if s == 0 and pr == 0:
                    pe.wait_ge(d_ctx[b].sem, i * 32 + 32)
                    dve.wait_ge(d_ctx[b].sem, i * 32 + 32)
                for half in range(HALF):
                    for k in range(KD):
                        m = pe.matmul(banks[pr][:, half * BANK:(half + 1) * BANK], qp[n % 2][:, k, pr * P:(pr + 1) * P],
                                      ctxT_buf[b][:, k, half * BANK:(half + 1) * BANK],
                                      start=k == 0, stop=k == KD - 1)
                m_S[n, pr] = PE(m)

            def query_dot_bias(n):
                b, s = steps[n]
                wait(pe, m_qp[n])
                for pr in range(2):
                    m = pe.matmul(QP[:, pr:pr + 1], q_bd[:, 2 * s + pr, b, :], bk1[:, 2 * s + pr:2 * s + pr + 1],
                                  start=True, stop=True)
                m = PE(m)
                wait(dve, m)
                m_qbk[n] = DVE(dve.tensor_copy(qbk[n % 2][:, :], QP[:, 0:2]))

            def softmax(n, pr):
                wait(dve, m_S[n, pr])
                m = DVE(dve.tensor_reduce(mx[pr][:, :], banks[pr][:, :], AX.X, ALU.max))
                wait(dve, m, m_qbk[n])
                m = DVE(dve.tensor_scalar(nb[pr][:, :], mx[pr][:, :], qbk[n % 2][:, pr:pr + 1], -SCALE1,
                                          ALU.add, ALU.mult))
                wait(dve, m)
                m = DVE(dve.scalar_tensor_tensor(nb[pr][:, :], qbk[n % 2][:, pr:pr + 1], SCALE1, nb[pr][:, :],
                                                 ALU.mult, ALU.add))
                wait(act, m, m_T.get((n - 1, pr)))
                m_exp[n, pr] = AC(act.activation(prob[pr][:, :], banks[pr][:, :], ACT.Exp, bias=nb[pr][:, 0:1],
                                                 scale=SCALE1, accum_out=rs[pr][:, 0:1]))
                wait(dve, m_exp[n, pr])
                m = DVE(dve.reciprocal(ri[pr][:, :], rs[pr][:, :]))
                wait(dve, m)
                m_P[n, pr] = DVE(dve.tensor_scalar(prob[pr][:, :], prob[pr][:, :], ri[pr][:, 0:1], None, ALU.mult))

            def transposed(n, pr):
                before = (n, 0) if pr else (n - 1, 1)
                wait(pe, m_P[n, pr], m_PT.get((*before, 0)), m_PT.get((*before, 1)))
                for c in range(KC):
                    t = pe.transpose(TP[c // 4][:, (c % 4) * P:(c % 4 + 1) * P], prob[pr][:, c * P:(c + 1) * P],
                                     ident[:, :])
                    if c == 3:
                        first = PE(t)
                m_T[n, pr] = PE(t)
                for hf, e, m in ((0, dve, first), (1, act, m_T[n, pr])):
                    wait(e, m, m_PV.get(n - 1))
                    dst = probT[:, hf * 4:(hf + 1) * 4, pr * P:(pr + 1) * P]
                    src = TP[hf].rearrange("p (c q) -> p c q", c=4)
                    if hf == 0:
                        m_PT[n, pr, 0] = DVE(dve.tensor_copy(dst, src))
                    else:
                        m_PT[n, pr, 1] = AC(act.activation(dst, src, ACT.Copy))

            def context_stats(n):
                b, s = steps[n]
                for c in (2 * s, 2 * s + 1):
                    at = (i * BT + b) * KC + c
                    dst = stats_c[:, bass.ds(at, 1), :].rearrange("p a s -> p (a s)")
                    m_stats[n] = DVE(dve.bn_stats(dst, ctx_buf[b][:, c, :]))

            def average(n):
                b, s = steps[n]
                wait(pe, m_PT[n, 1, 0], m_PT[n, 1, 1], m_at.get(n - 1))
                wait(pe, m_stats[n])
                for k in range(KD):
                    for c in range(KC):
                        m = pe.matmul(U[:, k * 2 * P:(k + 1) * 2 * P], ctx_buf[b][:, c, k * P:(k + 1) * P],
                                      probT[:, c, :], start=c == 0, stop=c == KC - 1)
                m_PV[n] = PE(m)
                wait(dve, m_PV[n], m_OB.get(n - 1))
                m_u[n] = DVE(dve.tensor_copy(u_sb[:, :, :], U.rearrange("p (k n) -> p k n", k=KD)))

            def values(n):
                b, s = steps[n]
                wait(pe, m_u[n])
                for pr in range(2):
                    for k in range(KD):
                        pair = 2 * s + pr
                        m = pe.matmul(U[:, pr * P:(pr + 1) * P], Wv1[:, k, pair * P:(pair + 1) * P],
                                      u_sb[:, k, pr * P:(pr + 1) * P], start=k == 0, stop=k == KD - 1)
                m_OB[n] = PE(m)
                wait(dve, m_OB[n])
                for h in range(2):
                    r = slice(h * S, (h + 1) * S)
                    bias = bv1[r, 2 * s:2 * s + 2].unsqueeze(2).broadcast_to([S, 2, S])
                    m_at[n] = DVE(dve.tensor_tensor(attn[r, 2 * s:2 * s + 2, b * S:(b + 1) * S],
                                                    U[r, 0:2 * P].rearrange("p (r n) -> p r n", r=2)[:, :, r],
                                                    bias, ALU.add))

            last = len(steps) - 1
            project(0)
            query_dot_bias(0)
            scores(0, 0)
            for n in range(last + 1):
                scores(n, 1)
                softmax(n, 0)
                if n < last:
                    project(n + 1)
                softmax(n, 1)
                if n > 0:
                    average(n - 1)
                transposed(n, 0)
                if n > 0:
                    values(n - 1)
                if n < last:
                    query_dot_bias(n + 1)
                    scores(n + 1, 0)
                transposed(n, 1)
                context_stats(n)
            average(last)
            values(last)
            wait(pe, m_at[last])
            for mm in range(M1):
                m = pe.matmul(U[:, 0:D], attn[:, mm, :], Wo1[:, mm, :], start=mm == 0, stop=mm == M1 - 1)
            m = PE(m)
            wait(dve, m)
            m = DVE(dve.tensor_tensor(xs[:, :], U[:, 0:D], bo1[:, :], ALU.add))
            wait(dve, m)
            DVE(dve.tensor_tensor(x[:, i, :], x[:, i, :], xs[:, :], ALU.add))
            ctx_read = [m_PV[G - 1], m_PV[2 * G - 1]]
        with nc.Fori(0, T - 1, engines=(sp.engine,)) as j:
            for b in range(BT):
                sp.wait_ge(PE.sem, ctx_read[b].at(j))
                load_ctx(b, j + 1)
        wait_before(sp, PE)
        d_w5(sp.dma_start(Wq5, rows("L1_attn_Wq")))
        d_w5(sp.dma_start(Wk5, rows("L1_attn_Wk")))
        d_w5(sp.dma_start(Wv5, rows("L1_attn_Wv")))
        d_w5(sp.dma_start(Wo5, rows("L1_attn_Wpost")))
        for b in range(BT):
            sp.wait_ge(PE.sem, ctx_read[b].at(T - 1))
            load_ctx4(b, 0)

    meet()
    moments(x)
    with ExitStack() as tmp:
        def buffers(name, shape):
            return [sb(f"{name}_{u}", shape, tmp) for u in range(U2)]

        xs, xT, c2, t2 = buffers("xs2", [P, D]), buffers("xT2", [P, KD, P]), buffers("c2", [P, P]), \
            buffers("t2", [P, 4, P])
        qT, kT, km = buffers("qT2", [P, 2, P]), buffers("kT2", [P, 2, P]), buffers("km2", [P, 2, 8, P])
        v, sm = buffers("v2", [P, D]), buffers("sm2", [P, 2, 8, P])
        smT, small, o, oT = buffers("smT2", [P, 2, 8, P]), buffers("small2", [P, 2, 2, 8]), \
            buffers("o2", [P, D]), buffers("oT2", [P, KD, P])
        wait_before(pe, d_w2)
        wait_before(dve, d_w2)
        wait_before(act, d_w2)

        def body2(i, u):
            t = i * U2 + u
            A, C = banks[2 * u], banks[2 * u + 1]
            a0, a1, c0, c1 = (bank(4 * u + n) for n in range(4))
            m = normed(xs[u][:, :], x, t)
            wait(pe, m)
            yield
            m_xT = transposed_tile(xs[u], xT[u], a0)
            wait(pe, m_xT)
            yield
            for k in range(KD):
                m = pe.matmul(a1[:, 0:P], w_qkv2[:, k, :], xT[u][:, k, :], start=k == 0, stop=k == KD - 1)
            m = PE(m)
            wait(act, m)
            m_c = AC(act.activation(c2[u][:, :], a1[:, 0:P], ACT.Gelu, bias=b_qkv2[:, 0:1]))
            for r in range(4):
                for k in range(KD):
                    m = pe.matmul(c0[:, r * P:(r + 1) * P], w_r2[:, r, k, :], xT[u][:, k, :],
                                  start=k == 0, stop=k == KD - 1)
            m_r = PE(m)
            yield
            wait(pe, m_c)
            for n in range(2):
                m = pe.matmul(a0[:, n * P:(n + 1) * P], w_c2[:, n, :], c2[u][:, :], start=True, stop=True)
            m_cc = PE(m)
            m_v = PE(pe.matmul(c1[:, 0:D], c2[u][:, :], w_v2[:, :], start=True, stop=True))
            wait(dve, m_r)
            for r in range(4):
                m = DVE(dve.scalar_tensor_tensor(t2[u][:, r, :], c0[:, r * P:(r + 1) * P], b_r2[:, r:r + 1],
                                                 rope2[:, r % 2, :], ALU.add, ALU.mult))
            wait(dve, m)
            t4 = t2[u][:, :, :].rearrange("p (n s) t -> p n s t", s=2)
            m_rot = DVE(dve.tensor_tensor(t4[:, :, 0, :], t4[:, :, 0, :], t4[:, :, 1, :], ALU.add))
            yield
            wait(act, m_cc)
            for n, dst in enumerate((qT[u], kT[u])):
                AC(act.activation(dst[:, 0, :], a0[:, n * P:(n + 1) * P], ACT.Gelu, bias=b_c2[:, n:n + 1]))
            wait(act, m_rot)
            for n, dst in enumerate((qT[u], kT[u])):
                m_qk = AC(act.activation(dst[:, 1, :], t2[u][:, 2 * n, :], ACT.Gelu))
            wait(dve, m_v)
            m_v = DVE(dve.tensor_tensor(v[u][:, :], c1[:, 0:D], b_v2[:, :], ALU.add))
            yield
            wait(dve, m_qk)
            m_S = []
            for c in range(2):
                m = DVE(dve.tensor_tensor(km[u][:, c, :, :], kT[u][:, c:c + 1, :].broadcast_to([P, 8, P]),
                                          head2[:, :].unsqueeze(2).broadcast_to([P, 8, P]), ALU.mult))
                wait(pe, m)
                for hf in range(2):
                    m = pe.matmul((A, C)[c][:, hf * BANK:(hf + 1) * BANK], qT[u][:, c, :],
                                  km[u][:, c, 4 * hf:4 * hf + 4, :], start=True, stop=True)
                m_S.append(PE(m))
                yield
            soft = [tile_softmax(m_S[c], (A, C)[c], sm[u][:, c], small[u][:, c], 1.0 / 4.0, 0) for c in range(2)]
            for step in range(3):
                m_soft = [next(s) for s in soft]
                yield
            m_T = []
            for c in range(2):
                m_T += tile_transposes(m_soft[c], (A, C)[c], sm[u][:, c], smT[u][:, c])
                yield
            wait(pe, *m_T)
            for h in range(16):
                cols = slice(h * HD2, (h + 1) * HD2)
                m = pe.matmul(a0[:, cols], smT[u][:, h // 8, h % 8, :], v[u][:, cols], start=True, stop=True)
            m = PE(m)
            wait(dve, m)
            m = DVE(dve.tensor_tensor(o[u][:, :].rearrange("p (c h e) -> p c h e", c=2, h=8),
                                      a0[:, 0:D].rearrange("p (c h e) -> p c h e", c=2, h=8),
                                      small[u][:, :, 1, :].unsqueeze(3).broadcast_to([P, 2, 8, HD2]), ALU.mult))
            wait(pe, m)
            yield
            m = transposed_tile(o[u], oT[u], a1)
            wait(pe, m)
            yield
            for k in range(KD):
                m = pe.matmul(c0[:, 0:D], oT[u][:, k, :], w_o2[:, k, :], start=k == 0, stop=k == KD - 1)
            m = PE(m)
            wait(dve, m)
            m = DVE(dve.tensor_tensor(o[u][:, :], c0[:, 0:D], b_o2[:, :], ALU.add))
            wait(dve, m)
            xt = x[:, bass.ds(t, 1), :].rearrange("p a d -> p (a d)")
            DVE(dve.tensor_tensor(xt, xt, o[u][:, :], ALU.add))

        with tiles(T // U2, pe=28, dve=52, act=18) as i:
            for e in (pe, dve, act):
                wait_before(e, PE, DVE, AC)
            interleave(*(body2(i, u) for u in range(U2)))

    meet()
    moments(x)
    with ExitStack() as tmp:
        def buffers(name, shape):
            return [sb(f"{name}_{u}", shape, tmp) for u in range(U2)]

        xs, xT, sq = buffers("xs3", [P, D]), buffers("xT3", [P, KD, P]), buffers("sq3", [P, 2, D])

        def body3(i, u):
            t = i * U2 + u
            into, ps = bank(2 * u), bank(2 * u + 1)
            m = normed(xs[u][:, :], x, t)
            wait(pe, m)
            m = transposed_tile(xs[u], xT[u], into)
            wait(pe, m)
            yield
            for n in range(2):
                for k in range(KD):
                    m = pe.matmul(ps[:, n * D:(n + 1) * D], xT[u][:, k, :], trig3[:, n, k, :],
                                  start=k == 0, stop=k == KD - 1)
            m = PE(m)
            wait(act, m)
            m = AC(act.activation(sq[u][:, :, :], ps.rearrange("p (n d) -> p n d", n=2), ACT.Square))
            wait(dve, m)
            yield
            m = DVE(dve.tensor_tensor(sq[u][:, 0, :], sq[u][:, 0, :], sq[u][:, 1, :], ALU.add))
            wait(act, m)
            m = AC(act.activation(sq[u][:, 0, :], sq[u][:, 0, :], ACT.Sqrt))
            yield
            wait(dve, m)
            xt = x[:, bass.ds(t, 1), :].rearrange("p a d -> p (a d)")
            DVE(dve.tensor_tensor(xt, xt, sq[u][:, 0, :], ALU.add))

        with tiles(T // U2, pe=4, dve=8, act=4) as i:
            for e in (pe, dve, act):
                wait_before(e, PE, DVE, AC)
            interleave(*(body3(i, u) for u in range(U2)))

    meet()
    moments(x)
    with tiles(T, dve=1) as i:
        normed(xn[:, bass.ds(i, 1), :].rearrange("p a d -> p (a d)"), x, i)
    wait_before(dve, DVE)
    moments(xn)
    NC_ = B * KC
    stat = [stats_c[:, 0:NC_, n] for n in range(6)]
    m = DVE(dve.tensor_tensor(mean_c[:, 0:NC_], stat[1], stat[4], ALU.add))
    m = DVE(dve.tensor_tensor(rstd_c[:, 0:NC_], stat[1], stat[4], ALU.subtract))
    wait(dve, m)
    m = DVE(dve.tensor_scalar(mean_c[:, 0:NC_], mean_c[:, 0:NC_], 0.5, None, ALU.mult))
    m = DVE(dve.tensor_tensor(rstd_c[:, 0:NC_], rstd_c[:, 0:NC_], rstd_c[:, 0:NC_], ALU.mult))
    wait(dve, m)
    m = DVE(dve.tensor_scalar(rstd_c[:, 0:NC_], rstd_c[:, 0:NC_], 0.25, EPS, ALU.mult, ALU.add))
    m = DVE(dve.tensor_tensor(stat[2], stat[2], stat[5], ALU.add))
    wait(dve, m)
    m = DVE(dve.scalar_tensor_tensor(rstd_c[:, 0:NC_], stat[2], 1.0 / D, rstd_c[:, 0:NC_], ALU.mult, ALU.add))
    wait(act, m)
    m = AC(act.activation(rstd_c[:, 0:NC_], rstd_c[:, 0:NC_], ACT.Sqrt))
    wait(dve, m)
    m = DVE(dve.reciprocal(rstd_c[:, 0:NC_], rstd_c[:, 0:NC_]))
    wait(dve, m)
    for c in (mean_c, rstd_c):
        m = DVE(dve.tensor_copy(c[:, NC_:NC_ + BT * KC], c[:, 0:BT * KC]))
    wait(dve, m)

    with ExitStack() as tmp:
        def tb(name, shape):
            return sb(name, shape, tmp)

        SCALE4 = 1.0 / 8.0
        KEYS = CTX + S
        xs = tb("xs4", [P, D])
        xT = tb("xT4", [P, KD, P])
        lat = tb("lat4", [P, BT, D])
        q_bd = tb("q_bd4", [P, 2, M4, BT, P])
        kcs = [tb(f"kcs4_{n}", [P, 2, CTX]) for n in range(2)]
        kl = tb("kl4", [P, M4, S])
        prob = [tb(f"prob4_{n}", [P, KEYS]) for n in range(2)]
        probT = tb("probT4", [P, KC + 1, 2 * P])
        u_sb = tb("u4", [P, KD, 2 * P])
        attn = tb("attn4", [P, M4, P])
        mx, nb, rs = ([tb(f"{a}4_{n}", [P, 2]) for n in range(2)] for a in ("mx", "nb", "rs"))
        MISC, U, TP = bank(6), bank(7), (bank(4), bank(5))
        KPS, SPS = banks[0], banks[1]
        DVE(dve.memset(q_bd[:, :, :, :, :], 0.0))
        DVE(dve.memset(lat[:, :, :], 0.0))
        DVE(dve.memset(probT[:, KC, :], 0.0))
        wait_before(pe, d_w4)
        wait_before(dve, d_w4)
        wait_before(pool, d_w4)
        STEPS = M4 // 2

        class Turn:
            pass

        def normalize(b, t, d_count, w):
            dve.wait_ge(d_ctx4[b].sem, d_count)
            for c in range(KC):
                at = (t * BT + b) * KC + c
                m = DVE(dve.tensor_scalar(ctx_buf[b][:, c, :], ctx_buf[b][:, c, :], mean_c[:, bass.ds(at, 1)],
                                          rstd_c[:, bass.ds(at, 1)], ALU.subtract, ALU.mult))
                if c == KC // 2 - 1:
                    first = m
            for hf, m in enumerate((first, m)):
                wait(pool, m)
                c = slice(hf * KC // 2, (hf + 1) * KC // 2)
                m = PL(pool.tensor_tensor(ctx_buf[b][:, c, :], ctx_buf[b][:, c, :],
                                          gb4[:, 0:1, :].broadcast_to([P, KC // 2, D]), ALU.mult))
                wait(pool, m)
                w.m_norm[b, hf] = PL(pool.tensor_tensor(ctx_buf[b][:, c, :], ctx_buf[b][:, c, :],
                                                        gb4[:, 1:2, :].broadcast_to([P, KC // 2, D]), ALU.add))

        def transpose_context(b, w):
            for k in range(KD):
                for hf in range(2):
                    wait(pe, w.m_norm[b, hf], *w.tp[hf])
                    for c in range(4):
                        m = pe.transpose(TP[hf][:, c * P:(c + 1) * P], ctx_buf[b][:, 4 * hf + c, k * P:(k + 1) * P],
                                         ident[:, :])
                    m = PE(m)
                    e, line = ((dve, DVE), (act, AC))[hf]
                    wait(e, m)
                    dst, src = ctxT_buf[b][:, k, hf * BANK:(hf + 1) * BANK], TP[hf]
                    m = line(dve.tensor_copy(dst, src) if e is dve else act.activation(dst, src, ACT.Copy))
                    w.tp[hf] = [m]
                    w.m_ctxT[b, hf] = m

        def keys(b, m_, w):
            s = m_ % 2
            wait(pe, w.m_ctxT.get((b, 0)), w.m_ctxT.get((b, 1)), w.m_kcs.get("ps"))
            for half in range(HALF):
                for k in range(KD):
                    m = pe.matmul(KPS[:, half * BANK:(half + 1) * BANK], w_k4[:, k, m_ * P:(m_ + 1) * P],
                                  ctxT_buf[b][:, k, half * BANK:(half + 1) * BANK], start=k == 0, stop=k == KD - 1)
                m = PE(m)
                wait(dve, m, w.m_S.get(w.last_S[s]))
                for part in range(2):
                    cols = slice(half * BANK, (half + 1) * BANK)
                    m = DVE(dve.tensor_tensor(kcs[s][:, part, cols], KPS[:, cols], rope4[:, part, cols], ALU.mult))
            w.m_kcs["ps"] = w.m_kcs[b, m_] = m

        def scores(b, m_, w):
            s = m_ % 2
            wait(pe, w.m_kcs[b, m_], w.m_misc, w.m_exp)
            for half in range(HALF):
                for part in range(2):
                    cols = slice(half * BANK, (half + 1) * BANK)
                    pe.matmul(SPS[:, cols], q_bd[:, part, m_, b, :], kcs[s][:, part, cols],
                              start=part == 0, stop=part == 1)
            m = pe.matmul(MISC[:, 0:S], q_bd[:, 0, m_, b, :], kl[:, m_, :], start=True, stop=True)
            w.m_S[b, m_] = PE(m)
            w.last_S[s] = (b, m_)

        def softmax(b, m_, w):
            p = m_ % 2
            wait(dve, w.m_S[b, m_])
            DVE(dve.tensor_reduce(mx[p][:, 0:1], SPS[:, :], AX.X, ALU.max))
            m = DVE(dve.tensor_reduce(mx[p][:, 1:2], MISC[:, 0:S], AX.X, ALU.max))
            wait(dve, m)
            m = DVE(dve.tensor_scalar(nb[p][:, 0:1], mx[p][:, 0:1], mx[p][:, 1:2], -SCALE4, ALU.max, ALU.mult))
            wait(act, m, w.m_T.get(w.last_T[p]))
            AC(act.activation(prob[p][:, 0:CTX], SPS[:, :], ACT.Exp, bias=nb[p][:, 0:1], scale=SCALE4,
                              accum_out=rs[p][:, 0:1]))
            m = AC(act.activation(prob[p][:, CTX:KEYS], MISC[:, 0:S], ACT.Exp, bias=nb[p][:, 0:1], scale=SCALE4,
                                  accum_out=rs[p][:, 1:2]))
            w.m_exp = m
            wait(dve, m)
            m = DVE(dve.tensor_tensor(nb[p][:, 1:2], rs[p][:, 0:1], rs[p][:, 1:2], ALU.add))
            wait(dve, m)
            m = DVE(dve.reciprocal(nb[p][:, 1:2], nb[p][:, 1:2]))
            wait(dve, m)
            w.m_P[b, m_] = DVE(dve.tensor_scalar(prob[p][:, :], prob[p][:, :], nb[p][:, 1:2], None, ALU.mult))

        def transposed(b, m_, w):
            p = m_ % 2
            wait(pe, w.m_P[b, m_], *w.tp[0], *w.tp[1])
            for c in range(KC):
                m = pe.transpose(TP[c // 4][:, (c % 4) * P:(c % 4 + 1) * P], prob[p][:, c * P:(c + 1) * P],
                                 ident[:, :])
                if c == 0:
                    PE(pe.transpose(MISC[0:S, P:2 * P], prob[p][:, CTX:KEYS], ident[:, :]))
                if c == 3:
                    first = PE(m)
            w.m_T[b, m_] = PE(m)
            w.last_T[p] = (b, m_)
            wait(dve, first, w.m_A)
            cols = slice(p * P, (p + 1) * P)
            w.m_misc = DVE(dve.tensor_copy(probT[0:S, KC, cols], MISC[0:S, P:2 * P]))
            m = DVE(dve.tensor_copy(probT[:, 0:4, cols], TP[0].rearrange("p (c q) -> p c q", c=4)))
            wait(act, w.m_T[b, m_], w.m_A)
            m2 = AC(act.activation(probT[:, 4:8, cols], TP[1].rearrange("p (c q) -> p c q", c=4), ACT.Copy))
            w.tp = [[m], [m2]]

        def average(b, s, w):
            wait(pe, *w.tp[0], *w.tp[1], w.m_at)
            for k in range(KD):
                for c in range(KC + 1):
                    src = ctx_buf[b][:, c, k * P:(k + 1) * P] if c < KC else lat[:, b, k * P:(k + 1) * P]
                    m = pe.matmul(U[:, k * 2 * P:(k + 1) * 2 * P], src, probT[:, c, :], start=c == 0, stop=c == KC)
            w.m_A = PE(m)
            w.read[b] = w.m_A
            wait(dve, w.m_A, w.m_V)
            w.m_u = DVE(dve.tensor_copy(u_sb[:, :, :], U.rearrange("p (k n) -> p k n", k=KD)))

        def values(b, s, w):
            wait(pe, w.m_u)
            for pr in range(2):
                for k in range(KD):
                    pair = 2 * s + pr
                    m = pe.matmul(U[:, pr * P:(pr + 1) * P], w_v4[:, k, pair * P:(pair + 1) * P],
                                  u_sb[:, k, pr * P:(pr + 1) * P], start=k == 0, stop=k == KD - 1)
            w.m_V = PE(m)
            wait(dve, w.m_V)
            for h in range(2):
                r = slice(h * S, (h + 1) * S)
                w.m_at = DVE(dve.tensor_copy(attn[r, 2 * s:2 * s + 2, b * S:(b + 1) * S],
                                             U[r, 0:2 * P].rearrange("p (r n) -> p r n", r=2)[:, :, r]))

        def latent_keys(b, w):
            wait(pe, w.m_misc, w.m_exp)
            for m_ in range(M4):
                for k in range(KD):
                    m = pe.matmul(MISC[:, m_ * S:(m_ + 1) * S], w_k4[:, k, m_ * P:(m_ + 1) * P],
                                  xT[:, k, b * S:(b + 1) * S], start=k == 0, stop=k == KD - 1)
            m = PE(m)
            wait(dve, m)
            w.m_misc = DVE(dve.tensor_copy(kl[:, :, :], MISC[:, 0:M4 * S].rearrange("p (m q) -> p m q", m=M4)))

        def fresh():
            w = Turn()
            w.m_norm, w.m_ctxT, w.m_kcs, w.m_S, w.m_T, w.m_P, w.read = ({} for _ in range(7))
            w.tp, w.last_S, w.last_T = [[], []], [None, None], [None, None]
            w.m_misc = w.m_exp = w.m_A = w.m_V = w.m_u = w.m_at = None
            return w

        w = fresh()
        normalize(0, 0, 16, w)
        transpose_context(0, w)
        wait_before(pe, DVE, AC, PL)
        with tiles(T, pe=70, dve=141, act=28, pool=8) as i:
            w = fresh()
            for e in (pe, dve, act, pool):
                wait_before(e, PE, DVE, AC, PL)
            m = normed(xs[:, :], xn, i)
            wait(dve, m)
            m = DVE(dve.tensor_tensor(xs[:, :], xs[:, :], gb4[:, 2, :], ALU.mult))
            wait(dve, m)
            m_ln = DVE(dve.tensor_tensor(xs[:, :], xs[:, :], gb4[:, 3, :], ALU.add))
            wait(pe, m_ln)
            m_lnT = transposed_tile(xs, xT, MISC)
            wait(dve, m_ln)
            for b in range(BT):
                DVE(dve.tensor_copy(lat[0:S, b, :], xs[b * S:(b + 1) * S, :]))
            wait(pe, m_lnT)
            for part, ps in enumerate((MISC, U)):
                for m_ in range(M4):
                    for k in range(KD):
                        m = pe.matmul(ps[:, m_ * P:(m_ + 1) * P], w_q4[:, part, k, m_ * P:(m_ + 1) * P], xT[:, k, :],
                                      start=k == 0, stop=k == KD - 1)
                m = PE(m)
                wait(dve, m)
                for h in range(2):
                    r = slice(h * S, (h + 1) * S)
                    w.m_misc = DVE(dve.tensor_scalar(q_bd[r, part, :, :, r],
                                                     ps[r, :].rearrange("p (m b q) -> p m b q", m=M4, b=BT),
                                                     turn4[r, part:part + 1], None, ALU.mult))
            latent_keys(0, w)
            keys(0, 0, w)
            units = [(b, m_) for b in range(BT) for m_ in range(M4)]
            for n, (b, m_) in enumerate(units):
                scores(b, m_, w)
                softmax(b, m_, w)
                if m_ + 1 < M4:
                    keys(b, m_ + 1, w)
                if m_ % 2 == 0 and m_ > 0:
                    average(b, m_ // 2 - 1, w)
                if m_ == 0 and b == 1:
                    average(0, STEPS - 1, w)
                if m_ == 0:
                    if b == 0:
                        normalize(1, i, i * 16 + 16, w)
                    else:
                        normalize(0, i + 1, i * 16 + 32, w)
                if m_ == M4 - 1 and b == 0:
                    keys(1, 0, w)
                transposed(b, m_, w)
                if m_ % 2 == 0 and m_ > 0:
                    values(b, m_ // 2 - 1, w)
                if m_ == 0 and b == 1:
                    values(0, STEPS - 1, w)
                if m_ == 1:
                    transpose_context(1 - b, w)
                if m_ == M4 - 1 and b == 0:
                    latent_keys(1, w)
            average(1, STEPS - 1, w)
            values(1, STEPS - 1, w)
            wait(pe, w.m_at)
            for m_ in range(M4):
                m = pe.matmul(U[:, 0:D], attn[:, m_, :], w_o4[:, m_, :], start=m_ == 0, stop=m_ == M4 - 1)
            m = PE(m)
            wait(dve, m)
            DVE(dve.tensor_tensor(x[:, i, :], x[:, i, :], U[:, 0:D], ALU.add))
            read = dict(w.read)
        with nc.Fori(0, T - 1, engines=(sp.engine,)) as j:
            for b in range(BT):
                sp.wait_ge(PE.sem, read[b].at(j))
                load_ctx4(b, j + 1)
        sp.wait_ge(PE.sem, read[0].at(T - 1))
        load_ctx4(0, 0)
    meet()
    load_expert(0)
    load_expert(1)

    meet()
    moments(x)
    with ExitStack() as tmp:
        def buffers(name, shape):
            return [sb(f"{name}_{u}", shape, tmp) for u in range(U2)]

        xs, xT, q5, k_bd = buffers("xs5", [P, D]), buffers("xT5", [P, KD, P]), buffers("q5", [P, M5, P]), \
            buffers("k_bd5", [P, M5, 2, P])
        v5, sm, smT, small = buffers("v5", [P, M5 * P]), buffers("sm5", [P, 8, P]), buffers("smT5", [P, 8, P]), \
            buffers("small5", [P, 2, 8])
        a5 = buffers("a5", [P, M5, P])
        for u in range(U2):
            DVE(dve.memset(k_bd[u][:, :, :, :], 0.0))
        wait_before(pe, d_w5)

        def body5(i, u):
            t = i * U2 + u
            A, C = banks[2 * u], banks[2 * u + 1]
            m_x = normed(xs[u][:, :], x, t)
            wait(pe, m_x)
            yield
            m_xT = transposed_tile(xs[u], xT[u], C)
            wait(pe, m_xT)
            yield
            for hf in range(2):
                for mm in range(4):
                    for k in range(KD):
                        pair = 4 * hf + mm
                        m = pe.matmul(A[:, pair * P:(pair + 1) * P], Wq5[:, k, pair * P:(pair + 1) * P], xT[u][:, k, :],
                                      start=k == 0, stop=k == KD - 1)
                m = PE(m)
                wait(act, m)
                m_q = AC(act.activation(q5[u][:, 4 * hf:4 * hf + 4, :],
                                        A[:, hf * BANK:(hf + 1) * BANK].rearrange("p (m q) -> p m q", m=4), ACT.Copy))
            yield
            for hf in range(2):
                for mm in range(4):
                    for k in range(KD):
                        pair = 4 * hf + mm
                        m = pe.matmul(C[:, pair * P:(pair + 1) * P], Wk5[:, k, pair * P:(pair + 1) * P], xT[u][:, k, :],
                                      start=k == 0, stop=k == KD - 1)
                m = PE(m)
                wait(dve, m)
                for h in range(2):
                    r = slice(h * S, (h + 1) * S)
                    m_k = DVE(dve.tensor_copy(k_bd[u][r, 4 * hf:4 * hf + 4, h, :],
                                              C[r, hf * BANK:(hf + 1) * BANK].rearrange("p (m q) -> p m q", m=4)))
            yield
            wait(pe, m_q)
            for hf in range(2):
                for k in range(KD):
                    m = pe.matmul(A[:, hf * BANK:(hf + 1) * BANK], xT[u][:, k, :],
                                  Wv5[:, k, hf * BANK:(hf + 1) * BANK], start=k == 0, stop=k == KD - 1)
                m = PE(m)
                wait(act, m)
                m_v = AC(act.activation(v5[u][:, hf * BANK:(hf + 1) * BANK], A[:, hf * BANK:(hf + 1) * BANK], ACT.Copy))
            yield
            m_av = []
            for grp in range(2):
                wait(pe, m_k, *m_av)
                for mm in range(4):
                    pair = 4 * grp + mm
                    m = pe.matmul(C[:, mm * 2 * P:(mm + 1) * 2 * P], q5[u][:, pair, :], k_bd[u][:, pair, :, :],
                                  start=True, stop=True)
                m = PE(m)
                soft = tile_softmax(m, C, sm[u], small[u], 1.0 / 8.0, 1)
                next(soft)
                yield
                next(soft)
                yield
                m = next(soft)
                wait(dve, m)
                m = DVE(dve.tensor_tensor(sm[u][:, :, :], sm[u][:, :, :],
                                          small[u][:, 1, :].unsqueeze(2).broadcast_to([P, 8, P]), ALU.mult))
                yield
                wait(pe, m_v)
                m_T = tile_transposes(m, A, sm[u], smT[u])
                wait(pe, *m_T)
                yield
                for h in range(8):
                    head = 8 * grp + h
                    m = pe.matmul(C[(h % 2) * S:(h % 2 + 1) * S, (h // 2) * P:(h // 2 + 1) * P],
                                  v5[u][:, head * S:(head + 1) * S], smT[u][:, h, :], start=True, stop=True)
                m = PE(m)
                wait(act, m)
                m_a = AC(act.activation(a5[u][:, 4 * grp:4 * grp + 4, :],
                                        C[:, 0:BANK].rearrange("p (m q) -> p m q", m=4), ACT.Gelu))
                m_av = [m_a]
                yield
            wait(pe, m_a, *m_T)
            for mm in range(M5):
                m = pe.matmul(A[:, 0:D], a5[u][:, mm, :], Wo5[:, mm, :], start=mm == 0, stop=mm == M5 - 1)
            m = PE(m)
            wait(dve, m)
            m = DVE(dve.tensor_tensor(xs[u][:, :], xs[u][:, :], A[:, 0:D], ALU.add))
            wait(dve, m)
            xt = x[:, bass.ds(t, 1), :].rearrange("p a d -> p (a d)")
            DVE(dve.tensor_tensor(xt, xt, xs[u][:, :], ALU.add))

        with tiles(T // U2, pe=32, dve=44, act=20) as i:
            for e in (pe, dve, act):
                wait_before(e, PE, DVE, AC)
            interleave(*(body5(i, u) for u in range(U2)))

    meet()
    load_expert(2)
    load_expert(3)
    moments(x)
    with ExitStack() as tmp:
        def tb(name, shape):
            return sb(name, shape, tmp)

        xs, xT = [tb(f"xs6_{u}", [P, D]) for u in range(U2)], [tb(f"xT6_{u}", [P, KD, P]) for u in range(U2)]
        logit, hot, work, rank_in = (tb(n, [P, T, E]) for n in ("logit6", "hot6", "work6", "rank6"))
        first6, top, p_tok, rank, slot, keep = (tb(n, [P, T]) for n in
                                                ("first6", "top6", "p_tok6", "rank_tok6", "slot6", "keep6"))
        iota6, earlier6 = tb("iota6", [P, E * CAP]), tb("earlier6", [P, P])
        d_w6(sp.dma_start(iota6[:, :], everywhere("iota6")))
        d_w6(sp.dma_start(earlier6[:, :], g["earlier6"]))
        select = tb("select6", [P, T, E * CAP])
        xe = tb("xe6", [P, KD, E * CAP])
        hT = [tb(f"hT6_{n}", [P, F // P, CAP]) for n in range(2)]
        ye = tb("ye6", [P, E, D])
        slot_row = tb("slot_row6", [P, T * P])
        wait_before(pe, d_w6)
        wait_before(dve, d_w6)

        def body6(i, u):
            t = i * U2 + u
            xt = xn[:, bass.ds(t, 1), :].rearrange("p a d -> p (a d)")
            normed(xt, x, t)
            m = normed(xs[u][:, :], x, t)
            wait(pe, m)
            m = transposed_tile(xs[u], xT[u], bank(2 * u))
            wait(pe, m)
            yield
            for k in range(KD):
                m = pe.matmul(bank(2 * u + 1)[:, 0:E], xT[u][:, k, :], w_r6[:, k, :], start=k == 0, stop=k == KD - 1)
            m = PE(m)
            wait(dve, m)
            DVE(dve.tensor_copy(logit[:, bass.ds(t, 1), :].rearrange("p a e -> p (a e)"), bank(2 * u + 1)[:, 0:E]))

        with tiles(T // U2, pe=4, dve=8) as i:
            for e in (pe, dve):
                wait_before(e, PE, DVE)
            interleave(*(body6(i, u) for u in range(U2)))
        wait_before(dve, DVE)

        def over_experts(v):
            return v[:, :].unsqueeze(2).broadcast_to([P, T, E])

        def over_tiles(v):
            return v.unsqueeze(1).broadcast_to([P, T, E])

        wait(dve, DVE(dve.tensor_reduce(top[:, :], logit[:, :, :], AX.X, ALU.max)))
        m = DVE(dve.tensor_tensor(logit[:, :, :], logit[:, :, :], over_experts(top), ALU.subtract))
        wait(act, m)
        m_e = AC(act.activation(work[:, :, :], logit[:, :, :], ACT.Exp))
        wait(dve, m_e)
        m = DVE(dve.tensor_reduce(p_tok[:, :], work[:, :, :], AX.X, ALU.add))
        wait(dve, m)
        DVE(dve.reciprocal(p_tok[:, :], p_tok[:, :]))
        m = DVE(dve.tensor_scalar(hot[:, :, :], logit[:, :, :], 0.0, None, ALU.is_ge))
        wait(dve, m)
        m = DVE(dve.tensor_tensor(work[:, :, :], hot[:, :, :], over_tiles(count6[:, 0:E]), ALU.mult))
        wait(dve, m)
        m = DVE(dve.tensor_reduce(first6[:, :], work[:, :, :], AX.X, ALU.max))
        wait(dve, m)
        m = DVE(dve.tensor_tensor(hot[:, :, :], work[:, :, :], over_experts(first6), ALU.is_equal))
        wait(pe, m)
        flat = hot[:, :, :].rearrange("p t e -> p (t e)")
        pe.matmul(bank(0)[:, 0:T * E], earlier6[:, :], flat, start=True, stop=True)
        m = PE(pe.matmul(bank(1)[:, 0:T * E], ones[:, :], flat, start=True, stop=True))
        wait(dve, m)
        DVE(dve.tensor_copy(rank_in[:, :, :], bank(0)[:, 0:T * E].rearrange("p (t e) -> p t e", t=T)))
        m = DVE(dve.tensor_copy(work[:, :, :], bank(1)[:, 0:T * E].rearrange("p (t e) -> p t e", t=T)))
        for t in range(1, T):
            wait(dve, m)
            m = DVE(dve.tensor_tensor(work[:, t, :], work[:, t, :], work[:, t - 1, :], ALU.add))
        wait(dve, m)
        m = DVE(dve.tensor_tensor(rank_in[:, 1:T, :], rank_in[:, 1:T, :], work[:, 0:T - 1, :], ALU.add))
        wait(dve, m)
        m = DVE(dve.tensor_tensor(rank_in[:, :, :], rank_in[:, :, :], hot[:, :, :], ALU.mult))
        wait(dve, m)
        m = DVE(dve.tensor_reduce(rank[:, :], rank_in[:, :, :], AX.X, ALU.add))
        wait(dve, m)
        DVE(dve.tensor_scalar(keep[:, :], rank[:, :], float(CAP), None, ALU.is_lt))
        m = DVE(dve.scalar_tensor_tensor(slot[:, :], first6[:, :], -float(CAP), rank[:, :], ALU.mult, ALU.add))
        wait(dve, m)
        m = DVE(dve.scalar_tensor_tensor(slot[:, :], slot[:, :], float(CAP * E + 1), keep[:, :], ALU.add, ALU.mult))
        wait(dve, m)
        m = DVE(dve.tensor_scalar(slot[:, :], slot[:, :], -1.0, None, ALU.add))
        wait(dve, m)
        for t in range(T):
            m = DVE(dve.tensor_scalar(select[:, t, :], iota6[:, :], slot[:, t:t + 1], None, ALU.is_equal))
        wait(pe, m)
        m_xe = []
        for k in range(KD):
            for half in range(2):
                n = 2 * k + half
                cols = slice(half * BANK, (half + 1) * BANK)
                for t in range(T):
                    m = pe.matmul(bank(4 + n), xn[:, t, k * P:(k + 1) * P], select[:, t, cols],
                                  start=t == 0, stop=t == T - 1)
                m = PE(m)
                e, line = ((dve, DVE), (act, AC))[half]
                wait(e, m)
                m_xe.append(line(dve.tensor_copy(xe[:, k, cols], bank(4 + n)) if e is dve else
                                 act.activation(xe[:, k, cols], bank(4 + n), ACT.Copy)))
        m_gather = m
        wait(dve, m_gather)
        for t in range(T):
            m = DVE(dve.tensor_scalar(select[:, 0, t * P:(t + 1) * P], ident[:, :], slot[:, t:t + 1], None, ALU.mult))
        wait(pe, m)
        for half in range(2):
            m = PE(pe.matmul(bank(2 + half), ones[:, :], select[:, 0, half * BANK:(half + 1) * BANK],
                             start=True, stop=True))
        wait(dve, m)
        m = DVE(dve.tensor_copy(slot_row[:, :], banks[1][:, :]))
        wait(dve, m)
        for e_ in range(E):
            m_back = DVE(dve.tensor_scalar(select[:, e_, :], slot_row[:, :], count6[:, E + e_:E + e_ + 1], None,
                                           ALU.is_equal))

        wait(pe, *m_xe)
        wait_before(pe, DVE, AC)

        RING = 4
        with tiles(E // RING, pe=12, dve=8, act=4) as i:
            m_h, m_H, m_Y, m_y = {}, {}, {}, {}
            for e in (pe, dve, act):
                wait_before(e, PE, DVE, AC)
            pe.wait_ge(d_e.sem, (i * RING + RING) * 32)

            def up(n):
                w1 = w1_ring[n]
                for hf in range(2):
                    wait(pe, m_h.get((n - 2, hf)))
                    ps = banks[n % 2][:, hf * BANK:(hf + 1) * BANK]
                    for ff in range(4):
                        f = 4 * hf + ff
                        for k in range(KD):
                            m = pe.matmul(ps[:, ff * CAP:(ff + 1) * CAP], w1[:, k, f * P:(f + 1) * P],
                                          xe[:, k, bass.ds((i * RING + n) * CAP, CAP)],
                                          start=k == 0, stop=k == KD - 1)
                    m_H[n] = m = PE(m)
                    e, line = ((dve, DVE), (act, AC))[hf]
                    wait(e, m, m_Y.get(n - 2))
                    dst, src = hT[n % 2][:, 4 * hf:4 * hf + 4, :], ps.rearrange("p (f c) -> p f c", f=4)
                    m_h[n, hf] = line(dve.tensor_scalar(dst, src, 0.0, None, ALU.max) if e is dve else
                                      act.activation(dst, src, ACT.Relu))

            def down(n):
                wait(pe, m_h[n, 0], m_h[n, 1], m_y.get(n - 2))
                ps = bank(4 + n % 2)[:, 0:D]
                for f in range(F // P):
                    m = pe.matmul(ps, hT[n % 2][:, f, :], w2_ring[n][:, f, :], start=f == 0, stop=f == F // P - 1)
                m_Y[n] = PE(m)
                wait(dve, m_Y[n])
                dst = ye[:, bass.ds(i * RING + n, 1), :].rearrange("p a d -> p (a d)")
                m_y[n] = DVE(dve.tensor_copy(dst, ps))

            up(0)
            for n in range(RING):
                if n + 1 < RING:
                    up(n + 1)
                down(n)
            ring_read = [m_Y[n] for n in range(RING)]
        for n in range(RING):
            sp.wait_ge(PE.sem, ring_read[n].at(0))
            load_expert(RING + n)

        wait_before(pe, DVE, AC)
        m_o = {}
        for t in range(T):
            wait(pe, m_o.get(t - 4))
            for e_ in range(E):
                m = pe.matmul(bank(2 * (t % 4))[:, 0:D], select[:, e_, t * P:(t + 1) * P], ye[:, e_, :],
                              start=e_ == 0, stop=e_ == E - 1)
            m = PE(m)
            wait(dve, m)
            m_o[t] = DVE(dve.scalar_tensor_tensor(x[:, t, :], bank(2 * (t % 4))[:, 0:D], p_tok[:, t:t + 1], x[:, t, :],
                                                  ALU.mult, ALU.add))
            wait(sp, m_o[t])
            d_out(sp.dma_start(out[t * P:(t + 1) * P, :], x[:, t, :]))
        sp.wait_ge(d_out.sem, T * 16)



def constants():
    f = np.float32
    token = np.arange(P)
    same = token[:, None] // S == token[None, :] // S
    masks = np.stack([np.where(same & (token[None, :] <= token[:, None]), 0.0, MASKED),
                      np.where(same, 0.0, MASKED)]).astype(f)

    def angles(positions, width):
        inv = f(1.0) / np.power(f(10000.0), np.arange(0, width, 2, dtype=f) / f(width), dtype=f)
        a = np.arange(positions, dtype=f)[:, None] * inv[None, :]
        return np.concatenate([a, a], axis=1).T

    a2 = angles(S, P)
    sign = np.where(token < P // 2, -1.0, 1.0).astype(f)[:, None]
    rope2 = np.stack([np.tile(np.cos(a2), (1, BT)), np.tile(np.sin(a2) * sign, (1, BT))]).astype(f)
    head2 = (token[:, None] // 16 == np.arange(8)[None, :]).astype(f)
    a4 = np.tile(angles(CTX, 64), (2, 1))
    rope4 = np.stack([np.cos(a4), np.sin(a4)]).astype(f)
    turn4 = np.stack([np.ones(P), np.where(token % 64 < 32, 1.0, -1.0)], axis=1).astype(f)
    return {"masks": masks, "rope2": rope2, "head2": head2, "rope4": rope4, "turn4": turn4,
            "count6": np.concatenate([np.tile(8 - np.arange(8), (P, 1)),
                                      token[:, None] + P * np.arange(8)[None, :]], axis=1).astype(f),
            "iota6": np.arange(8 * P).astype(f), "earlier6": (token[:, None] < token[None, :]).astype(f)}


def kernel(**inputs):
    import numpy as _np
    import concourse.bacc as _bacc
    from concourse import mybir as _mybir
    from concourse.bass_utils import run_bass_kernel_spmd as _run

    a = {k: _np.asarray(v) for k, v in inputs.items()}

    def pairs(v):
        return v.reshape(-1, P).T

    lay = {
        "x": a["x"].reshape(B * S, D),
        "ctx_1024": a["ctx_1024"].reshape(B * CTX, D).reshape(B, CTX, D),
        "ctx_T": a["ctx_1024"].transpose(0, 2, 1),
        "L0_xattn_Wq": a["L0_xattn_Wq"].reshape(D, -1),
        "L0_xattn_WkT": a["L0_xattn_Wk"].reshape(D, -1).T,
        "L0_xattn_Wv": a["L0_xattn_Wv"].reshape(D, -1),
        "L0_xattn_Wo": a["L0_xattn_Wo"].reshape(-1, D),
        "L0_xattn_bq": pairs(a["L0_xattn_bq"].reshape(-1)),
        "L0_xattn_bk": pairs(a["L0_xattn_bk"].reshape(-1)),
        "L0_xattn_bv": pairs(a["L0_xattn_bv"].reshape(-1)),
        "L0_xattn_bo": a["L0_xattn_bo"],
    }
    for name in ("wq", "bq", "wqc", "bqc", "wqr", "bqr", "wkv", "bkv", "wkr", "bkr", "wkc", "bkc", "wv", "bv",
                 "wo", "bo"):
        lay["L0_attn_" + name] = a["L0_attn_" + name]
    for name in ("theta", "phi", "theta_noise", "phi_noise"):
        lay["L0_ffn_" + name] = a["L0_ffn_" + name]
    for name in ("gamma_x", "beta_x", "gamma_l", "beta_l", "Wq", "Wkv", "Wo"):
        lay["L1_xattn_" + name] = a["L1_xattn_" + name]
    lay["L1_xattn_Wq_turned"] = a["L1_xattn_Wq"].reshape(D, -1, 2, 32)[:, :, ::-1].reshape(D, -1)
    for name in ("L1_attn_Wq", "L1_attn_Wk", "L1_attn_Wv", "L1_attn_Wpost", "L1_ffn_Wr", "L1_ffn_W1", "L1_ffn_W2"):
        lay[name] = a[name]
    lay |= constants()
    nc = _bacc.Bacc("TRN2", target_bir_lowering=False, num_devices=1)
    arrays, g = {}, {}
    for name, v in lay.items():
        v = _np.ascontiguousarray(v)
        arrays[f"in_{name}"] = v
        g[name] = nc.dram_tensor(f"in_{name}", v.shape, _mybir.dt.from_np(v.dtype), kind="ExternalInput").ap()
    out = nc.dram_tensor("out", (B * S, D), F32, kind="ExternalOutput").ap()
    program(nc, g, out)
    r = _run(nc, [arrays], core_ids=[0])
    return r.results[0]["out"].reshape(B, S, D)
```

```python
from contextlib import ExitStack, contextmanager

import numpy as np

import concourse.bass as bass
from concourse import mybir

F32 = mybir.dt.float32
ACT = mybir.ActivationFunctionType
ALU = mybir.AluOpType
AX = mybir.AxisListType

P = 128
B, S, D = 16, 64, 256
T = B * S // P
BT = P // S
KD = D // P
CTX = 1024
KC = CTX // P
BANK = 512
HALF = CTX // BANK
EPS = 1e-5
MASKED = -1.0e30


class Mark:

    def __init__(self, line):
        self.line, self.n, self.base, self.per, self.epoch = line, line.n, line.total, line.per, line.epoch

    def at(self, iteration):
        return (iteration * self.per + (self.base + self.n)) * self.line.step


class Line:

    def __init__(self, nc, ctx, name, step=1):
        self.name, self.sem = name, ctx.enter_context(nc.semaphore(name))
        self.step, self.total, self.epoch, self.i, self.per, self.n = step, 0, 0, None, 0, 0

    def __call__(self, instruction):
        instruction.then_inc(self.sem, self.step)
        self.n += 1
        return Mark(self)

    def start(self, per, i):
        self.total, self.n, self.per, self.i, self.epoch = self.total + self.n, 0, per, i, self.epoch + 1

    def stop(self, times):
        assert self.n == self.per, f"{self.name}: {self.n} counts in the loop, {self.per} declared"
        self.total, self.n, self.per, self.i = self.total + self.per * times, 0, 0, None
        self.epoch += 1

    def before(self):
        if self.i is None:
            return (self.total + self.n) * self.step
        return self.i * (self.per * self.step) + self.total * self.step


def wait(engine, *marks):
    for m in marks:
        if m is None:
            continue
        line = m.line
        if m.epoch == line.epoch and line.i is not None:
            engine.wait_ge(line.sem, line.i * (line.per * line.step) + (line.total + m.n) * line.step)
        elif m.epoch == line.epoch:
            engine.wait_ge(line.sem, (line.total + m.n) * line.step)
        else:
            engine.wait_ge(line.sem, line.total * line.step)


def wait_before(engine, *lines):
    for line in lines:
        engine.wait_ge(line.sem, line.before())



def program(nc, g, out):
    with ExitStack() as ctx:
        build(nc, ctx, g, out)


def build(nc, ctx, g, out):
    pe, dve, act, pool, sp = nc.tensor, nc.vector, nc.scalar, nc.gpsimd, nc.sync

    def sb(name, shape, stack=ctx, dt=F32):
        return stack.enter_context(nc.sbuf_tensor(name, shape, dt))

    PE, DVE, AC, PL = (Line(nc, ctx, n) for n in ("s_pe", "s_dve", "s_act", "s_pool"))
    engine_of = {PE: pe.engine, DVE: dve.engine, AC: act.engine, PL: pool.engine}

    @contextmanager
    def tiles(times, **per):
        lines = {"pe": PE, "dve": DVE, "act": AC, "pool": PL}
        with nc.Fori(0, times, engines=tuple(engine_of[lines[k]] for k in per)) as i:
            for k, n in per.items():
                lines[k].start(n, i)
            yield i
        for k in per:
            lines[k].stop(times)

    def meet(*engines):
        for e in engines or (pe, dve, act, pool, sp):
            wait_before(e, *(l for l in (PE, DVE, AC, PL) if l.total + l.n))

    x = sb("x", [P, T, D])
    xn = sb("xn", [P, T + 1, D])
    ident = sb("ident", [P, P])
    ones = sb("ones", [P, P])
    big = sb("big", [P, 8192])
    ctx_buf = [sb(f"ctx_buf{b}", [P, KC, D]) for b in range(BT)]
    ctxT_buf = [sb(f"ctxT_buf{b}", [P, KD, CTX]) for b in range(BT)]
    st6 = sb("st6", [P, T, 6])
    mv = sb("mv", [P, T, 2])
    rstd = sb("rstd", [P, T])
    sd = sb("sd", [P, T])
    banks = [ctx.enter_context(nc.psum_tensor(f"bank{n}", [P, 2 * BANK], F32)) for n in range(4)]

    def bank(n):
        return banks[n // 2][:, (n % 2) * BANK:(n % 2 + 1) * BANK]

    def stream(name):
        return Line(nc, ctx, name, 16)

    d_x, d_w1, d_w2, d_w3, d_w4, d_w5, d_w6, d_out = (
        stream(n) for n in ("d_x", "d_w1", "d_w2", "d_w3", "d_w4", "d_w5", "d_w6", "d_out"))
    d_ctx = [stream(f"d_ctx{b}") for b in range(BT)]
    d_raw = stream("d_raw")
    H1, M1 = 16, 8
    Wq1, WkT1, Wv1, Wo1 = (big[:, n * 2048:(n + 1) * 2048] for n in range(4))
    Wq1 = Wq1.rearrange("p (k n) -> p k n", k=KD)
    WkT1 = WkT1.rearrange("p (m d) -> p m d", m=M1)
    Wv1 = Wv1.rearrange("p (k n) -> p k n", k=KD)
    Wo1 = Wo1.rearrange("p (m d) -> p m d", m=M1)
    bq1, bk1, bv1 = (sb(n, [P, M1]) for n in ("bq1", "bk1", "bv1"))
    bo1 = sb("bo1", [P, D])

    def rows(name):
        return g[name].rearrange("(k p) n -> p k n", p=P)

    def everywhere(name):
        return g[name].partition_broadcast(P)

    d_x(sp.dma_start(x[:, :, :], g["x"].rearrange("(t p) d -> p t d", p=P)))
    d_w1(sp.dma_start(Wq1, rows("L0_xattn_Wq")))
    d_w1(sp.dma_start(WkT1, rows("L0_xattn_WkT")))
    for dst, name in ((bq1, "L0_xattn_bq"), (bk1, "L0_xattn_bk"), (bv1, "L0_xattn_bv")):
        d_w1(act.dma_start(dst[:, :], g[name]))
    d_w1(act.dma_start(bo1[:, :], everywhere("L0_xattn_bo")))
    ctx_rows = g["ctx_1024"].rearrange("(t b) (k p) d -> t b p k d", b=BT, p=P)
    ctxT_rows = g["ctx_T"].rearrange("(t b) (k p) c -> t b p k c", b=BT, p=P)

    def load_ctx(b, t):
        src = [rows_[bass.ds(t, 1), b].rearrange("a p k n -> (a p) k n") for rows_ in (ctxT_rows, ctx_rows)]
        d_ctx[b](sp.dma_start(ctxT_buf[b][:, :, :], src[0]))
        d_ctx[b](sp.dma_start(ctx_buf[b][:, :, :], src[1]))

    load_ctx(0, 0)
    d_w1(sp.dma_start(Wv1, rows("L0_xattn_Wv")))
    d_w1(sp.dma_start(Wo1, rows("L0_xattn_Wo")))
    load_ctx(1, 0)

    PL(pool.memset(ones[:, :], 1.0))
    m = PL(pool.memset(ident[:, :], 0.0))
    wait(pool, m)
    m_ident = PL(pool.affine_select(out=ident[:, :], in_=ident[:, :], compare_op=ALU.not_equal, fill=1.0, base=0,
                                    pattern=[[-1, P]], channel_multiplier=1))
    wait(pe, m_ident)
    PE(pe.matmul(bank(7)[:, 0:P], ones[:, :], ident[:, :], start=True, stop=True))

    def moments(src):
        with tiles(T, dve=1) as i:
            DVE(dve.bn_stats(st6[:, i, :], src[:, i, :]))
        wait_before(dve, DVE)
        for t in range(T):
            m = DVE(dve.bn_aggr(mv[:, t, :], st6[:, t, :]))
        wait(dve, m)
        m = DVE(dve.tensor_scalar(sd[:, :], mv[:, :, 1], EPS, None, ALU.add))
        wait(act, m)
        m = AC(act.activation(sd[:, :], sd[:, :], ACT.Sqrt))
        wait(dve, m)
        wait(dve, DVE(dve.reciprocal(rstd[:, :], sd[:, :])))

    def normed(dst, src, i):
        return DVE(dve.tensor_scalar(dst, src[:, bass.ds(i, 1), :].rearrange("p a d -> p (a d)"),
                                     mv[:, bass.ds(i, 1), 0], rstd[:, bass.ds(i, 1)], ALU.subtract, ALU.mult))

    mask = sb("mask", [P, 2, P])
    d_w2(act.dma_start(mask[:, :, :], g["masks"].rearrange("m p k -> p m k")))

    def transposed_tile(src, dst, into):
        for k in range(KD):
            m = pe.transpose(into[:, k * P:(k + 1) * P], src[:, k * P:(k + 1) * P], ident[:, :])
        m = PE(m)
        wait(dve, m)
        return DVE(dve.tensor_copy(dst[:, :, :], into[:, 0:D].rearrange("p (k n) -> p k n", k=KD)))

    def tile_softmax(m_scores, ps, sm, small, scale, which):
        wait(dve, m_scores)
        m = DVE(dve.scalar_tensor_tensor(sm[:, :, :], ps[:, :].rearrange("p (h k) -> p h k", h=8), scale,
                                         mask[:, which:which + 1, :].broadcast_to([P, 8, P]), ALU.mult, ALU.add))
        yield m
        wait(dve, m)
        m = DVE(dve.tensor_reduce(small[:, 0, :], sm[:, :, :], AX.X, ALU.max))
        wait(dve, m)
        m = DVE(dve.tensor_tensor(sm[:, :, :], sm[:, :, :], small[:, 0, :].unsqueeze(2).broadcast_to([P, 8, P]),
                                  ALU.subtract))
        wait(act, m)
        m = AC(act.activation(sm[:, :, :], sm[:, :, :], ACT.Exp))
        yield m
        wait(dve, m)
        m = DVE(dve.tensor_reduce(small[:, 0, :], sm[:, :, :], AX.X, ALU.add))
        wait(dve, m)
        m = DVE(dve.reciprocal(small[:, 1, :], small[:, 0, :]))
        yield m

    def tile_transposes(m_prob, ps, sm, smT):
        wait(pe, m_prob)
        marks = []
        for hf, (line, e) in enumerate(((DVE, dve), (AC, act))):
            for h in range(4 * hf, 4 * hf + 4):
                m = pe.transpose(ps[:, h * P:(h + 1) * P], sm[:, h, :], ident[:, :])
            m = PE(m)
            wait(e, m)
            dst = smT[:, 4 * hf:4 * hf + 4, :]
            src = ps[:, 4 * hf * P:4 * (hf + 1) * P].rearrange("p (h q) -> p h q", h=4)
            marks.append(line(e.tensor_copy(dst, src) if e is dve else e.activation(dst, src, ACT.Copy)))
        return marks

    def interleave(*bodies):
        left = list(bodies)
        while left:
            left = [b for b in left if next(b, "end") != "end"]

    U2 = 2

    HD2, DC = 16, 64
    w_qkv2 = sb("w_qkv2", [P, KD, P])
    b_qkv2 = sb("b_qkv2", [P, 1])
    w_c2 = sb("w_c2", [P, 2, P])
    w_r2 = sb("w_r2", [P, 4, KD, P])
    b_c2 = sb("b_c2", [P, 2])
    b_r2 = sb("b_r2", [P, 4])
    w_v2 = sb("w_v2", [P, D])
    b_v2 = sb("b_v2", [P, D])
    w_o2 = sb("w_o2", [P, KD, D])
    b_o2 = sb("b_o2", [P, D])
    rope2 = sb("rope2", [P, 2, P])
    head2 = sb("head2", [P, 8])
    HF = P // 2
    m = PL(pool.memset(w_c2[:, :, :], 0.0))
    m = PL(pool.memset(w_v2[:, :], 0.0))
    wait(act, m)
    d_w2(act.dma_start(w_qkv2[:, :, 0:DC], rows("L0_attn_wq")))
    d_w2(act.dma_start(w_qkv2[:, :, DC:2 * DC], rows("L0_attn_wkv")))
    d_w2(act.dma_start(b_qkv2[0:DC, :], g["L0_attn_bq"].unsqueeze(1)))
    d_w2(act.dma_start(b_qkv2[DC:2 * DC, :], g["L0_attn_bkv"].unsqueeze(1)))
    d_w2(act.dma_start(w_c2[0:DC, 0, :], g["L0_attn_wqc"]))
    d_w2(act.dma_start(w_c2[DC:2 * DC, 1, :], g["L0_attn_wkc"]))
    d_w2(act.dma_start(w_v2[DC:2 * DC, :], g["L0_attn_wv"]))
    d_w2(act.dma_start(w_o2[:, :, :], rows("L0_attn_wo")))
    for n, (w, v) in enumerate((("L0_attn_wqr", "L0_attn_bqr"), ("L0_attn_wkr", "L0_attn_bkr"))):
        d_w2(act.dma_start(b_c2[:, n:n + 1], g[("L0_attn_bqc", "L0_attn_bkc")[n]].unsqueeze(1)))
        d_w2(act.dma_start(w_r2[:, 2 * n, :, :], rows(w)))
        d_w2(act.dma_start(b_r2[:, 2 * n:2 * n + 1], g[v].unsqueeze(1)))
        for h in range(2):
            to, fro = slice(h * HF, (h + 1) * HF), slice((1 - h) * HF, (2 - h) * HF)
            d_w2(act.dma_start(w_r2[:, 2 * n + 1, :, to], rows(w)[:, :, fro]))
            d_w2(act.dma_start(b_r2[to, 2 * n + 1:2 * n + 2], g[v][fro].unsqueeze(1)))
    d_w2(act.dma_start(b_v2[:, :], everywhere("L0_attn_bv")))
    d_w2(act.dma_start(b_o2[:, :], everywhere("L0_attn_bo")))
    d_w2(act.dma_start(rope2[:, :, :], g["rope2"].rearrange("c p t -> p c t")))
    d_w2(act.dma_start(head2[:, :], g["head2"]))

    trig3 = sb("trig3", [P, 2, KD, D])
    noise3, turns3 = (xn[:, h * 4:h * 4 + 4, :].rearrange("p (n k) d -> p n k d", n=2) for h in range(2))
    for n, name in enumerate(("theta", "phi")):
        d_w3(act.dma_start(trig3[:, n, :, :], rows("L0_ffn_" + name)))
        d_w3(act.dma_start(noise3[:, n, :, :], rows(f"L0_ffn_{name}_noise")))

    H4, M4 = 8, 4
    w_q4 = sb("w_q4", [P, 2, KD, M4 * P])
    w_k4 = sb("w_k4", [P, KD, M4 * P])
    w_v4 = sb("w_v4", [P, KD, M4 * P])
    w_o4 = sb("w_o4", [P, M4, D])
    gb4 = sb("gb4", [P, 4, D])
    rope4 = sb("rope4", [P, 2, CTX])
    turn4 = sb("turn4", [P, 2])
    stats_c = sb("stats_c", [P, B * KC, 6])
    mean_c = sb("mean_c", [P, (B + BT) * KC])
    rstd_c = sb("rstd_c", [P, (B + BT) * KC])
    INNER = M4 * P
    d_w4(sp.dma_start(w_q4[:, 0, :, :], rows("L1_xattn_Wq")))
    d_w4(sp.dma_start(w_q4[:, 1, :, :], rows("L1_xattn_Wq_turned")))
    d_w4(sp.dma_start(w_k4[:, :, :], rows("L1_xattn_Wkv")[:, :, 0:INNER]))
    d_w4(sp.dma_start(w_v4[:, :, :], rows("L1_xattn_Wkv")[:, :, INNER:2 * INNER]))
    d_w4(sp.dma_start(w_o4[:, :, :], rows("L1_xattn_Wo")))
    for n, name in enumerate(("gamma_x", "beta_x", "gamma_l", "beta_l")):
        d_w4(sp.dma_start(gb4[:, n, :], everywhere("L1_xattn_" + name)))
    d_w4(sp.dma_start(rope4[:, :, :], g["rope4"].rearrange("c p t -> p c t")))
    d_w4(sp.dma_start(turn4[:, :], g["turn4"]))

    M5 = 8
    E, F, CAP = 8, 1024, 128
    Wq5, Wk5, Wv5, Wo5 = (big[:, n * 2048:(n + 1) * 2048] for n in range(4))
    Wq5, Wk5, Wv5 = (w.rearrange("p (k n) -> p k n", k=KD) for w in (Wq5, Wk5, Wv5))
    Wo5 = Wo5.rearrange("p (m d) -> p m d", m=M5)
    w_r6 = sb("w_r6", [P, KD, E])
    count6 = sb("count6", [P, 2 * E])
    d_w6(sp.dma_start(w_r6[:, :, :], rows("L1_ffn_Wr")))
    d_w6(sp.dma_start(count6[:, :], g["count6"]))
    w1_ring = [ctxT_buf[0][:, :, :], ctxT_buf[1][:, :, :]] + \
        [big[:, 4096 * n:4096 * n + 2048].rearrange("p (k f) -> p k f", k=KD) for n in range(2)]
    w2_ring = [ctx_buf[0][:, :, :], ctx_buf[1][:, :, :]] + \
        [big[:, 4096 * n + 2048:4096 * n + 4096].rearrange("p (f d) -> p f d", d=D) for n in range(2)]
    d_e = stream("d_e")

    def load_expert(n):
        d_e(sp.dma_start(w1_ring[n % 4], g["L1_ffn_W1"][n].rearrange("(k p) f -> p k f", p=P)))
        d_e(sp.dma_start(w2_ring[n % 4], g["L1_ffn_W2"][n].rearrange("(f p) d -> p f d", p=P)))

    wait_before(dve, d_x)
    moments(x)

    with ExitStack() as tmp:
        def tb(name, shape):
            return sb(name, shape, tmp)

        G = M1 // 2
        xs = tb("xs1", [P, D])
        xT = tb("xT1", [P, KD, P])
        q_bd = tb("q_bd1", [P, M1, BT, P])
        qp = [tb(f"qp1_{n}", [P, KD, 2 * P]) for n in range(2)]
        qbk = [tb(f"qbk1_{n}", [P, 2]) for n in range(2)]
        prob = [tb(f"prob1_{n}", [P, CTX]) for n in range(2)]
        probT = tb("probT1", [P, KC, 2 * P])
        u_sb = tb("u1", [P, KD, 2 * P])
        attn = tb("attn1", [P, M1, P])
        mx, nb, rs, ri = ([tb(f"{a}1_{n}", [P, 1]) for n in range(2)] for a in ("mx", "nb", "rs", "ri"))
        SCALE1 = 1.0 / 8.0
        DVE(dve.memset(q_bd[:, :, :, :], 0.0))
        QP, U, TP = bank(6), bank(7), (bank(4), bank(5))
        wait_before(pe, d_w1)
        wait_before(dve, d_w1)

        with tiles(T, pe=85, dve=152, act=40) as i:
            wait_before(dve, PE, DVE)
            wait_before(pe, DVE, AC)
            m = normed(xs[:, :], x, i)
            wait(pe, m)
            for k in range(KD):
                m = PE(pe.transpose(QP[:, k * P:(k + 1) * P], xs[:, k * P:(k + 1) * P], ident[:, :]))
            wait(dve, m)
            m_xT = DVE(dve.tensor_copy(xT[:, :, :], QP[:, 0:D].rearrange("p (k n) -> p k n", k=KD)))
            wait(pe, m_xT)
            for half in range(2):
                for mm in range(4):
                    for k in range(KD):
                        pair = half * 4 + mm
                        m = pe.matmul(bank(half)[:, mm * P:(mm + 1) * P], Wq1[:, k, pair * P:(pair + 1) * P],
                                      xT[:, k, :], start=k == 0, stop=k == KD - 1)
                m = PE(m)
                wait(dve, m)
                for h in range(2):
                    r = slice(h * S, (h + 1) * S)
                    ps = bank(half)[r, :].rearrange("p (m b q) -> p m b q", m=4, b=BT)
                    bias = bq1[r, half * 4:(half + 1) * 4].unsqueeze(2).unsqueeze(3).broadcast_to([S, 4, BT, S])
                    m_q = DVE(dve.tensor_tensor(q_bd[r, half * 4:(half + 1) * 4, :, r], ps, bias, ALU.add))

            m_stats = {}
            steps = [(b, s) for b in range(BT) for s in range(G)]
            m_qp, m_qbk, m_S, m_exp, m_T, m_PT, m_PV, m_u, m_OB, m_at, m_P = ({} for _ in range(11))

            def project(n):
                b, s = steps[n]
                wait(pe, m_q, m_qbk.get(n - 1))
                for pr in range(2):
                    for k in range(KD):
                        m = pe.matmul(QP[:, (k * 2 + pr) * P:(k * 2 + pr + 1) * P],
                                      WkT1[:, 2 * s + pr, k * P:(k + 1) * P], q_bd[:, 2 * s + pr, b, :],
                                      start=True, stop=True)
                m = PE(m)
                wait(act, m, m_S.get((n - 2, 1)))
                m_qp[n] = AC(act.activation(qp[n % 2][:, :, :], QP.rearrange("p (k n) -> p k n", k=KD), ACT.Copy))

            def scores(n, pr):
                b, s = steps[n]
                wait(pe, m_qp[n], m_exp.get((n - 1, pr)))
                if s == 0 and pr == 0:
                    pe.wait_ge(d_ctx[b].sem, i * 32 + 32)
                    dve.wait_ge(d_ctx[b].sem, i * 32 + 32)
                for half in range(HALF):
                    for k in range(KD):
                        m = pe.matmul(banks[pr][:, half * BANK:(half + 1) * BANK], qp[n % 2][:, k, pr * P:(pr + 1) * P],
                                      ctxT_buf[b][:, k, half * BANK:(half + 1) * BANK],
                                      start=k == 0, stop=k == KD - 1)
                m_S[n, pr] = PE(m)

            def query_dot_bias(n):
                b, s = steps[n]
                wait(pe, m_qp[n])
                for pr in range(2):
                    m = pe.matmul(QP[:, pr:pr + 1], q_bd[:, 2 * s + pr, b, :], bk1[:, 2 * s + pr:2 * s + pr + 1],
                                  start=True, stop=True)
                m = PE(m)
                wait(dve, m)
                m_qbk[n] = DVE(dve.tensor_copy(qbk[n % 2][:, :], QP[:, 0:2]))

            def softmax(n, pr):
                wait(dve, m_S[n, pr])
                m = DVE(dve.tensor_reduce(mx[pr][:, :], banks[pr][:, :], AX.X, ALU.max))
                wait(dve, m, m_qbk[n])
                m = DVE(dve.tensor_scalar(nb[pr][:, :], mx[pr][:, :], qbk[n % 2][:, pr:pr + 1], -SCALE1,
                                          ALU.add, ALU.mult))
                wait(dve, m)
                m = DVE(dve.scalar_tensor_tensor(nb[pr][:, :], qbk[n % 2][:, pr:pr + 1], SCALE1, nb[pr][:, :],
                                                 ALU.mult, ALU.add))
                wait(act, m, m_T.get((n - 1, pr)))
                m_exp[n, pr] = AC(act.activation(prob[pr][:, :], banks[pr][:, :], ACT.Exp, bias=nb[pr][:, 0:1],
                                                 scale=SCALE1, accum_out=rs[pr][:, 0:1]))
                wait(dve, m_exp[n, pr])
                m = DVE(dve.reciprocal(ri[pr][:, :], rs[pr][:, :]))
                wait(dve, m)
                m_P[n, pr] = DVE(dve.tensor_scalar(prob[pr][:, :], prob[pr][:, :], ri[pr][:, 0:1], None, ALU.mult))

            def transposed(n, pr):
                before = (n, 0) if pr else (n - 1, 1)
                wait(pe, m_P[n, pr], m_PT.get((*before, 0)), m_PT.get((*before, 1)))
                for c in range(KC):
                    t = pe.transpose(TP[c // 4][:, (c % 4) * P:(c % 4 + 1) * P], prob[pr][:, c * P:(c + 1) * P],
                                     ident[:, :])
                    if c == 3:
                        first = PE(t)
                m_T[n, pr] = PE(t)
                for hf, e, m in ((0, dve, first), (1, act, m_T[n, pr])):
                    wait(e, m, m_PV.get(n - 1))
                    dst = probT[:, hf * 4:(hf + 1) * 4, pr * P:(pr + 1) * P]
                    src = TP[hf].rearrange("p (c q) -> p c q", c=4)
                    if hf == 0:
                        m_PT[n, pr, 0] = DVE(dve.tensor_copy(dst, src))
                    else:
                        m_PT[n, pr, 1] = AC(act.activation(dst, src, ACT.Copy))

            def context_stats(n):
                b, s = steps[n]
                for c in (2 * s, 2 * s + 1):
                    at = (i * BT + b) * KC + c
                    dst = stats_c[:, bass.ds(at, 1), :].rearrange("p a s -> p (a s)")
                    m_stats[n] = DVE(dve.bn_stats(dst, ctx_buf[b][:, c, :]))

            def average(n):
                b, s = steps[n]
                wait(pe, m_PT[n, 1, 0], m_PT[n, 1, 1], m_at.get(n - 1))
                wait(pe, m_stats[n])
                for k in range(KD):
                    for c in range(KC):
                        m = pe.matmul(U[:, k * 2 * P:(k + 1) * 2 * P], ctx_buf[b][:, c, k * P:(k + 1) * P],
                                      probT[:, c, :], start=c == 0, stop=c == KC - 1)
                m_PV[n] = PE(m)
                wait(dve, m_PV[n], m_OB.get(n - 1))
                m_u[n] = DVE(dve.tensor_copy(u_sb[:, :, :], U.rearrange("p (k n) -> p k n", k=KD)))

            def values(n):
                b, s = steps[n]
                wait(pe, m_u[n])
                for pr in range(2):
                    for k in range(KD):
                        pair = 2 * s + pr
                        m = pe.matmul(U[:, pr * P:(pr + 1) * P], Wv1[:, k, pair * P:(pair + 1) * P],
                                      u_sb[:, k, pr * P:(pr + 1) * P], start=k == 0, stop=k == KD - 1)
                m_OB[n] = PE(m)
                wait(dve, m_OB[n])
                for h in range(2):
                    r = slice(h * S, (h + 1) * S)
                    bias = bv1[r, 2 * s:2 * s + 2].unsqueeze(2).broadcast_to([S, 2, S])
                    m_at[n] = DVE(dve.tensor_tensor(attn[r, 2 * s:2 * s + 2, b * S:(b + 1) * S],
                                                    U[r, 0:2 * P].rearrange("p (r n) -> p r n", r=2)[:, :, r],
                                                    bias, ALU.add))

            last = len(steps) - 1
            project(0)
            query_dot_bias(0)
            scores(0, 0)
            for n in range(last + 1):
                scores(n, 1)
                softmax(n, 0)
                if n < last:
                    project(n + 1)
                softmax(n, 1)
                if n > 0:
                    average(n - 1)
                transposed(n, 0)
                if n > 0:
                    values(n - 1)
                if n < last:
                    query_dot_bias(n + 1)
                    scores(n + 1, 0)
                transposed(n, 1)
                context_stats(n)
            average(last)
            values(last)
            wait(pe, m_at[last])
            for mm in range(M1):
                m = pe.matmul(U[:, 0:D], attn[:, mm, :], Wo1[:, mm, :], start=mm == 0, stop=mm == M1 - 1)
            m = PE(m)
            wait(dve, m)
            m = DVE(dve.tensor_tensor(xs[:, :], U[:, 0:D], bo1[:, :], ALU.add))
            wait(dve, m)
            DVE(dve.tensor_tensor(x[:, i, :], x[:, i, :], xs[:, :], ALU.add))
            ctx_read = [m_PV[G - 1], m_PV[2 * G - 1]]
        with nc.Fori(0, T - 1, engines=(sp.engine,)) as j:
            for b in range(BT):
                sp.wait_ge(PE.sem, ctx_read[b].at(j))
                load_ctx(b, j + 1)
        wait_before(sp, PE)
        d_w5(sp.dma_start(Wq5, rows("L1_attn_Wq")))
        d_w5(sp.dma_start(Wk5, rows("L1_attn_Wk")))
        d_w5(sp.dma_start(Wv5, rows("L1_attn_Wv")))
        d_w5(sp.dma_start(Wo5, rows("L1_attn_Wpost")))

    meet()
    moments(x)
    wait_before(dve, d_w3)
    a3, t3 = trig3[:, :, :, :], turns3
    wait(dve, DVE(dve.tensor_tensor(a3, a3, noise3[:, :, :, :], ALU.add)))
    ROUND = 1.5 * 2.0 ** 23
    wait(dve, DVE(dve.tensor_scalar(t3, a3, 1.0 / (2.0 * np.pi), ROUND, ALU.mult, ALU.add)))
    wait(dve, DVE(dve.tensor_scalar(t3, t3, ROUND, None, ALU.subtract)))
    high = 6.28125
    for part in (high, 2.0 * np.pi - high):
        wait(dve, DVE(dve.scalar_tensor_tensor(a3, t3, -float(part), a3, ALU.mult, ALU.add)))
    PI = 3.1415925
    wait(dve, DVE(dve.tensor_scalar(a3, a3, -PI, PI, ALU.max, ALU.min)))
    c3 = trig3[:, 0, :, :]
    wait(dve, DVE(dve.scalar_tensor_tensor(c3, c3, -1.0, c3, ALU.mult, ALU.min)))
    m = DVE(dve.tensor_scalar(c3, c3, float(np.pi / 2), None, ALU.add))
    wait(act, m)
    AC(act.activation(a3, a3, ACT.Sin))
    with ExitStack() as tmp:
        def buffers(name, shape):
            return [sb(f"{name}_{u}", shape, tmp) for u in range(U2)]

        xs, xT, c2, t2 = buffers("xs2", [P, D]), buffers("xT2", [P, KD, P]), buffers("c2", [P, P]), \
            buffers("t2", [P, 4, P])
        qT, kT, km = buffers("qT2", [P, 2, P]), buffers("kT2", [P, 2, P]), buffers("km2", [P, 2, 8, P])
        v, sm = buffers("v2", [P, D]), buffers("sm2", [P, 2, 8, P])
        smT, small, o, oT = buffers("smT2", [P, 2, 8, P]), buffers("small2", [P, 2, 2, 8]), \
            buffers("o2", [P, D]), buffers("oT2", [P, KD, P])
        wait_before(pe, d_w2)
        wait_before(dve, d_w2)
        wait_before(act, d_w2)

        def body2(i, u):
            t = i * U2 + u
            A, C = banks[2 * u], banks[2 * u + 1]
            a0, a1, c0, c1 = (bank(4 * u + n) for n in range(4))
            m = normed(xs[u][:, :], x, t)
            wait(pe, m)
            yield
            m_xT = transposed_tile(xs[u], xT[u], a0)
            wait(pe, m_xT)
            yield
            for k in range(KD):
                m = pe.matmul(a1[:, 0:P], w_qkv2[:, k, :], xT[u][:, k, :], start=k == 0, stop=k == KD - 1)
            m = PE(m)
            wait(act, m)
            m_c = AC(act.activation(c2[u][:, :], a1[:, 0:P], ACT.Gelu, bias=b_qkv2[:, 0:1]))
            for r in range(4):
                for k in range(KD):
                    m = pe.matmul(c0[:, r * P:(r + 1) * P], w_r2[:, r, k, :], xT[u][:, k, :],
                                  start=k == 0, stop=k == KD - 1)
            m_r = PE(m)
            yield
            wait(pe, m_c)
            for n in range(2):
                m = pe.matmul(a0[:, n * P:(n + 1) * P], w_c2[:, n, :], c2[u][:, :], start=True, stop=True)
            m_cc = PE(m)
            m_v = PE(pe.matmul(c1[:, 0:D], c2[u][:, :], w_v2[:, :], start=True, stop=True))
            wait(dve, m_r)
            for r in range(4):
                m = DVE(dve.scalar_tensor_tensor(t2[u][:, r, :], c0[:, r * P:(r + 1) * P], b_r2[:, r:r + 1],
                                                 rope2[:, r % 2, :], ALU.add, ALU.mult))
            wait(dve, m)
            t4 = t2[u][:, :, :].rearrange("p (n s) t -> p n s t", s=2)
            m_rot = DVE(dve.tensor_tensor(t4[:, :, 0, :], t4[:, :, 0, :], t4[:, :, 1, :], ALU.add))
            yield
            wait(act, m_cc)
            for n, dst in enumerate((qT[u], kT[u])):
                AC(act.activation(dst[:, 0, :], a0[:, n * P:(n + 1) * P], ACT.Gelu, bias=b_c2[:, n:n + 1]))
            wait(act, m_rot)
            for n, dst in enumerate((qT[u], kT[u])):
                m_qk = AC(act.activation(dst[:, 1, :], t2[u][:, 2 * n, :], ACT.Gelu))
            wait(dve, m_v)
            m_v = DVE(dve.tensor_tensor(v[u][:, :], c1[:, 0:D], b_v2[:, :], ALU.add))
            yield
            wait(dve, m_qk)
            m_S = []
            for c in range(2):
                m = DVE(dve.tensor_tensor(km[u][:, c, :, :], kT[u][:, c:c + 1, :].broadcast_to([P, 8, P]),
                                          head2[:, :].unsqueeze(2).broadcast_to([P, 8, P]), ALU.mult))
                wait(pe, m)
                for hf in range(2):
                    m = pe.matmul((A, C)[c][:, hf * BANK:(hf + 1) * BANK], qT[u][:, c, :],
                                  km[u][:, c, 4 * hf:4 * hf + 4, :], start=True, stop=True)
                m_S.append(PE(m))
                yield
            soft = [tile_softmax(m_S[c], (A, C)[c], sm[u][:, c], small[u][:, c], 1.0 / 4.0, 0) for c in range(2)]
            for step in range(3):
                m_soft = [next(s) for s in soft]
                yield
            m_T = []
            for c in range(2):
                m_T += tile_transposes(m_soft[c], (A, C)[c], sm[u][:, c], smT[u][:, c])
                yield
            wait(pe, *m_T)
            for h in range(16):
                cols = slice(h * HD2, (h + 1) * HD2)
                m = pe.matmul(a0[:, cols], smT[u][:, h // 8, h % 8, :], v[u][:, cols], start=True, stop=True)
            m = PE(m)
            wait(dve, m)
            m = DVE(dve.tensor_tensor(o[u][:, :].rearrange("p (c h e) -> p c h e", c=2, h=8),
                                      a0[:, 0:D].rearrange("p (c h e) -> p c h e", c=2, h=8),
                                      small[u][:, :, 1, :].unsqueeze(3).broadcast_to([P, 2, 8, HD2]), ALU.mult))
            wait(pe, m)
            yield
            m = transposed_tile(o[u], oT[u], a1)
            wait(pe, m)
            yield
            for k in range(KD):
                m = pe.matmul(c0[:, 0:D], oT[u][:, k, :], w_o2[:, k, :], start=k == 0, stop=k == KD - 1)
            m = PE(m)
            wait(dve, m)
            m = DVE(dve.tensor_tensor(o[u][:, :], c0[:, 0:D], b_o2[:, :], ALU.add))
            wait(dve, m)
            xt = x[:, bass.ds(t, 1), :].rearrange("p a d -> p (a d)")
            DVE(dve.tensor_tensor(xt, xt, o[u][:, :], ALU.add))

        with tiles(T // U2, pe=28, dve=52, act=18) as i:
            for e in (pe, dve, act):
                wait_before(e, PE, DVE, AC)
            interleave(*(body2(i, u) for u in range(U2)))

    meet()
    moments(x)
    with ExitStack() as tmp:
        def buffers(name, shape):
            return [sb(f"{name}_{u}", shape, tmp) for u in range(U2)]

        xs, xT, sq = buffers("xs3", [P, D]), buffers("xT3", [P, KD, P]), buffers("sq3", [P, 2, D])

        def body3(i, u):
            t = i * U2 + u
            into, ps = bank(2 * u), bank(2 * u + 1)
            m = normed(xs[u][:, :], x, t)
            wait(pe, m)
            m = transposed_tile(xs[u], xT[u], into)
            wait(pe, m)
            yield
            for n in range(2):
                for k in range(KD):
                    m = pe.matmul(ps[:, n * D:(n + 1) * D], xT[u][:, k, :], trig3[:, n, k, :],
                                  start=k == 0, stop=k == KD - 1)
            m = PE(m)
            wait(act, m)
            m = AC(act.activation(sq[u][:, :, :], ps.rearrange("p (n d) -> p n d", n=2), ACT.Square))
            wait(dve, m)
            yield
            m = DVE(dve.tensor_tensor(sq[u][:, 0, :], sq[u][:, 0, :], sq[u][:, 1, :], ALU.add))
            wait(act, m)
            m = AC(act.activation(sq[u][:, 0, :], sq[u][:, 0, :], ACT.Sqrt))
            yield
            wait(dve, m)
            xt = x[:, bass.ds(t, 1), :].rearrange("p a d -> p (a d)")
            DVE(dve.tensor_tensor(xt, xt, sq[u][:, 0, :], ALU.add))

        with tiles(T // U2, pe=4, dve=8, act=4) as i:
            for e in (pe, dve, act):
                wait_before(e, PE, DVE, AC)
            interleave(*(body3(i, u) for u in range(U2)))

    meet()
    with ExitStack() as tmp:
        def tb(name, shape):
            return sb(name, shape, tmp)

        raw = tb("raw", [P, KC, D])

        def load_ctx4(b, t):
            d_raw(sp.dma_start(raw[:, :, :], ctx_rows[bass.ds(t, 1), b].rearrange("a p k n -> (a p) k n")))

        load_ctx4(0, 0)
        moments(x)
        with tiles(T, dve=1) as i:
            normed(xn[:, bass.ds(i, 1), :].rearrange("p a d -> p (a d)"), x, i)
        wait_before(dve, DVE)
        moments(xn)
        with tiles(T, dve=1) as i:
            normed(xn[:, bass.ds(i, 1), :].rearrange("p a d -> p (a d)"), xn, i)
        wait_before(dve, DVE, d_w4)
        wait(dve, DVE(dve.tensor_tensor(xn[:, 0:T, :], xn[:, 0:T, :], gb4[:, 2:3, :].broadcast_to([P, T, D]), ALU.mult)))
        wait(dve, DVE(dve.tensor_tensor(xn[:, 0:T, :], xn[:, 0:T, :], gb4[:, 3:4, :].broadcast_to([P, T, D]), ALU.add)))
        DVE(dve.tensor_copy(xn[:, T, :], xn[:, 0, :]))
        NC_ = B * KC
        stat = [stats_c[:, 0:NC_, n] for n in range(6)]
        m = DVE(dve.tensor_tensor(mean_c[:, 0:NC_], stat[1], stat[4], ALU.add))
        m = DVE(dve.tensor_tensor(rstd_c[:, 0:NC_], stat[1], stat[4], ALU.subtract))
        wait(dve, m)
        m = DVE(dve.tensor_scalar(mean_c[:, 0:NC_], mean_c[:, 0:NC_], 0.5, None, ALU.mult))
        m = DVE(dve.tensor_tensor(rstd_c[:, 0:NC_], rstd_c[:, 0:NC_], rstd_c[:, 0:NC_], ALU.mult))
        wait(dve, m)
        m = DVE(dve.tensor_scalar(rstd_c[:, 0:NC_], rstd_c[:, 0:NC_], 0.25, EPS, ALU.mult, ALU.add))
        m = DVE(dve.tensor_tensor(stat[2], stat[2], stat[5], ALU.add))
        wait(dve, m)
        m = DVE(dve.scalar_tensor_tensor(rstd_c[:, 0:NC_], stat[2], 1.0 / D, rstd_c[:, 0:NC_], ALU.mult, ALU.add))
        wait(act, m)
        m = AC(act.activation(rstd_c[:, 0:NC_], rstd_c[:, 0:NC_], ACT.Sqrt))
        wait(dve, m)
        m = DVE(dve.reciprocal(rstd_c[:, 0:NC_], rstd_c[:, 0:NC_]))
        wait(dve, m)
        for c in (mean_c, rstd_c):
            m = DVE(dve.tensor_copy(c[:, NC_:NC_ + BT * KC], c[:, 0:BT * KC]))
        wait(dve, m)

        SCALE4 = 1.0 / 8.0
        KEYS = CTX + S
        xs = tb("xs4", [P, D])
        xT = tb("xT4", [P, KD, P])
        lat = tb("lat4", [P, BT, D])
        q_bd = tb("q_bd4", [P, 2, M4, BT, P])
        kcs = tb("kcs4", [P, 2, CTX])
        kl = tb("kl4", [P, M4, BT, S])
        prob = [tb(f"prob4_{n}", [P, KEYS]) for n in range(2)]
        probT = [tb(f"probT4_{n}", [P, KC + 1, 2 * P]) for n in range(2)]
        u_sb = tb("u4", [P, KD, 2 * P])
        attn = tb("attn4", [P, M4, P])
        mx, nb, rs = ([tb(f"{a}4_{n}", [P, 2]) for n in range(2)] for a in ("mx", "nb", "rs"))
        MISC, U, TP = bank(6), bank(7), (bank(4), bank(5))
        KPS, SPS = banks[0], banks[1]
        DVE(dve.memset(q_bd[:, :, :, :, :], 0.0))
        DVE(dve.memset(lat[:, :, :], 0.0))
        for p in probT:
            DVE(dve.memset(p[:, KC, :], 0.0))
        wait_before(pe, d_w4)
        wait_before(dve, d_w4)
        wait_before(pool, d_w4)
        STEPS = M4 // 2
        UNITS = BT * M4

        class Turn:

            def __init__(self):
                self.kcs, self.S, self.exp, self.P, self.T, self.PT, self.latT = ({} for _ in range(7))
                self.A, self.u, self.V, self.at, self.ctxT, self.norm, self.raw = ({} for _ in range(7))
                self.q = []
                self.tp = [None, None]

        def normalize_rows(half, t, b, d_count, w):
            if half == 0:
                dve.wait_ge(d_raw.sem, d_count)
            for c in range(half * KC // 2, (half + 1) * KC // 2):
                at = (t * BT + b) * KC + c
                m = DVE(dve.tensor_scalar(raw[:, c, :], raw[:, c, :], mean_c[:, bass.ds(at, 1)],
                                          rstd_c[:, bass.ds(at, 1)], ALU.subtract, ALU.mult))
            wait(pool, m)
            c = slice(half * KC // 2, (half + 1) * KC // 2)
            w.norm[half] = PL(pool.tensor_tensor(raw[:, c, :], raw[:, c, :],
                                                 gb4[:, 0:1, :].broadcast_to([P, KC // 2, D]), ALU.mult))

        def shift_rows(b, w, read=None):
            wait(pool, read)
            for half in range(2):
                wait(pool, w.norm[half])
                c = slice(half * KC // 2, (half + 1) * KC // 2)
                w.raw[b, half] = PL(pool.tensor_tensor(ctx_buf[b][:, c, :], raw[:, c, :],
                                                       gb4[:, 1:2, :].broadcast_to([P, KC // 2, D]), ALU.add))

        def transpose_context(b, k, w):
            for hf in range(2):
                wait(pe, w.raw[b, hf], w.tp[hf])
                for c in range(4):
                    m = pe.transpose(TP[hf][:, c * P:(c + 1) * P], ctx_buf[b][:, 4 * hf + c, k * P:(k + 1) * P],
                                     ident[:, :])
                m = PE(m)
                dst, src = ctxT_buf[b][:, k, hf * BANK:(hf + 1) * BANK], TP[hf]
                if hf == 0:
                    wait(dve, m)
                    m = DVE(dve.tensor_copy(dst, src))
                else:
                    wait(act, m)
                    m = AC(act.activation(dst, src, ACT.Copy))
                w.tp[hf] = w.ctxT[b, k, hf] = m

        def keys(n, half, w):
            b, m_ = n // M4 % BT, n % M4
            wait(pe, w.kcs.get((n - 1, half)))
            if m_ == 0:
                wait(pe, *(w.ctxT.get((b, k, half)) for k in range(KD)))
            cols = slice(half * BANK, (half + 1) * BANK)
            for k in range(KD):
                m = pe.matmul(KPS[:, cols], w_k4[:, k, m_ * P:(m_ + 1) * P], ctxT_buf[b][:, k, cols],
                              start=k == 0, stop=k == KD - 1)
            m = PE(m)
            wait(dve, m, w.S.get(n - 1))
            for part in range(2):
                m = DVE(dve.tensor_tensor(kcs[:, part, cols], KPS[:, cols], rope4[:, part, cols], ALU.mult))
            w.kcs[n, half] = m

        def scores(n, w):
            b, m_ = n // M4, n % M4
            wait(pe, *(w.q if n == 0 else ()))
            wait(pe, w.kcs.get((n, 0)), w.kcs.get((n, 1)), w.exp.get(n - 1), w.latT.get(n - 1))
            for half in range(HALF):
                for part in range(2):
                    cols = slice(half * BANK, (half + 1) * BANK)
                    pe.matmul(SPS[:, cols], q_bd[:, part, m_, b, :], kcs[:, part, cols],
                              start=part == 0, stop=part == 1)
            w.S[n] = PE(pe.matmul(MISC[:, 0:S], q_bd[:, 0, m_, b, :], kl[:, m_, b, :], start=True, stop=True))

        def exponentials(n, w):
            p = n % 2
            wait(dve, w.S[n])
            DVE(dve.tensor_reduce(mx[p][:, 0:1], SPS[:, :], AX.X, ALU.max))
            m = DVE(dve.tensor_reduce(mx[p][:, 1:2], MISC[:, 0:S], AX.X, ALU.max))
            wait(dve, m)
            m = DVE(dve.tensor_scalar(nb[p][:, 0:1], mx[p][:, 0:1], mx[p][:, 1:2], -SCALE4, ALU.max, ALU.mult))
            wait(act, m, w.T.get(n - 2))
            AC(act.activation(prob[p][:, 0:CTX], SPS[:, :], ACT.Exp, bias=nb[p][:, 0:1], scale=SCALE4,
                              accum_out=rs[p][:, 0:1]))
            w.exp[n] = AC(act.activation(prob[p][:, CTX:KEYS], MISC[:, 0:S], ACT.Exp, bias=nb[p][:, 0:1],
                                         scale=SCALE4, accum_out=rs[p][:, 1:2]))

        def weights(n, w):
            p = n % 2
            wait(dve, w.exp[n])
            m = DVE(dve.tensor_tensor(nb[p][:, 1:2], rs[p][:, 0:1], rs[p][:, 1:2], ALU.add))
            wait(dve, m)
            m = DVE(dve.reciprocal(nb[p][:, 1:2], nb[p][:, 1:2]))
            wait(dve, m)
            w.P[n] = DVE(dve.tensor_scalar(prob[p][:, :], prob[p][:, :], nb[p][:, 1:2], None, ALU.mult))

        def transposed(n, w):
            p, s = n % 2, n // 2
            wait(pe, w.P[n], *w.tp)
            for c in range(KC):
                m = pe.transpose(TP[c // 4][:, (c % 4) * P:(c % 4 + 1) * P], prob[p][:, c * P:(c + 1) * P],
                                 ident[:, :])
                if c == 0:
                    PE(pe.transpose(MISC[0:S, P:2 * P], prob[p][:, CTX:KEYS], ident[:, :]))
                if c == 3:
                    first = PE(m)
            w.T[n] = PE(m)
            cols = slice(p * P, (p + 1) * P)
            wait(dve, first, w.A.get((s - 2, 1)))
            w.latT[n] = DVE(dve.tensor_copy(probT[s % 2][0:S, KC, cols], MISC[0:S, P:2 * P]))
            w.tp[0] = DVE(dve.tensor_copy(probT[s % 2][:, 0:4, cols], TP[0].rearrange("p (c q) -> p c q", c=4)))
            wait(act, w.T[n], w.A.get((s - 2, 1)))
            w.tp[1] = AC(act.activation(probT[s % 2][:, 4:8, cols], TP[1].rearrange("p (c q) -> p c q", c=4), ACT.Copy))
            w.PT[n] = list(w.tp)

        def average(s, k, w):
            b = s // STEPS
            if k == 0:
                wait(pe, *w.PT[2 * s + 1], w.at.get(s - 1))
            else:
                wait(pe, w.u[s, 0])
            for c in range(KC + 1):
                src = ctx_buf[b][:, c, k * P:(k + 1) * P] if c < KC else lat[:, b, k * P:(k + 1) * P]
                m = pe.matmul(U[:, k * 2 * P:(k + 1) * 2 * P], src, probT[s % 2][:, c, :], start=c == 0, stop=c == KC)
            w.A[s, k] = PE(m)
            wait(act, w.A[s, k], w.V.get(s - 1))
            w.u[s, k] = AC(act.activation(u_sb[:, k, :], U[:, k * 2 * P:(k + 1) * 2 * P], ACT.Copy))

        def values(s, w):
            b = s // STEPS
            wait(pe, w.u[s, 1])
            first = 2 * (s % STEPS)
            for pr in range(2):
                for k in range(KD):
                    pair = first + pr
                    m = pe.matmul(U[:, pr * P:(pr + 1) * P], w_v4[:, k, pair * P:(pair + 1) * P],
                                  u_sb[:, k, pr * P:(pr + 1) * P], start=k == 0, stop=k == KD - 1)
            w.V[s] = PE(m)
            wait(dve, w.V[s])
            for h in range(2):
                r = slice(h * S, (h + 1) * S)
                w.at[s] = DVE(dve.tensor_copy(attn[r, first:first + 2, b * S:(b + 1) * S],
                                              U[r, 0:2 * P].rearrange("p (r n) -> p r n", r=2)[:, :, r]))

        w = Turn()
        for half in range(2):
            normalize_rows(half, 0, 0, 16, w)
        shift_rows(0, w)
        m_shift = w.raw[0, 1]
        for k in range(KD):
            transpose_context(0, k, w)
        for half in range(HALF):
            keys(0, half, w)
        DVE(dve.tensor_copy(xs[:, :], xn[:, 0, :]))
        wait(sp, m_shift)
        load_ctx4(1, 0)
        with tiles(T, pe=73, dve=133, act=37, pool=8) as i:
            w = Turn()
            for e in (pe, dve, act, pool):
                wait_before(e, PE, DVE, AC, PL)
            for b in range(BT):
                DVE(dve.tensor_copy(lat[0:S, b, :], xs[b * S:(b + 1) * S, :]))
            m_lnT = transposed_tile(xs, xT, MISC)
            wait(pe, m_lnT)
            for part, ps in enumerate((MISC, U)):
                for m_ in range(M4):
                    for k in range(KD):
                        m = pe.matmul(ps[:, m_ * P:(m_ + 1) * P], w_q4[:, part, k, m_ * P:(m_ + 1) * P], xT[:, k, :],
                                      start=k == 0, stop=k == KD - 1)
                m = PE(m)
                wait(dve, m)
                for h in range(2):
                    r = slice(h * S, (h + 1) * S)
                    m = DVE(dve.tensor_scalar(q_bd[r, part, :, :, r],
                                              ps[r, :].rearrange("p (m b q) -> p m b q", m=M4, b=BT),
                                              turn4[r, part:part + 1], None, ALU.mult))
            w.q.append(m)
            for m_ in range(M4):
                for k in range(KD):
                    m = pe.matmul(KPS[:, m_ * P:(m_ + 1) * P], w_k4[:, k, m_ * P:(m_ + 1) * P], xT[:, k, :],
                                  start=k == 0, stop=k == KD - 1)
            m = PE(m)
            wait(act, m)
            m = AC(act.activation(kl[:, :, :, :], KPS[:, 0:M4 * P].rearrange("p (m b q) -> p m b q", m=M4, b=BT),
                                  ACT.Copy))
            w.q.append(m)
            w.kcs[0, 0] = m
            scores(0, w)
            for n in range(UNITS):
                m_, other = n % M4, (n // M4 + 1) % BT
                exponentials(n, w)
                if m_ == M4 - 1 and n >= 2:
                    average(n // 2 - 1, n % 2, w)
                keys(n + 1, 0, w)
                weights(n, w)
                keys(n + 1, 1, w)
                if m_ == 2:
                    transpose_context(other, 0, w)
                if m_ != M4 - 1 and n >= 2:
                    average(n // 2 - 1, n % 2, w)
                if m_ == M4 - 1:
                    values(n // 2 - 1, w)
                transposed(n, w)
                if m_ < 2:
                    normalize_rows(m_, i + n // M4, other, i * 32 + (n // M4) * 16 + 32, w)
                if m_ == 1:
                    shift_rows(other, w, w.A.get((STEPS - 1, 1)))
                if n + 1 < UNITS:
                    scores(n + 1, w)
                if m_ == 1 and n >= 2:
                    values(n // 2 - 1, w)
                if m_ == 2:
                    transpose_context(other, 1, w)
            DVE(dve.tensor_copy(xs[:, :], xn[:, bass.ds(i + 1, 1), :].rearrange("p a d -> p (a d)")))
            last = UNITS // 2 - 1
            average(last, 0, w)
            average(last, 1, w)
            values(last, w)
            wait(pe, w.at[last])
            for m_ in range(M4):
                m = pe.matmul(U[:, 0:D], attn[:, m_, :], w_o4[:, m_, :], start=m_ == 0, stop=m_ == M4 - 1)
            m = PE(m)
            wait(dve, m)
            DVE(dve.tensor_tensor(x[:, i, :], x[:, i, :], U[:, 0:D], ALU.add))
            shifted = [w.raw[1, 1], w.raw[0, 1]]
        with nc.Fori(0, T - 1, engines=(sp.engine,)) as j:
            for b in range(BT):
                sp.wait_ge(PL.sem, shifted[b].at(j))
                load_ctx4(b, j + 1)
        sp.wait_ge(PL.sem, shifted[0].at(T - 1))
        load_ctx4(0, 0)
    meet()
    load_expert(0)
    load_expert(1)

    meet()
    moments(x)
    with ExitStack() as tmp:
        def buffers(name, shape):
            return [sb(f"{name}_{u}", shape, tmp) for u in range(U2)]

        xs, xT, q5, k_bd = buffers("xs5", [P, D]), buffers("xT5", [P, KD, P]), buffers("q5", [P, M5, P]), \
            buffers("k_bd5", [P, M5, 2, P])
        v5, sm, smT, small = buffers("v5", [P, M5 * P]), buffers("sm5", [P, 8, P]), buffers("smT5", [P, 8, P]), \
            buffers("small5", [P, 2, 8])
        a5 = buffers("a5", [P, M5, P])
        for u in range(U2):
            DVE(dve.memset(k_bd[u][:, :, :, :], 0.0))
        wait_before(pe, d_w5)

        def body5(i, u):
            t = i * U2 + u
            A, C = banks[2 * u], banks[2 * u + 1]
            m_x = normed(xs[u][:, :], x, t)
            wait(pe, m_x)
            yield
            m_xT = transposed_tile(xs[u], xT[u], C)
            wait(pe, m_xT)
            yield
            for hf in range(2):
                for mm in range(4):
                    for k in range(KD):
                        pair = 4 * hf + mm
                        m = pe.matmul(A[:, pair * P:(pair + 1) * P], Wq5[:, k, pair * P:(pair + 1) * P], xT[u][:, k, :],
                                      start=k == 0, stop=k == KD - 1)
                m = PE(m)
                wait(act, m)
                m_q = AC(act.activation(q5[u][:, 4 * hf:4 * hf + 4, :],
                                        A[:, hf * BANK:(hf + 1) * BANK].rearrange("p (m q) -> p m q", m=4), ACT.Copy))
            yield
            for hf in range(2):
                for mm in range(4):
                    for k in range(KD):
                        pair = 4 * hf + mm
                        m = pe.matmul(C[:, pair * P:(pair + 1) * P], Wk5[:, k, pair * P:(pair + 1) * P], xT[u][:, k, :],
                                      start=k == 0, stop=k == KD - 1)
                m = PE(m)
                wait(dve, m)
                for h in range(2):
                    r = slice(h * S, (h + 1) * S)
                    m_k = DVE(dve.tensor_copy(k_bd[u][r, 4 * hf:4 * hf + 4, h, :],
                                              C[r, hf * BANK:(hf + 1) * BANK].rearrange("p (m q) -> p m q", m=4)))
            yield
            wait(pe, m_q)
            for hf in range(2):
                for k in range(KD):
                    m = pe.matmul(A[:, hf * BANK:(hf + 1) * BANK], xT[u][:, k, :],
                                  Wv5[:, k, hf * BANK:(hf + 1) * BANK], start=k == 0, stop=k == KD - 1)
                m = PE(m)
                wait(act, m)
                m_v = AC(act.activation(v5[u][:, hf * BANK:(hf + 1) * BANK], A[:, hf * BANK:(hf + 1) * BANK], ACT.Copy))
            yield
            m_av = []
            for grp in range(2):
                wait(pe, m_k, *m_av)
                for mm in range(4):
                    pair = 4 * grp + mm
                    m = pe.matmul(C[:, mm * 2 * P:(mm + 1) * 2 * P], q5[u][:, pair, :], k_bd[u][:, pair, :, :],
                                  start=True, stop=True)
                m = PE(m)
                soft = tile_softmax(m, C, sm[u], small[u], 1.0 / 8.0, 1)
                next(soft)
                yield
                next(soft)
                yield
                m = next(soft)
                wait(dve, m)
                m = DVE(dve.tensor_tensor(sm[u][:, :, :], sm[u][:, :, :],
                                          small[u][:, 1, :].unsqueeze(2).broadcast_to([P, 8, P]), ALU.mult))
                yield
                wait(pe, m_v)
                m_T = tile_transposes(m, A, sm[u], smT[u])
                wait(pe, *m_T)
                yield
                for h in range(8):
                    head = 8 * grp + h
                    m = pe.matmul(C[(h % 2) * S:(h % 2 + 1) * S, (h // 2) * P:(h // 2 + 1) * P],
                                  v5[u][:, head * S:(head + 1) * S], smT[u][:, h, :], start=True, stop=True)
                m = PE(m)
                wait(act, m)
                m_a = AC(act.activation(a5[u][:, 4 * grp:4 * grp + 4, :],
                                        C[:, 0:BANK].rearrange("p (m q) -> p m q", m=4), ACT.Gelu))
                m_av = [m_a]
                yield
            wait(pe, m_a, *m_T)
            for mm in range(M5):
                m = pe.matmul(A[:, 0:D], a5[u][:, mm, :], Wo5[:, mm, :], start=mm == 0, stop=mm == M5 - 1)
            m = PE(m)
            wait(dve, m)
            m = DVE(dve.tensor_tensor(xs[u][:, :], xs[u][:, :], A[:, 0:D], ALU.add))
            wait(dve, m)
            xt = x[:, bass.ds(t, 1), :].rearrange("p a d -> p (a d)")
            DVE(dve.tensor_tensor(xt, xt, xs[u][:, :], ALU.add))

        with tiles(T // U2, pe=32, dve=44, act=20) as i:
            for e in (pe, dve, act):
                wait_before(e, PE, DVE, AC)
            interleave(*(body5(i, u) for u in range(U2)))

    meet()
    load_expert(2)
    load_expert(3)
    moments(x)
    with ExitStack() as tmp:
        def tb(name, shape):
            return sb(name, shape, tmp)

        xs, xT = [tb(f"xs6_{u}", [P, D]) for u in range(U2)], [tb(f"xT6_{u}", [P, KD, P]) for u in range(U2)]
        logit, hot, work, rank_in = (tb(n, [P, T, E]) for n in ("logit6", "hot6", "work6", "rank6"))
        first6, top, p_tok, rank, slot, keep = (tb(n, [P, T]) for n in
                                                ("first6", "top6", "p_tok6", "rank_tok6", "slot6", "keep6"))
        iota6, earlier6 = tb("iota6", [P, E * CAP]), tb("earlier6", [P, P])
        d_w6(sp.dma_start(iota6[:, :], everywhere("iota6")))
        d_w6(sp.dma_start(earlier6[:, :], g["earlier6"]))
        select = tb("select6", [P, T, E * CAP])
        xe = tb("xe6", [P, KD, E * CAP])
        hT = [tb(f"hT6_{n}", [P, F // P, CAP]) for n in range(2)]
        ye = tb("ye6", [P, E, D])
        slot_row = tb("slot_row6", [P, T * P])
        wait_before(pe, d_w6)
        wait_before(dve, d_w6)

        def body6(i, u):
            t = i * U2 + u
            xt = xn[:, bass.ds(t, 1), :].rearrange("p a d -> p (a d)")
            normed(xt, x, t)
            m = normed(xs[u][:, :], x, t)
            wait(pe, m)
            m = transposed_tile(xs[u], xT[u], bank(2 * u))
            wait(pe, m)
            yield
            for k in range(KD):
                m = pe.matmul(bank(2 * u + 1)[:, 0:E], xT[u][:, k, :], w_r6[:, k, :], start=k == 0, stop=k == KD - 1)
            m = PE(m)
            wait(dve, m)
            DVE(dve.tensor_copy(logit[:, bass.ds(t, 1), :].rearrange("p a e -> p (a e)"), bank(2 * u + 1)[:, 0:E]))

        with tiles(T // U2, pe=4, dve=8) as i:
            for e in (pe, dve):
                wait_before(e, PE, DVE)
            interleave(*(body6(i, u) for u in range(U2)))
        wait_before(dve, DVE)

        def over_experts(v):
            return v[:, :].unsqueeze(2).broadcast_to([P, T, E])

        def over_tiles(v):
            return v.unsqueeze(1).broadcast_to([P, T, E])

        wait(dve, DVE(dve.tensor_reduce(top[:, :], logit[:, :, :], AX.X, ALU.max)))
        m = DVE(dve.tensor_tensor(logit[:, :, :], logit[:, :, :], over_experts(top), ALU.subtract))
        wait(act, m)
        m_e = AC(act.activation(work[:, :, :], logit[:, :, :], ACT.Exp))
        wait(dve, m_e)
        m = DVE(dve.tensor_reduce(p_tok[:, :], work[:, :, :], AX.X, ALU.add))
        wait(dve, m)
        DVE(dve.reciprocal(p_tok[:, :], p_tok[:, :]))
        m = DVE(dve.tensor_scalar(hot[:, :, :], logit[:, :, :], 0.0, None, ALU.is_ge))
        wait(dve, m)
        m = DVE(dve.tensor_tensor(work[:, :, :], hot[:, :, :], over_tiles(count6[:, 0:E]), ALU.mult))
        wait(dve, m)
        m = DVE(dve.tensor_reduce(first6[:, :], work[:, :, :], AX.X, ALU.max))
        wait(dve, m)
        m = DVE(dve.tensor_tensor(hot[:, :, :], work[:, :, :], over_experts(first6), ALU.is_equal))
        wait(pe, m)
        flat = hot[:, :, :].rearrange("p t e -> p (t e)")
        pe.matmul(bank(0)[:, 0:T * E], earlier6[:, :], flat, start=True, stop=True)
        m = PE(pe.matmul(bank(1)[:, 0:T * E], ones[:, :], flat, start=True, stop=True))
        wait(dve, m)
        DVE(dve.tensor_copy(rank_in[:, :, :], bank(0)[:, 0:T * E].rearrange("p (t e) -> p t e", t=T)))
        m = DVE(dve.tensor_copy(work[:, :, :], bank(1)[:, 0:T * E].rearrange("p (t e) -> p t e", t=T)))
        for t in range(1, T):
            wait(dve, m)
            m = DVE(dve.tensor_tensor(work[:, t, :], work[:, t, :], work[:, t - 1, :], ALU.add))
        wait(dve, m)
        m = DVE(dve.tensor_tensor(rank_in[:, 1:T, :], rank_in[:, 1:T, :], work[:, 0:T - 1, :], ALU.add))
        wait(dve, m)
        m = DVE(dve.tensor_tensor(rank_in[:, :, :], rank_in[:, :, :], hot[:, :, :], ALU.mult))
        wait(dve, m)
        m = DVE(dve.tensor_reduce(rank[:, :], rank_in[:, :, :], AX.X, ALU.add))
        wait(dve, m)
        DVE(dve.tensor_scalar(keep[:, :], rank[:, :], float(CAP), None, ALU.is_lt))
        m = DVE(dve.scalar_tensor_tensor(slot[:, :], first6[:, :], -float(CAP), rank[:, :], ALU.mult, ALU.add))
        wait(dve, m)
        m = DVE(dve.scalar_tensor_tensor(slot[:, :], slot[:, :], float(CAP * E + 1), keep[:, :], ALU.add, ALU.mult))
        wait(dve, m)
        m = DVE(dve.tensor_scalar(slot[:, :], slot[:, :], -1.0, None, ALU.add))
        wait(dve, m)
        for t in range(T):
            m = DVE(dve.tensor_scalar(select[:, t, :], iota6[:, :], slot[:, t:t + 1], None, ALU.is_equal))
        wait(pe, m)
        m_xe = []
        for k in range(KD):
            for half in range(2):
                n = 2 * k + half
                cols = slice(half * BANK, (half + 1) * BANK)
                for t in range(T):
                    m = pe.matmul(bank(4 + n), xn[:, t, k * P:(k + 1) * P], select[:, t, cols],
                                  start=t == 0, stop=t == T - 1)
                m = PE(m)
                e, line = ((dve, DVE), (act, AC))[half]
                wait(e, m)
                m_xe.append(line(dve.tensor_copy(xe[:, k, cols], bank(4 + n)) if e is dve else
                                 act.activation(xe[:, k, cols], bank(4 + n), ACT.Copy)))
        m_gather = m
        wait(dve, m_gather)
        for t in range(T):
            m = DVE(dve.tensor_scalar(select[:, 0, t * P:(t + 1) * P], ident[:, :], slot[:, t:t + 1], None, ALU.mult))
        wait(pe, m)
        for half in range(2):
            m = PE(pe.matmul(bank(2 + half), ones[:, :], select[:, 0, half * BANK:(half + 1) * BANK],
                             start=True, stop=True))
        wait(dve, m)
        m = DVE(dve.tensor_copy(slot_row[:, :], banks[1][:, :]))
        wait(dve, m)
        for e_ in range(E):
            m_back = DVE(dve.tensor_scalar(select[:, e_, :], slot_row[:, :], count6[:, E + e_:E + e_ + 1], None,
                                           ALU.is_equal))

        wait(pe, *m_xe)
        wait_before(pe, DVE, AC)

        RING = 4
        with tiles(E // RING, pe=12, dve=8, act=4) as i:
            m_h, m_H, m_Y, m_y = {}, {}, {}, {}
            for e in (pe, dve, act):
                wait_before(e, PE, DVE, AC)
            pe.wait_ge(d_e.sem, (i * RING + RING) * 32)

            def up(n):
                w1 = w1_ring[n]
                for hf in range(2):
                    wait(pe, m_h.get((n - 2, hf)))
                    ps = banks[n % 2][:, hf * BANK:(hf + 1) * BANK]
                    for ff in range(4):
                        f = 4 * hf + ff
                        for k in range(KD):
                            m = pe.matmul(ps[:, ff * CAP:(ff + 1) * CAP], w1[:, k, f * P:(f + 1) * P],
                                          xe[:, k, bass.ds((i * RING + n) * CAP, CAP)],
                                          start=k == 0, stop=k == KD - 1)
                    m_H[n] = m = PE(m)
                    e, line = ((dve, DVE), (act, AC))[hf]
                    wait(e, m, m_Y.get(n - 2))
                    dst, src = hT[n % 2][:, 4 * hf:4 * hf + 4, :], ps.rearrange("p (f c) -> p f c", f=4)
                    m_h[n, hf] = line(dve.tensor_scalar(dst, src, 0.0, None, ALU.max) if e is dve else
                                      act.activation(dst, src, ACT.Relu))

            def down(n):
                wait(pe, m_h[n, 0], m_h[n, 1], m_y.get(n - 2))
                ps = bank(4 + n % 2)[:, 0:D]
                for f in range(F // P):
                    m = pe.matmul(ps, hT[n % 2][:, f, :], w2_ring[n][:, f, :], start=f == 0, stop=f == F // P - 1)
                m_Y[n] = PE(m)
                wait(dve, m_Y[n])
                dst = ye[:, bass.ds(i * RING + n, 1), :].rearrange("p a d -> p (a d)")
                m_y[n] = DVE(dve.tensor_copy(dst, ps))

            up(0)
            for n in range(RING):
                if n + 1 < RING:
                    up(n + 1)
                down(n)
            ring_read = [m_Y[n] for n in range(RING)]
        for n in range(RING):
            sp.wait_ge(PE.sem, ring_read[n].at(0))
            load_expert(RING + n)

        wait_before(pe, DVE, AC)
        m_o = {}
        for t in range(T):
            wait(pe, m_o.get(t - 4))
            for e_ in range(E):
                m = pe.matmul(bank(2 * (t % 4))[:, 0:D], select[:, e_, t * P:(t + 1) * P], ye[:, e_, :],
                              start=e_ == 0, stop=e_ == E - 1)
            m = PE(m)
            wait(dve, m)
            m_o[t] = DVE(dve.scalar_tensor_tensor(x[:, t, :], bank(2 * (t % 4))[:, 0:D], p_tok[:, t:t + 1], x[:, t, :],
                                                  ALU.mult, ALU.add))
            wait(sp, m_o[t])
            d_out(sp.dma_start(out[t * P:(t + 1) * P, :], x[:, t, :]))
        sp.wait_ge(d_out.sem, T * 16)



def constants():
    f = np.float32
    token = np.arange(P)
    same = token[:, None] // S == token[None, :] // S
    masks = np.stack([np.where(same & (token[None, :] <= token[:, None]), 0.0, MASKED),
                      np.where(same, 0.0, MASKED)]).astype(f)

    def angles(positions, width):
        inv = f(1.0) / np.power(f(10000.0), np.arange(0, width, 2, dtype=f) / f(width), dtype=f)
        a = np.arange(positions, dtype=f)[:, None] * inv[None, :]
        return np.concatenate([a, a], axis=1).T

    a2 = angles(S, P)
    sign = np.where(token < P // 2, -1.0, 1.0).astype(f)[:, None]
    rope2 = np.stack([np.tile(np.cos(a2), (1, BT)), np.tile(np.sin(a2) * sign, (1, BT))]).astype(f)
    head2 = (token[:, None] // 16 == np.arange(8)[None, :]).astype(f)
    a4 = np.tile(angles(CTX, 64), (2, 1))
    rope4 = np.stack([np.cos(a4), np.sin(a4)]).astype(f)
    turn4 = np.stack([np.ones(P), np.where(token % 64 < 32, 1.0, -1.0)], axis=1).astype(f)
    return {"masks": masks, "rope2": rope2, "head2": head2, "rope4": rope4, "turn4": turn4,
            "count6": np.concatenate([np.tile(8 - np.arange(8), (P, 1)),
                                      token[:, None] + P * np.arange(8)[None, :]], axis=1).astype(f),
            "iota6": np.arange(8 * P).astype(f), "earlier6": (token[:, None] < token[None, :]).astype(f)}


def kernel(**inputs):
    import numpy as _np
    import concourse.bacc as _bacc
    from concourse import mybir as _mybir
    from concourse.bass_utils import run_bass_kernel_spmd as _run

    a = {k: _np.asarray(v) for k, v in inputs.items()}

    def pairs(v):
        return v.reshape(-1, P).T

    lay = {
        "x": a["x"].reshape(B * S, D),
        "ctx_1024": a["ctx_1024"].reshape(B * CTX, D).reshape(B, CTX, D),
        "ctx_T": a["ctx_1024"].transpose(0, 2, 1),
        "L0_xattn_Wq": a["L0_xattn_Wq"].reshape(D, -1),
        "L0_xattn_WkT": a["L0_xattn_Wk"].reshape(D, -1).T,
        "L0_xattn_Wv": a["L0_xattn_Wv"].reshape(D, -1),
        "L0_xattn_Wo": a["L0_xattn_Wo"].reshape(-1, D),
        "L0_xattn_bq": pairs(a["L0_xattn_bq"].reshape(-1)),
        "L0_xattn_bk": pairs(a["L0_xattn_bk"].reshape(-1)),
        "L0_xattn_bv": pairs(a["L0_xattn_bv"].reshape(-1)),
        "L0_xattn_bo": a["L0_xattn_bo"],
    }
    for name in ("wq", "bq", "wqc", "bqc", "wqr", "bqr", "wkv", "bkv", "wkr", "bkr", "wkc", "bkc", "wv", "bv",
                 "wo", "bo"):
        lay["L0_attn_" + name] = a["L0_attn_" + name]
    for name in ("theta", "phi", "theta_noise", "phi_noise"):
        lay["L0_ffn_" + name] = a["L0_ffn_" + name]
    for name in ("gamma_x", "beta_x", "gamma_l", "beta_l", "Wq", "Wkv", "Wo"):
        lay["L1_xattn_" + name] = a["L1_xattn_" + name]
    lay["L1_xattn_Wq_turned"] = a["L1_xattn_Wq"].reshape(D, -1, 2, 32)[:, :, ::-1].reshape(D, -1)
    for name in ("L1_attn_Wq", "L1_attn_Wk", "L1_attn_Wv", "L1_attn_Wpost", "L1_ffn_Wr", "L1_ffn_W1", "L1_ffn_W2"):
        lay[name] = a[name]
    lay |= constants()
    nc = _bacc.Bacc("TRN2", target_bir_lowering=False, num_devices=1)
    arrays, g = {}, {}
    for name, v in lay.items():
        v = _np.ascontiguousarray(v)
        arrays[f"in_{name}"] = v
        g[name] = nc.dram_tensor(f"in_{name}", v.shape, _mybir.dt.from_np(v.dtype), kind="ExternalInput").ap()
    out = nc.dram_tensor("out", (B * S, D), F32, kind="ExternalOutput").ap()
    program(nc, g, out)
    r = _run(nc, [arrays], core_ids=[0])
    return r.results[0]["out"].reshape(B, S, D)
```

```python
from contextlib import ExitStack, contextmanager

import numpy as np

import concourse.bass as bass
from concourse import mybir

F32 = mybir.dt.float32
BF16 = mybir.dt.bfloat16
F32R = mybir.dt.float32r
ACT = mybir.ActivationFunctionType
ALU = mybir.AluOpType
AX = mybir.AxisListType

P = 128
B, S, D = 16, 64, 256
T = B * S // P
BT = P // S
KD = D // P
CTX = 1024
KC = CTX // P
BANK = 512
HALF = CTX // BANK
EPS = 1e-5
MASKED = -1.0e30


class Mark:

    def __init__(self, line):
        self.line, self.n, self.base, self.per, self.epoch = line, line.n, line.total, line.per, line.epoch

    def at(self, iteration):
        return (iteration * self.per + (self.base + self.n)) * self.line.step


class Line:

    def __init__(self, nc, ctx, name, step=1):
        self.name, self.sem = name, ctx.enter_context(nc.semaphore(name))
        self.step, self.total, self.epoch, self.i, self.per, self.n = step, 0, 0, None, 0, 0

    def __call__(self, instruction):
        instruction.then_inc(self.sem, self.step)
        self.n += 1
        return Mark(self)

    def start(self, per, i):
        self.total, self.n, self.per, self.i, self.epoch = self.total + self.n, 0, per, i, self.epoch + 1

    def stop(self, times):
        assert self.n == self.per, f"{self.name}: {self.n} counts in the loop, {self.per} declared"
        self.total, self.n, self.per, self.i = self.total + self.per * times, 0, 0, None
        self.epoch += 1

    def before(self):
        if self.i is None:
            return (self.total + self.n) * self.step
        return self.i * (self.per * self.step) + self.total * self.step


def wait(engine, *marks):
    marks = [m for m in marks if m is not None]
    for m in marks:
        line = m.line
        if any(o.line is line and (o.epoch, o.n) > (m.epoch, m.n) for o in marks) or \
                any(o.line is line and o.epoch == m.epoch and o.n == m.n for o in marks[:marks.index(m)]):
            continue
        if m.epoch == line.epoch and line.i is not None:
            engine.wait_ge(line.sem, line.i * (line.per * line.step) + (line.total + m.n) * line.step)
        elif m.epoch == line.epoch:
            engine.wait_ge(line.sem, (line.total + m.n) * line.step)
        else:
            engine.wait_ge(line.sem, line.total * line.step)


def wait_before(engine, *lines):
    for line in lines:
        engine.wait_ge(line.sem, line.before())



def program(nc, g, out):
    with ExitStack() as ctx:
        build(nc, ctx, g, out)


def build(nc, ctx, g, out):
    pe, dve, act, pool, sp = nc.tensor, nc.vector, nc.scalar, nc.gpsimd, nc.sync

    def sb(name, shape, stack=ctx, dt=F32):
        return stack.enter_context(nc.sbuf_tensor(name, shape, dt))

    PE, DVE, AC, PL = (Line(nc, ctx, n) for n in ("s_pe", "s_dve", "s_act", "s_pool"))
    engine_of = {PE: pe.engine, DVE: dve.engine, AC: act.engine, PL: pool.engine}

    @contextmanager
    def tiles(times, **per):
        lines = {"pe": PE, "dve": DVE, "act": AC, "pool": PL}
        with nc.Fori(0, times, engines=tuple(engine_of[lines[k]] for k in per)) as i:
            for k, n in per.items():
                lines[k].start(n, i)
            yield i
        for k in per:
            lines[k].stop(times)

    def meet(*engines):
        for e in engines or (pe, dve, act, pool, sp):
            wait_before(e, *(l for l in (PE, DVE, AC, PL) if l.total + l.n))

    x = sb("x", [P, T + 1, D])
    xn = sb("xn", [P, T + 1, D])
    ident = sb("ident", [P, P])
    ones = sb("ones", [P, P])
    big = sb("big", [P, 8192])
    ctx_buf = [sb("ctx_buf0", [P, KC, D])]
    ctxT_buf = [sb("ctxT_buf0", [P, KD, CTX])]
    st6 = sb("st6", [P, T, 6])
    mv = sb("mv", [P, T + 1, 2])
    rstd = sb("rstd", [P, T + 1])
    sd = sb("sd", [P, T + 1])
    banks = [ctx.enter_context(nc.psum_tensor(f"bank{n}", [P, 2 * BANK], F32)) for n in range(4)]

    def bank(n):
        return banks[n // 2][:, (n % 2) * BANK:(n % 2 + 1) * BANK]

    def stream(name):
        return Line(nc, ctx, name, 16)

    d_x, d_mask, d_w1, d_w2, d_w3, d_w4, d_w5, d_w6, d_out = (
        stream(n) for n in ("d_x", "d_mask", "d_w1", "d_w2", "d_w3", "d_w4", "d_w5", "d_w6", "d_out"))
    d_ctx = stream("d_ctx")
    d_raw = stream("d_raw")
    H1, M1 = 16, 8
    Wq1, WkT1, Wv1, Wo1 = (big[:, n * 2048:(n + 1) * 2048] for n in range(4))
    Wq1 = Wq1.rearrange("p (k n) -> p k n", k=KD)
    WkT1 = WkT1.rearrange("p (m d) -> p m d", m=M1)
    Wv1 = Wv1.rearrange("p (k n) -> p k n", k=KD)
    Wo1 = Wo1.rearrange("p (m d) -> p m d", m=M1)
    bq1, bk1, bv1 = (sb(n, [P, M1]) for n in ("bq1", "bk1", "bv1"))
    bo1 = sb("bo1", [P, D])

    def rows(name):
        return g[name].rearrange("(k p) n -> p k n", p=P)

    def everywhere(name):
        return g[name].partition_broadcast(P)

    d_x(sp.dma_start(x[:, 0:T, :], g["x"].rearrange("(t p) d -> p t d", p=P)))
    d_w1(sp.dma_start(Wq1, rows("L0_xattn_Wq")))
    d_w1(sp.dma_start(WkT1, rows("L0_xattn_WkT")))
    for dst, name in ((bq1, "L0_xattn_bq"), (bk1, "L0_xattn_bk"), (bv1, "L0_xattn_bv")):
        d_w1(act.dma_start(dst[:, :], g[name]))
    d_w1(act.dma_start(bo1[:, :], everywhere("L0_xattn_bo")))
    ctx_rows = g["ctx_1024"].rearrange("(t b) (k p) d -> t b p k d", b=BT, p=P)
    ctxT_rows = g["ctx_T"].rearrange("(t b) (k p) c -> t b p k c", b=BT, p=P)

    def load_ctx(b, t):
        src = [rows_[bass.ds(t, 1), b].rearrange("a p k n -> (a p) k n") for rows_ in (ctxT_rows, ctx_rows)]
        d_ctx(sp.dma_start(ctxT_buf[0][:, :, :], src[0]))
        d_ctx(sp.dma_start(ctx_buf[0][:, :, :], src[1]))

    load_ctx(0, 0)
    d_w1(sp.dma_start(Wv1, rows("L0_xattn_Wv")))
    d_w1(sp.dma_start(Wo1, rows("L0_xattn_Wo")))

    PL(pool.memset(ones[:, :], 1.0))
    m = PL(pool.memset(ident[:, :], 0.0))
    wait(pool, m)
    m_ident = PL(pool.affine_select(out=ident[:, :], in_=ident[:, :], compare_op=ALU.not_equal, fill=1.0, base=0,
                                    pattern=[[-1, P]], channel_multiplier=1))
    wait(pe, m_ident)
    PE(pe.matmul(bank(7)[:, 0:P], ones[:, :], ident[:, :], start=True, stop=True))

    def moments(src):
        with tiles(T, dve=1) as i:
            DVE(dve.bn_stats(st6[:, i, :], src[:, i, :]))
        wait_before(dve, DVE)
        for t in range(T):
            m = DVE(dve.bn_aggr(mv[:, t, :], st6[:, t, :]))
        wait(dve, m)
        m = DVE(dve.tensor_scalar(sd[:, :], mv[:, :, 1], EPS, None, ALU.add))
        wait(act, m)
        m = AC(act.activation(sd[:, :], sd[:, :], ACT.Sqrt))
        wait(dve, m)
        wait(dve, DVE(dve.reciprocal(rstd[:, :], sd[:, :])))

    def normed(dst, src, i):
        return DVE(dve.tensor_scalar(dst, src[:, bass.ds(i, 1), :].rearrange("p a d -> p (a d)"),
                                     mv[:, bass.ds(i, 1), 0], rstd[:, bass.ds(i, 1)], ALU.subtract, ALU.mult))

    mask_in = xn[:, T, :].rearrange("p (m k) -> p m k", m=2)
    mask = sb("mask", [P, 2, P], dt=BF16)
    ident16 = sb("ident16", [P, P], dt=BF16)
    d_mask(act.dma_start(mask_in[:, :, :], g["masks"].rearrange("m p k -> p m k")))

    def transposed_tile(src, dst, into):
        for k in range(KD):
            m = pe.transpose(into[:, k * P:(k + 1) * P], src[:, k * P:(k + 1) * P], ident[:, :])
        m = PE(m)
        wait(dve, m)
        return DVE(dve.tensor_copy(dst[:, :, :], into[:, 0:D].rearrange("p (k n) -> p k n", k=KD)))

    def mask_scores(ps, which):
        pe.matmul(ps, ident16[:, :], mask[:, which:which + 1, :].broadcast_to([P, 4, P]), start=True, stop=False)

    def tile_exponentials(m_scores, ps, sm, top, scale):
        wait(dve, m_scores)
        m = DVE(dve.tensor_reduce(top, ps[:, :].rearrange("p (h k) -> p h k", h=8), AX.X, ALU.max))
        wait(dve, m)
        m = DVE(dve.tensor_tensor(sm[:, :, :], ps[:, :].rearrange("p (h k) -> p h k", h=8),
                                  top.unsqueeze(2).broadcast_to([P, 8, P]), ALU.subtract))
        wait(act, m)
        return AC(act.activation(sm[:, :, :], sm[:, :, :], ACT.Exp, scale=scale))

    def tile_transposes(m_prob, ps, sm, smT):
        wait(pe, m_prob)
        marks = []
        for hf, (line, e) in enumerate(((DVE, dve), (AC, act))):
            for h in range(4 * hf, 4 * hf + 4):
                m = pe.transpose(ps[:, h * P:(h + 1) * P], sm[:, h, :], ident[:, :])
            m = PE(m)
            wait(e, m)
            dst = smT[:, 4 * hf:4 * hf + 4, :]
            src = ps[:, 4 * hf * P:4 * (hf + 1) * P].rearrange("p (h q) -> p h q", h=4)
            marks.append(line(e.tensor_copy(dst, src) if e is dve else e.activation(dst, src, ACT.Copy)))
        return marks

    def interleave(*bodies):
        left = list(bodies)
        while left:
            left = [b for b in left if next(b, "end") != "end"]

    U2 = 2

    HD2, DC = 16, 64
    w_qkv2 = sb("w_qkv2", [P, KD, P])
    b_qkv2 = sb("b_qkv2", [P, 1])
    w_c2 = sb("w_c2", [P, 2, P])
    w_r2 = sb("w_r2", [P, 4, KD, P])
    b_c2 = sb("b_c2", [P, 2])
    b_r2 = sb("b_r2", [P, 4])
    w_v2 = sb("w_v2", [P, D])
    b_v2 = sb("b_v2", [P, D])
    w_o2 = sb("w_o2", [P, KD, D])
    b_o2 = sb("b_o2", [P, D])
    rope2 = sb("rope2", [P, 2, P])
    H2 = 16
    head2 = sb("head2", [P, 8])
    HF = P // 2
    m = PL(pool.memset(w_c2[:, :, :], 0.0))
    m = PL(pool.memset(w_v2[:, :], 0.0))
    wait(act, m)
    d_w2(act.dma_start(w_qkv2[:, :, 0:DC], rows("L0_attn_wq")))
    d_w2(act.dma_start(w_qkv2[:, :, DC:2 * DC], rows("L0_attn_wkv")))
    d_w2(act.dma_start(b_qkv2[0:DC, :], g["L0_attn_bq"].unsqueeze(1)))
    d_w2(act.dma_start(b_qkv2[DC:2 * DC, :], g["L0_attn_bkv"].unsqueeze(1)))
    d_w2(act.dma_start(w_c2[0:DC, 0, :], g["L0_attn_wqc"]))
    d_w2(act.dma_start(w_c2[DC:2 * DC, 1, :], g["L0_attn_wkc"]))
    d_w2(act.dma_start(w_v2[DC:2 * DC, :], g["L0_attn_wv"]))
    d_w2(act.dma_start(w_o2[:, :, :], rows("L0_attn_wo")))
    for n, (w, v) in enumerate((("L0_attn_wqr", "L0_attn_bqr"), ("L0_attn_wkr", "L0_attn_bkr"))):
        d_w2(act.dma_start(b_c2[:, n:n + 1], g[("L0_attn_bqc", "L0_attn_bkc")[n]].unsqueeze(1)))
        d_w2(act.dma_start(w_r2[:, 2 * n, :, :], rows(w)))
        d_w2(act.dma_start(b_r2[:, 2 * n:2 * n + 1], g[v].unsqueeze(1)))
        for h in range(2):
            to, fro = slice(h * HF, (h + 1) * HF), slice((1 - h) * HF, (2 - h) * HF)
            d_w2(act.dma_start(w_r2[:, 2 * n + 1, :, to], rows(w)[:, :, fro]))
            d_w2(act.dma_start(b_r2[to, 2 * n + 1:2 * n + 2], g[v][fro].unsqueeze(1)))
    d_w2(act.dma_start(b_v2[:, :], everywhere("L0_attn_bv")))
    d_w2(act.dma_start(b_o2[:, :], everywhere("L0_attn_bo")))
    d_w2(act.dma_start(rope2[:, :, :], g["rope2"].rearrange("c p t -> p c t")))
    d_w2(act.dma_start(head2[:, :], g["head2"]))

    trig3 = sb("trig3", [P, 2, KD, D])
    noise3, turns3 = (xn[:, h * 4:h * 4 + 4, :].rearrange("p (n k) d -> p n k d", n=2) for h in range(2))
    for n, name in enumerate(("theta", "phi")):
        d_w3(act.dma_start(trig3[:, n, :, :], rows("L0_ffn_" + name)))
        d_w3(act.dma_start(noise3[:, n, :, :], rows(f"L0_ffn_{name}_noise")))

    stats_c = sb("stats_c", [P, (B + 1) * KC, 6])
    mean_c = sb("mean_c", [P, (B + BT) * KC])
    rstd_c = sb("rstd_c", [P, (B + BT) * KC])

    DVE(dve.memset(x[:, T, :], 0.0))
    DVE(dve.memset(mv[:, T, :], 0.0))
    wait_before(dve, d_x)
    moments(x)

    with ExitStack() as tmp:
        def tb(name, shape):
            return sb(name, shape, tmp)

        G = M1 // 2
        xs, y = tb("xs1", [P, D]), tb("y1", [P, D])
        xT = tb("xT1", [P, KD, P])
        q_bd = tb("q_bd1", [P, M1, BT, P])
        def halves(name, shape):
            return [sb(f"{name}_{part}", shape, tmp, F32R) for part in ("high", "low")]

        ctxT_hl = [halves(f"ctxT1_{b}", [P, KD, CTX]) for b in range(BT)]
        ctx_hl = [halves(f"ctx1_{b}", [P, KC, D]) for b in range(BT)]
        qp = [halves(f"qp1_{n}", [P, KD, 2 * P]) for n in range(2)]
        qbk = [tb(f"qbk1_{n}", [P, 2]) for n in range(2)]
        prob = [tb(f"prob1_{n}", [P, CTX]) for n in range(2)]
        probT = halves("probT1", [P, KC, 2 * P])
        PASSES = ((0, 0), (0, 1), (1, 0))
        u_sb = tb("u1", [P, KD, 2 * P])
        attn = tb("attn1", [P, M1, P])
        mx, nb, rs, ri = ([tb(f"{a}1_{n}", [P, 1]) for n in range(2)] for a in ("mx", "nb", "rs", "ri"))
        SCALE1 = 1.0 / 8.0
        DVE(dve.memset(q_bd[:, :, :, :], 0.0))
        QP, U, TP = bank(6), bank(7), (bank(4), bank(5))
        wait_before(pe, d_w1)
        wait_before(dve, d_w1)

        def split_context(b, which, count, m_read, m_stats=None):
            src, (high, low) = ((ctxT_buf[0], ctxT_hl[b]), (ctx_buf[0], ctx_hl[b]))[which]
            pool.wait_ge(d_ctx.sem, count)
            wait(pool, m_read)
            n = src.shape[1]
            for c in (slice(0, n // 2), slice(n // 2, n)):
                part = src[:, c, :]
                one = ones[:, 0:1].unsqueeze(2).broadcast_to(list(part.shape))
                m = PL(pool.tensor_tensor(high[:, c, :], part, one, ALU.mult))
                wait(pool, m, m_stats)
                m = PL(pool.tensor_tensor(low[:, c, :], part, high[:, c, :], ALU.subtract))
            return m

        def context_stats(batch, chunks, count):
            dve.wait_ge(d_ctx.sem, count)
            for c in chunks:
                dst = stats_c[:, bass.ds(batch * KC + c, 1), :].rearrange("p a s -> p (a s)")
                m = DVE(dve.bn_stats(dst, ctx_buf[0][:, c, :]))
            return m

        m = context_stats(0, range(KC), 32)
        split_context(0, 0, 32, None)
        m = split_context(0, 1, 32, None, m)
        wait(sp, m)
        load_ctx(1, 0)

        m_split = {}
        steps = [(b, s) for b in range(BT) for s in range(G)]
        m_qp, m_qbk, m_S, m_exp, m_T, m_PT, m_PV, m_u, m_OB, m_at, m_P, m_nb, m_q = ({} for _ in range(13))
        last = len(steps) - 1

        def project(n):
            b, s = steps[n % len(steps)]
            wait(pe, m_q.get("q"), m_qbk.get(n - 1))
            for pr in range(2):
                for k in range(KD):
                    m = pe.matmul(QP[:, (k * 2 + pr) * P:(k * 2 + pr + 1) * P],
                                  WkT1[:, 2 * s + pr, k * P:(k + 1) * P], q_bd[:, 2 * s + pr, b, :],
                                  start=True, stop=True)
            m = PE(m)
            high, low = qp[n % 2]
            wait(act, m, m_S.get((n - 2, 1)))
            m = AC(act.activation(high[:, :, :], QP.rearrange("p (k n) -> p k n", k=KD), ACT.Copy))
            wait(dve, m)
            m_qp[n] = DVE(dve.tensor_tensor(low[:, :, :], QP.rearrange("p (k n) -> p k n", k=KD), high[:, :, :],
                                            ALU.subtract))

        def scores(n, pr):
            b, s = steps[n]
            wait(pe, m_qp.get(n), m_exp.get((n - 1, pr)), *(m_q.values() if n == 0 else ()))
            if n == G and pr == 0:
                wait(pe, m_split[1])
            for half in range(HALF):
                cols = slice(half * BANK, (half + 1) * BANK)
                for k in range(KD):
                    for a, c in PASSES:
                        m = pe.matmul(banks[pr][:, cols], qp[n % 2][a][:, k, pr * P:(pr + 1) * P],
                                      ctxT_hl[b][c][:, k, cols], start=k == 0 and a + c == 0,
                                      stop=k == KD - 1 and a == 1)
            m_S[n, pr] = PE(m)

        def query_dot_bias(n):
            b, s = steps[n % len(steps)]
            wait(pe, m_qp[n])
            for pr in range(2):
                m = pe.matmul(QP[:, pr:pr + 1], q_bd[:, 2 * s + pr, b, :], bk1[:, 2 * s + pr:2 * s + pr + 1],
                              start=True, stop=True)
            m = PE(m)
            wait(dve, m)
            m_qbk[n] = DVE(dve.tensor_copy(qbk[n % 2][:, :], QP[:, 0:2]))

        def peak(n, pr):
            wait(dve, m_S[n, pr])
            m = DVE(dve.tensor_reduce(mx[pr][:, :], banks[pr][:, :], AX.X, ALU.max))
            wait(dve, m, m_qbk.get(n))
            m = DVE(dve.tensor_scalar(nb[pr][:, :], mx[pr][:, :], qbk[n % 2][:, pr:pr + 1], -SCALE1,
                                      ALU.add, ALU.mult))
            wait(dve, m)
            m_nb[n, pr] = DVE(dve.scalar_tensor_tensor(nb[pr][:, :], qbk[n % 2][:, pr:pr + 1], SCALE1,
                                                       nb[pr][:, :], ALU.mult, ALU.add))

        def exponentials(n, pr):
            wait(act, m_nb[n, pr], m_T.get((n - 1, pr)))
            m_exp[n, pr] = AC(act.activation(prob[pr][:, :], banks[pr][:, :], ACT.Exp, bias=nb[pr][:, 0:1],
                                             scale=SCALE1, accum_out=rs[pr][:, 0:1]))

        def weights(n, pr):
            wait(dve, m_exp[n, pr])
            m = DVE(dve.reciprocal(ri[pr][:, :], rs[pr][:, :]))
            wait(dve, m)
            m_P[n, pr] = DVE(dve.tensor_scalar(prob[pr][:, :], prob[pr][:, :], ri[pr][:, 0:1], None, ALU.mult))

        def transposed(n, pr):
            before = (n, 0) if pr else (n - 1, 1)
            wait(pe, m_P[n, pr], m_PT.get((*before, 0)), m_PT.get((*before, 1)))
            for c in range(KC):
                t = pe.transpose(TP[c // 4][:, (c % 4) * P:(c % 4 + 1) * P], prob[pr][:, c * P:(c + 1) * P],
                                 ident[:, :])
                if c == 3:
                    first = PE(t)
            m_T[n, pr] = PE(t)
            for hf, m in enumerate((first, m_T[n, pr])):
                wait(act, m, m_PV.get(n - 1))
                at = (slice(0, P), slice(hf * 4, (hf + 1) * 4), slice(pr * P, (pr + 1) * P))
                src = TP[hf].rearrange("p (c q) -> p c q", c=4)
                m = AC(act.activation(probT[0][at], src, ACT.Copy))
                wait(dve, m, m_PV.get(n - 1))
                m_PT[n, pr, hf] = DVE(dve.tensor_tensor(probT[1][at], src, probT[0][at], ALU.subtract))

        def average(n):
            b, s = steps[n]
            wait(pe, m_PT[n, 1, 0], m_PT[n, 1, 1], m_at.get(n - 1))
            for k in range(KD):
                for c in range(KC):
                    for a, p in PASSES:
                        m = pe.matmul(U[:, k * 2 * P:(k + 1) * 2 * P], ctx_hl[b][a][:, c, k * P:(k + 1) * P],
                                      probT[p][:, c, :], start=c == 0 and a + p == 0, stop=c == KC - 1 and a == 1)
            m_PV[n] = PE(m)
            wait(dve, m_PV[n], m_OB.get(n - 1))
            m_u[n] = DVE(dve.tensor_copy(u_sb[:, :, :], U.rearrange("p (k n) -> p k n", k=KD)))

        def values(n):
            b, s = steps[n]
            wait(pe, m_u[n])
            for pr in range(2):
                for k in range(KD):
                    pair = 2 * s + pr
                    m = pe.matmul(U[:, pr * P:(pr + 1) * P], Wv1[:, k, pair * P:(pair + 1) * P],
                                  u_sb[:, k, pr * P:(pr + 1) * P], start=k == 0, stop=k == KD - 1)
            m_OB[n] = PE(m)
            wait(dve, m_OB[n])
            for h in range(2):
                r = slice(h * S, (h + 1) * S)
                bias = bv1[r, 2 * s:2 * s + 2].unsqueeze(2).broadcast_to([S, 2, S])
                m_at[n] = DVE(dve.tensor_tensor(attn[r, 2 * s:2 * s + 2, b * S:(b + 1) * S],
                                                U[r, 0:2 * P].rearrange("p (r n) -> p r n", r=2)[:, :, r],
                                                bias, ALU.add))

        def normed_transposed(t):
            m = normed(xs[:, :], x, t)
            wait(pe, m, m_qbk.get(last))
            for k in range(KD):
                m = pe.transpose(QP[:, k * P:(k + 1) * P], xs[:, k * P:(k + 1) * P], ident[:, :])
            m = PE(m)
            wait(dve, m)
            m_q["xT"] = DVE(dve.tensor_copy(xT[:, :, :], QP[:, 0:D].rearrange("p (k n) -> p k n", k=KD)))

        def queries():
            wait(pe, m_q["xT"], m_exp.get((last, 0)))
            for half in range(2):
                for mm in range(4):
                    for k in range(KD):
                        pair = half * 4 + mm
                        m = pe.matmul(bank(half)[:, mm * P:(mm + 1) * P], Wq1[:, k, pair * P:(pair + 1) * P],
                                      xT[:, k, :], start=k == 0, stop=k == KD - 1)
                m = PE(m)
                wait(dve, m)
                for h in range(2):
                    r = slice(h * S, (h + 1) * S)
                    ps = bank(half)[r, :].rearrange("p (m b q) -> p m b q", m=4, b=BT)
                    bias = bq1[r, half * 4:(half + 1) * 4].unsqueeze(2).unsqueeze(3).broadcast_to([S, 4, BT, S])
                    m_q["q"] = DVE(dve.tensor_tensor(q_bd[r, half * 4:(half + 1) * 4, :, r], ps, bias, ALU.add))

        wait_before(pe, DVE)
        normed_transposed(0)
        queries()
        project(0)
        query_dot_bias(0)
        with tiles(T, pe=84, dve=176, act=56, pool=16) as i:
            for e in (pe, dve, act, pool):
                wait_before(e, PE, DVE, AC, PL)
            for marks in (m_split, m_qp, m_qbk, m_S, m_exp, m_T, m_PT, m_PV, m_u, m_OB, m_at, m_P, m_nb, m_q):
                marks.clear()
            scores(0, 0)
            peak(0, 0)
            exponentials(0, 0)
            for n in range(last + 1):
                scores(n, 1)
                weights(n, 0)
                if n < last:
                    project(n + 1)
                else:
                    normed_transposed(i + 1)
                peak(n, 1)
                exponentials(n, 1)
                b, s = steps[n]
                ahead = i * 2 * BT * 16 + (b + 2) * 32
                if s == 1:
                    m_stats = context_stats(i * BT + (b + 1), range(KC // 2), ahead)
                    split_context(1 - b, 0, ahead, m_PV.get(G - 1) if b else None)
                weights(n, 1)
                if n > 0:
                    average(n - 1)
                if n == last:
                    queries()
                transposed(n, 0)
                if s == 2:
                    m_stats = context_stats(i * BT + (b + 1), range(KC // 2, KC), ahead)
                    m_split[1 - b] = split_context(1 - b, 1, ahead, None, m_stats)
                if n > 0:
                    values(n - 1)
                if n < last:
                    query_dot_bias(n + 1)
                    scores(n + 1, 0)
                    peak(n + 1, 0)
                transposed(n, 1)
                if n < last:
                    exponentials(n + 1, 0)
            project(last + 1)
            query_dot_bias(last + 1)
            average(last)
            values(last)
            wait(pe, m_at[last])
            for mm in range(M1):
                m = pe.matmul(U[:, 0:D], attn[:, mm, :], Wo1[:, mm, :], start=mm == 0, stop=mm == M1 - 1)
            m = PE(m)
            wait(dve, m)
            m = DVE(dve.tensor_tensor(y[:, :], U[:, 0:D], bo1[:, :], ALU.add))
            wait(dve, m)
            DVE(dve.tensor_tensor(x[:, i, :], x[:, i, :], y[:, :], ALU.add))
        with nc.Fori(0, T - 1, engines=(sp.engine,)) as j:
            for b in range(BT):
                sp.wait_ge(PL.sem, m_split[1 - b].at(j))
                load_ctx(b, j + 1)
        sp.wait_ge(PL.sem, m_split[1].at(T - 1))
        load_ctx(0, 0)

    meet()
    ctx_buf.append(sb("ctx_buf1", [P, KC, D]))
    ctxT_buf.append(sb("ctxT_buf1", [P, KD, CTX]))

    H4, M4 = 8, 4
    w_q4 = sb("w_q4", [P, 2, KD, M4 * P])
    w_k4 = sb("w_k4", [P, KD, M4 * P])
    w_v4 = sb("w_v4", [P, KD, M4 * P])
    w_o4 = sb("w_o4", [P, M4, D])
    gb4 = sb("gb4", [P, 4, D])
    rope4 = sb("rope4", [P, 2, CTX])
    turn4 = sb("turn4", [P, 2])
    INNER = M4 * P
    d_w4(sp.dma_start(w_q4[:, 0, :, :], rows("L1_xattn_Wq")))
    d_w4(sp.dma_start(w_q4[:, 1, :, :], rows("L1_xattn_Wq_turned")))
    d_w4(sp.dma_start(w_k4[:, :, :], rows("L1_xattn_Wkv")[:, :, 0:INNER]))
    d_w4(sp.dma_start(w_v4[:, :, :], rows("L1_xattn_Wkv")[:, :, INNER:2 * INNER]))
    d_w4(sp.dma_start(w_o4[:, :, :], rows("L1_xattn_Wo")))
    for n, name in enumerate(("gamma_x", "beta_x", "gamma_l", "beta_l")):
        d_w4(sp.dma_start(gb4[:, n, :], everywhere("L1_xattn_" + name)))
    d_w4(sp.dma_start(rope4[:, :, :], g["rope4"].rearrange("c p t -> p c t")))
    d_w4(sp.dma_start(turn4[:, :], g["turn4"]))

    M5 = 8
    E, F, CAP = 8, 1024, 128
    Wq5, Wk5, Wv5, Wo5 = (big[:, n * 2048:(n + 1) * 2048] for n in range(4))
    Wq5, Wk5, Wv5 = (w.rearrange("p (k n) -> p k n", k=KD) for w in (Wq5, Wk5, Wv5))
    Wo5 = Wo5.rearrange("p (m d) -> p m d", m=M5)
    w_r6 = sb("w_r6", [P, KD, E])
    count6 = sb("count6", [P, 2 * E])
    d_w6(sp.dma_start(w_r6[:, :, :], rows("L1_ffn_Wr")))
    d_w6(sp.dma_start(count6[:, :], g["count6"]))
    w1_ring = [ctxT_buf[0][:, :, :], ctxT_buf[1][:, :, :]] + \
        [big[:, 4096 * n:4096 * n + 2048].rearrange("p (k f) -> p k f", k=KD) for n in range(2)]
    w2_ring = [ctx_buf[0][:, :, :], ctx_buf[1][:, :, :]] + \
        [big[:, 4096 * n + 2048:4096 * n + 4096].rearrange("p (f d) -> p f d", d=D) for n in range(2)]
    d_e = stream("d_e")

    def load_expert(n):
        d_e(sp.dma_start(w1_ring[n % 4], g["L1_ffn_W1"][n].rearrange("(k p) f -> p k f", p=P)))
        d_e(sp.dma_start(w2_ring[n % 4], g["L1_ffn_W2"][n].rearrange("(f p) d -> p f d", p=P)))

    d_w5(sp.dma_start(Wq5, rows("L1_attn_Wq")))
    d_w5(sp.dma_start(Wk5, rows("L1_attn_Wk")))
    d_w5(sp.dma_start(Wv5, rows("L1_attn_Wv")))
    d_w5(sp.dma_start(Wo5, rows("L1_attn_Wpost")))

    meet()
    moments(x)
    wait_before(dve, d_w3)
    a3, t3 = trig3[:, :, :, :], turns3
    wait(dve, DVE(dve.tensor_tensor(a3, a3, noise3[:, :, :, :], ALU.add)))
    ROUND = 1.5 * 2.0 ** 23
    wait(dve, DVE(dve.tensor_scalar(t3, a3, 1.0 / (2.0 * np.pi), ROUND, ALU.mult, ALU.add)))
    wait(dve, DVE(dve.tensor_scalar(t3, t3, ROUND, None, ALU.subtract)))
    high = 6.28125
    for part in (high, 2.0 * np.pi - high):
        wait(dve, DVE(dve.scalar_tensor_tensor(a3, t3, -float(part), a3, ALU.mult, ALU.add)))
    PI = 3.1415925
    wait(dve, DVE(dve.tensor_scalar(a3, a3, -PI, PI, ALU.max, ALU.min)))
    c3 = trig3[:, 0, :, :]
    wait(dve, DVE(dve.scalar_tensor_tensor(c3, c3, -1.0, c3, ALU.mult, ALU.min)))
    m = DVE(dve.tensor_scalar(c3, c3, float(np.pi / 2), None, ALU.add))
    wait(act, m)
    AC(act.activation(a3, a3, ACT.Sin))
    with ExitStack() as tmp:
        def buffers(name, shape):
            return [sb(f"{name}_{u}", shape, tmp) for u in range(U2)]

        xs, xT, c2, t2 = buffers("xs2", [P, D]), buffers("xT2", [P, KD, P]), buffers("c2", [P, P]), \
            buffers("t2", [P, 4, P])
        qT, kT, km = buffers("qT2", [P, 2, P]), buffers("kT2", [P, 2, P]), buffers("km2", [P, 2, 8, P])
        v, sm = buffers("v2", [P, 16, HD2 + 1]), buffers("sm2", [P, 2, 8, P])
        smT, top, inv, o, oT = buffers("smT2", [P, 2, 8, P]), buffers("top2", [P, 2, 8]), buffers("inv2", [P, H2]), \
            buffers("o2", [P, D]), buffers("oT2", [P, KD, P])
        for u in range(U2):
            DVE(dve.memset(v[u][:, :, HD2:HD2 + 1], 1.0))
        wait_before(dve, d_mask)
        DVE(dve.tensor_copy(mask[:, :, :], mask_in[:, :, :]))
        DVE(dve.tensor_copy(ident16[:, :], ident[:, :]))
        wait_before(pe, d_w2)
        wait_before(dve, d_w2)
        wait_before(act, d_w2)

        def body2(i, u):
            t = i * U2 + u
            A, C = banks[2 * u], banks[2 * u + 1]
            a0, a1, c0, c1 = (bank(4 * u + n) for n in range(4))
            m = normed(xs[u][:, :], x, t)
            wait(pe, m)
            yield
            m_xT = transposed_tile(xs[u], xT[u], a0)
            wait(pe, m_xT)
            yield
            for k in range(KD):
                m = pe.matmul(a1[:, 0:P], w_qkv2[:, k, :], xT[u][:, k, :], start=k == 0, stop=k == KD - 1)
            m = PE(m)
            wait(act, m)
            m_c = AC(act.activation(c2[u][:, :], a1[:, 0:P], ACT.Gelu, bias=b_qkv2[:, 0:1]))
            for r in range(4):
                for k in range(KD):
                    m = pe.matmul(c0[:, r * P:(r + 1) * P], w_r2[:, r, k, :], xT[u][:, k, :],
                                  start=k == 0, stop=k == KD - 1)
            m_r = PE(m)
            yield
            wait(pe, m_c)
            for n in range(2):
                m = pe.matmul(a0[:, n * P:(n + 1) * P], w_c2[:, n, :], c2[u][:, :], start=True, stop=True)
            m_cc = PE(m)
            m_v = PE(pe.matmul(c1[:, 0:D], c2[u][:, :], w_v2[:, :], start=True, stop=True))
            wait(dve, m_r)
            for r in range(4):
                m = DVE(dve.scalar_tensor_tensor(t2[u][:, r, :], c0[:, r * P:(r + 1) * P], b_r2[:, r:r + 1],
                                                 rope2[:, r % 2, :], ALU.add, ALU.mult))
            wait(dve, m)
            t4 = t2[u][:, :, :].rearrange("p (n s) t -> p n s t", s=2)
            m_rot = DVE(dve.tensor_tensor(t4[:, :, 0, :], t4[:, :, 0, :], t4[:, :, 1, :], ALU.add))
            yield
            wait(act, m_cc)
            for n, dst in enumerate((qT[u], kT[u])):
                AC(act.activation(dst[:, 0, :], a0[:, n * P:(n + 1) * P], ACT.Gelu, bias=b_c2[:, n:n + 1]))
            wait(act, m_rot)
            for n, dst in enumerate((qT[u], kT[u])):
                m_qk = AC(act.activation(dst[:, 1, :], t2[u][:, 2 * n, :], ACT.Gelu))
            wait(dve, m_v)
            m_v = DVE(dve.tensor_tensor(v[u][:, :, 0:HD2], c1[:, 0:D].rearrange("p (h e) -> p h e", e=HD2),
                                        b_v2[:, :].rearrange("p (h e) -> p h e", e=HD2), ALU.add))
            yield
            m_km, m_E, m_T = [], [], []
            for c, (line, e) in enumerate(((DVE, dve), (PL, pool))):
                wait(e, m_qk)
                m_km.append(line(e.tensor_tensor(km[u][:, c, :, :], kT[u][:, c:c + 1, :].broadcast_to([P, 8, P]),
                                                 head2[:, :].unsqueeze(2).broadcast_to([P, 8, P]), ALU.mult)))
            for c in range(2):
                wait(pe, m_qk, m_v)
                for hf in range(2):
                    mask_scores((A, C)[c][:, hf * BANK:(hf + 1) * BANK], 0)
                wait(pe, m_km[c])
                for hf in range(2):
                    m = pe.matmul((A, C)[c][:, hf * BANK:(hf + 1) * BANK], qT[u][:, c, :],
                                  km[u][:, c, 4 * hf:4 * hf + 4, :], start=False, stop=True)
                m_E.append(tile_exponentials(PE(m), (A, C)[c], sm[u][:, c], top[u][:, c, :], 1.0 / 4.0))
                yield
            for c in range(2):
                m_T += tile_transposes(m_E[c], (A, C)[c], sm[u][:, c], smT[u][:, c])
                yield
            wait(pe, *m_T)
            for h in range(H2):
                m = pe.matmul(a0[:, h * (HD2 + 1):(h + 1) * (HD2 + 1)], smT[u][:, h // 8, h % 8, :], v[u][:, h, :],
                              start=True, stop=True)
            m = PE(m)
            wait(dve, m)
            a0_ = a0[:, 0:16 * (HD2 + 1)].rearrange("p (h e) -> p h e", h=H2)
            m = DVE(dve.reciprocal(inv[u][:, :], a0_[:, :, HD2]))
            wait(dve, m)
            m = DVE(dve.tensor_tensor(o[u][:, :].rearrange("p (h e) -> p h e", h=H2), a0_[:, :, 0:HD2],
                                      inv[u][:, :].unsqueeze(2).broadcast_to([P, 16, HD2]), ALU.mult))
            wait(pe, m)
            yield
            m = transposed_tile(o[u], oT[u], a1)
            wait(pe, m)
            yield
            for k in range(KD):
                m = pe.matmul(c0[:, 0:D], oT[u][:, k, :], w_o2[:, k, :], start=k == 0, stop=k == KD - 1)
            m = PE(m)
            wait(dve, m)
            m = DVE(dve.tensor_tensor(o[u][:, :], c0[:, 0:D], b_o2[:, :], ALU.add))
            wait(dve, m)
            xt = x[:, bass.ds(t, 1), :].rearrange("p a d -> p (a d)")
            DVE(dve.tensor_tensor(xt, xt, o[u][:, :], ALU.add))

        with tiles(T // U2, pe=28, dve=40, act=18, pool=2) as i:
            for e in (pe, dve, act, pool):
                wait_before(e, PE, DVE, AC, PL)
            interleave(*(body2(i, u) for u in range(U2)))

    meet()
    moments(x)
    with ExitStack() as tmp:
        def buffers(name, shape):
            return [sb(f"{name}_{u}", shape, tmp) for u in range(U2)]

        xs, xT, sq = buffers("xs3", [P, D]), buffers("xT3", [P, KD, P]), buffers("sq3", [P, 2, D])

        def body3(i, u):
            t = i * U2 + u
            into, ps = bank(2 * u), bank(2 * u + 1)
            m = normed(xs[u][:, :], x, t)
            wait(pe, m)
            m = transposed_tile(xs[u], xT[u], into)
            wait(pe, m)
            yield
            for n in range(2):
                for k in range(KD):
                    m = pe.matmul(ps[:, n * D:(n + 1) * D], xT[u][:, k, :], trig3[:, n, k, :],
                                  start=k == 0, stop=k == KD - 1)
            m = PE(m)
            wait(act, m)
            m = AC(act.activation(sq[u][:, :, :], ps.rearrange("p (n d) -> p n d", n=2), ACT.Square))
            wait(dve, m)
            yield
            m = DVE(dve.tensor_tensor(sq[u][:, 0, :], sq[u][:, 0, :], sq[u][:, 1, :], ALU.add))
            wait(act, m)
            m = AC(act.activation(sq[u][:, 0, :], sq[u][:, 0, :], ACT.Sqrt))
            yield
            wait(dve, m)
            xt = x[:, bass.ds(t, 1), :].rearrange("p a d -> p (a d)")
            DVE(dve.tensor_tensor(xt, xt, sq[u][:, 0, :], ALU.add))

        with tiles(T // U2, pe=4, dve=8, act=4) as i:
            for e in (pe, dve, act):
                wait_before(e, PE, DVE, AC)
            interleave(*(body3(i, u) for u in range(U2)))

    meet()
    with ExitStack() as tmp:
        def tb(name, shape):
            return sb(name, shape, tmp)

        raw = tb("raw", [P, KC, D])

        def load_ctx4(b, t):
            d_raw(sp.dma_start(raw[:, :, :], ctx_rows[bass.ds(t, 1), b].rearrange("a p k n -> (a p) k n")))

        load_ctx4(0, 0)
        moments(x)
        with tiles(T, dve=1) as i:
            normed(xn[:, bass.ds(i, 1), :].rearrange("p a d -> p (a d)"), x, i)
        wait_before(dve, DVE)
        moments(xn)
        with tiles(T, dve=1) as i:
            normed(xn[:, bass.ds(i, 1), :].rearrange("p a d -> p (a d)"), xn, i)
        wait_before(dve, DVE, d_w4)
        wait(dve, DVE(dve.tensor_tensor(xn[:, 0:T, :], xn[:, 0:T, :], gb4[:, 2:3, :].broadcast_to([P, T, D]), ALU.mult)))
        wait(dve, DVE(dve.tensor_tensor(xn[:, 0:T, :], xn[:, 0:T, :], gb4[:, 3:4, :].broadcast_to([P, T, D]), ALU.add)))
        DVE(dve.tensor_copy(xn[:, T, :], xn[:, 0, :]))
        NC_ = B * KC
        stat = [stats_c[:, 0:NC_, n] for n in range(6)]
        m = DVE(dve.tensor_tensor(mean_c[:, 0:NC_], stat[1], stat[4], ALU.add))
        m = DVE(dve.tensor_tensor(rstd_c[:, 0:NC_], stat[1], stat[4], ALU.subtract))
        wait(dve, m)
        m = DVE(dve.tensor_scalar(mean_c[:, 0:NC_], mean_c[:, 0:NC_], 0.5, None, ALU.mult))
        m = DVE(dve.tensor_tensor(rstd_c[:, 0:NC_], rstd_c[:, 0:NC_], rstd_c[:, 0:NC_], ALU.mult))
        wait(dve, m)
        m = DVE(dve.tensor_scalar(rstd_c[:, 0:NC_], rstd_c[:, 0:NC_], 0.25, EPS, ALU.mult, ALU.add))
        m = DVE(dve.tensor_tensor(stat[2], stat[2], stat[5], ALU.add))
        wait(dve, m)
        m = DVE(dve.scalar_tensor_tensor(rstd_c[:, 0:NC_], stat[2], 1.0 / D, rstd_c[:, 0:NC_], ALU.mult, ALU.add))
        wait(act, m)
        m = AC(act.activation(rstd_c[:, 0:NC_], rstd_c[:, 0:NC_], ACT.Sqrt))
        wait(dve, m)
        m = DVE(dve.reciprocal(rstd_c[:, 0:NC_], rstd_c[:, 0:NC_]))
        wait(dve, m)
        for c in (mean_c, rstd_c):
            m = DVE(dve.tensor_copy(c[:, NC_:NC_ + BT * KC], c[:, 0:BT * KC]))
        wait(dve, m)

        SCALE4 = 1.0 / 8.0
        KEYS = CTX + S
        xs = tb("xs4", [P, D])
        xT = tb("xT4", [P, KD, P])
        lat = tb("lat4", [P, BT, D])
        q_bd = tb("q_bd4", [P, 2, M4, BT, P])
        kcs = tb("kcs4", [P, 2, CTX])
        kl = tb("kl4", [P, M4, BT, S])
        prob = [tb(f"prob4_{n}", [P, KEYS]) for n in range(2)]
        probT = [tb(f"probT4_{n}", [P, KC + 1, 2 * P]) for n in range(2)]
        u_sb = tb("u4", [P, KD, 2 * P])
        attn = tb("attn4", [P, M4, P])
        mx, nb, rs = ([tb(f"{a}4_{n}", [P, 2]) for n in range(2)] for a in ("mx", "nb", "rs"))
        MISC, U, TP = bank(6), bank(7), (bank(4), bank(5))
        KPS, SPS = banks[0], banks[1]
        DVE(dve.memset(q_bd[:, :, :, :, :], 0.0))
        DVE(dve.memset(lat[:, :, :], 0.0))
        for p in probT:
            DVE(dve.memset(p[:, KC, :], 0.0))
        wait_before(pe, d_w4)
        wait_before(dve, d_w4)
        wait_before(pool, d_w4)
        STEPS = M4 // 2
        UNITS = BT * M4

        class Turn:

            def __init__(self):
                self.kcs, self.S, self.exp, self.P, self.T, self.PT, self.latT = ({} for _ in range(7))
                self.A, self.u, self.V, self.at, self.ctxT, self.norm, self.raw = ({} for _ in range(7))
                self.q = []
                self.tp = [None, None]

        def normalize_rows(half, t, b, d_count, w):
            if half == 0:
                dve.wait_ge(d_raw.sem, d_count)
            for c in range(half * KC // 2, (half + 1) * KC // 2):
                at = (t * BT + b) * KC + c
                m = DVE(dve.tensor_scalar(raw[:, c, :], raw[:, c, :], mean_c[:, bass.ds(at, 1)],
                                          rstd_c[:, bass.ds(at, 1)], ALU.subtract, ALU.mult))
            wait(pool, m)
            c = slice(half * KC // 2, (half + 1) * KC // 2)
            w.norm[half] = PL(pool.tensor_tensor(raw[:, c, :], raw[:, c, :],
                                                 gb4[:, 0:1, :].broadcast_to([P, KC // 2, D]), ALU.mult))

        def shift_rows(b, w, read=None):
            wait(pool, read)
            for half in range(2):
                wait(pool, w.norm[half])
                c = slice(half * KC // 2, (half + 1) * KC // 2)
                w.raw[b, half] = PL(pool.tensor_tensor(ctx_buf[b][:, c, :], raw[:, c, :],
                                                       gb4[:, 1:2, :].broadcast_to([P, KC // 2, D]), ALU.add))

        def transpose_context(b, k, w):
            for hf in range(2):
                wait(pe, w.raw[b, hf], w.tp[hf])
                for c in range(4):
                    m = pe.transpose(TP[hf][:, c * P:(c + 1) * P], ctx_buf[b][:, 4 * hf + c, k * P:(k + 1) * P],
                                     ident[:, :])
                m = PE(m)
                dst, src = ctxT_buf[b][:, k, hf * BANK:(hf + 1) * BANK], TP[hf]
                if hf == 0:
                    wait(dve, m)
                    m = DVE(dve.tensor_copy(dst, src))
                else:
                    wait(act, m)
                    m = AC(act.activation(dst, src, ACT.Copy))
                w.tp[hf] = w.ctxT[b, k, hf] = m

        def keys(n, half, w):
            b, m_ = n // M4 % BT, n % M4
            wait(pe, w.kcs.get((n - 1, half)))
            if m_ == 0:
                wait(pe, *(w.ctxT.get((b, k, half)) for k in range(KD)))
            cols = slice(half * BANK, (half + 1) * BANK)
            for k in range(KD):
                m = pe.matmul(KPS[:, cols], w_k4[:, k, m_ * P:(m_ + 1) * P], ctxT_buf[b][:, k, cols],
                              start=k == 0, stop=k == KD - 1)
            m = PE(m)
            wait(dve, m, w.S.get(n - 1))
            for part in range(2):
                m = DVE(dve.tensor_tensor(kcs[:, part, cols], KPS[:, cols], rope4[:, part, cols], ALU.mult))
            w.kcs[n, half] = m

        def scores(n, w):
            b, m_ = n // M4, n % M4
            wait(pe, *(w.q if n == 0 else ()))
            wait(pe, w.kcs.get((n, 0)), w.kcs.get((n, 1)), w.exp.get(n - 1), w.latT.get(n - 1))
            for half in range(HALF):
                for part in range(2):
                    cols = slice(half * BANK, (half + 1) * BANK)
                    pe.matmul(SPS[:, cols], q_bd[:, part, m_, b, :], kcs[:, part, cols],
                              start=part == 0, stop=part == 1)
            w.S[n] = PE(pe.matmul(MISC[:, 0:S], q_bd[:, 0, m_, b, :], kl[:, m_, b, :], start=True, stop=True))

        def exponentials(n, w):
            p = n % 2
            wait(dve, w.S[n])
            DVE(dve.tensor_reduce(mx[p][:, 0:1], SPS[:, :], AX.X, ALU.max))
            m = DVE(dve.tensor_reduce(mx[p][:, 1:2], MISC[:, 0:S], AX.X, ALU.max))
            wait(dve, m)
            m = DVE(dve.tensor_scalar(nb[p][:, 0:1], mx[p][:, 0:1], mx[p][:, 1:2], -SCALE4, ALU.max, ALU.mult))
            wait(act, m, w.T.get(n - 2))
            AC(act.activation(prob[p][:, 0:CTX], SPS[:, :], ACT.Exp, bias=nb[p][:, 0:1], scale=SCALE4,
                              accum_out=rs[p][:, 0:1]))
            w.exp[n] = AC(act.activation(prob[p][:, CTX:KEYS], MISC[:, 0:S], ACT.Exp, bias=nb[p][:, 0:1],
                                         scale=SCALE4, accum_out=rs[p][:, 1:2]))

        def weights(n, w):
            p = n % 2
            wait(dve, w.exp[n])
            m = DVE(dve.tensor_tensor(nb[p][:, 1:2], rs[p][:, 0:1], rs[p][:, 1:2], ALU.add))
            wait(dve, m)
            m = DVE(dve.reciprocal(nb[p][:, 1:2], nb[p][:, 1:2]))
            wait(dve, m)
            w.P[n] = DVE(dve.tensor_scalar(prob[p][:, :], prob[p][:, :], nb[p][:, 1:2], None, ALU.mult))

        def transposed(n, w):
            p, s = n % 2, n // 2
            wait(pe, w.P[n], *w.tp)
            for c in range(KC):
                m = pe.transpose(TP[c // 4][:, (c % 4) * P:(c % 4 + 1) * P], prob[p][:, c * P:(c + 1) * P],
                                 ident[:, :])
                if c == 0:
                    PE(pe.transpose(MISC[0:S, P:2 * P], prob[p][:, CTX:KEYS], ident[:, :]))
                if c == 3:
                    first = PE(m)
            w.T[n] = PE(m)
            cols = slice(p * P, (p + 1) * P)
            wait(dve, first, w.A.get((s - 2, 1)))
            w.latT[n] = DVE(dve.tensor_copy(probT[s % 2][0:S, KC, cols], MISC[0:S, P:2 * P]))
            w.tp[0] = DVE(dve.tensor_copy(probT[s % 2][:, 0:4, cols], TP[0].rearrange("p (c q) -> p c q", c=4)))
            wait(act, w.T[n], w.A.get((s - 2, 1)))
            w.tp[1] = AC(act.activation(probT[s % 2][:, 4:8, cols], TP[1].rearrange("p (c q) -> p c q", c=4), ACT.Copy))
            w.PT[n] = list(w.tp)

        def average(s, k, w):
            b = s // STEPS
            if k == 0:
                wait(pe, *w.PT[2 * s + 1], w.at.get(s - 1))
            else:
                wait(pe, w.u[s, 0])
            for c in range(KC + 1):
                src = ctx_buf[b][:, c, k * P:(k + 1) * P] if c < KC else lat[:, b, k * P:(k + 1) * P]
                m = pe.matmul(U[:, k * 2 * P:(k + 1) * 2 * P], src, probT[s % 2][:, c, :], start=c == 0, stop=c == KC)
            w.A[s, k] = PE(m)
            wait(act, w.A[s, k], w.V.get(s - 1))
            w.u[s, k] = AC(act.activation(u_sb[:, k, :], U[:, k * 2 * P:(k + 1) * 2 * P], ACT.Copy))

        def values(s, w):
            b = s // STEPS
            wait(pe, w.u[s, 1])
            first = 2 * (s % STEPS)
            for pr in range(2):
                for k in range(KD):
                    pair = first + pr
                    m = pe.matmul(U[:, pr * P:(pr + 1) * P], w_v4[:, k, pair * P:(pair + 1) * P],
                                  u_sb[:, k, pr * P:(pr + 1) * P], start=k == 0, stop=k == KD - 1)
            w.V[s] = PE(m)
            wait(dve, w.V[s])
            for h in range(2):
                r = slice(h * S, (h + 1) * S)
                w.at[s] = DVE(dve.tensor_copy(attn[r, first:first + 2, b * S:(b + 1) * S],
                                              U[r, 0:2 * P].rearrange("p (r n) -> p r n", r=2)[:, :, r]))

        w = Turn()
        for half in range(2):
            normalize_rows(half, 0, 0, 16, w)
        shift_rows(0, w)
        m_shift = w.raw[0, 1]
        for k in range(KD):
            transpose_context(0, k, w)
        for half in range(HALF):
            keys(0, half, w)
        DVE(dve.tensor_copy(xs[:, :], xn[:, 0, :]))
        wait(sp, m_shift)
        load_ctx4(1, 0)
        with tiles(T, pe=73, dve=133, act=37, pool=8) as i:
            w = Turn()
            for e in (pe, dve, act, pool):
                wait_before(e, PE, DVE, AC, PL)
            for b in range(BT):
                DVE(dve.tensor_copy(lat[0:S, b, :], xs[b * S:(b + 1) * S, :]))
            m_lnT = transposed_tile(xs, xT, MISC)
            wait(pe, m_lnT)
            for part, ps in enumerate((MISC, U)):
                for m_ in range(M4):
                    for k in range(KD):
                        m = pe.matmul(ps[:, m_ * P:(m_ + 1) * P], w_q4[:, part, k, m_ * P:(m_ + 1) * P], xT[:, k, :],
                                      start=k == 0, stop=k == KD - 1)
                m = PE(m)
                wait(dve, m)
                for h in range(2):
                    r = slice(h * S, (h + 1) * S)
                    m = DVE(dve.tensor_scalar(q_bd[r, part, :, :, r],
                                              ps[r, :].rearrange("p (m b q) -> p m b q", m=M4, b=BT),
                                              turn4[r, part:part + 1], None, ALU.mult))
            w.q.append(m)
            for m_ in range(M4):
                for k in range(KD):
                    m = pe.matmul(KPS[:, m_ * P:(m_ + 1) * P], w_k4[:, k, m_ * P:(m_ + 1) * P], xT[:, k, :],
                                  start=k == 0, stop=k == KD - 1)
            m = PE(m)
            wait(act, m)
            m = AC(act.activation(kl[:, :, :, :], KPS[:, 0:M4 * P].rearrange("p (m b q) -> p m b q", m=M4, b=BT),
                                  ACT.Copy))
            w.q.append(m)
            w.kcs[0, 0] = m
            scores(0, w)
            for n in range(UNITS):
                m_, other = n % M4, (n // M4 + 1) % BT
                exponentials(n, w)
                if m_ == M4 - 1 and n >= 2:
                    average(n // 2 - 1, n % 2, w)
                keys(n + 1, 0, w)
                weights(n, w)
                keys(n + 1, 1, w)
                if m_ == 2:
                    transpose_context(other, 0, w)
                if m_ != M4 - 1 and n >= 2:
                    average(n // 2 - 1, n % 2, w)
                if m_ == M4 - 1:
                    values(n // 2 - 1, w)
                transposed(n, w)
                if m_ < 2:
                    normalize_rows(m_, i + n // M4, other, i * 32 + (n // M4) * 16 + 32, w)
                if m_ == 1:
                    shift_rows(other, w, w.A.get((STEPS - 1, 1)))
                if n + 1 < UNITS:
                    scores(n + 1, w)
                if m_ == 1 and n >= 2:
                    values(n // 2 - 1, w)
                if m_ == 2:
                    transpose_context(other, 1, w)
            DVE(dve.tensor_copy(xs[:, :], xn[:, bass.ds(i + 1, 1), :].rearrange("p a d -> p (a d)")))
            last = UNITS // 2 - 1
            average(last, 0, w)
            average(last, 1, w)
            values(last, w)
            wait(pe, w.at[last])
            for m_ in range(M4):
                m = pe.matmul(U[:, 0:D], attn[:, m_, :], w_o4[:, m_, :], start=m_ == 0, stop=m_ == M4 - 1)
            m = PE(m)
            wait(dve, m)
            DVE(dve.tensor_tensor(x[:, i, :], x[:, i, :], U[:, 0:D], ALU.add))
            shifted = [w.raw[1, 1], w.raw[0, 1]]
        with nc.Fori(0, T - 1, engines=(sp.engine,)) as j:
            for b in range(BT):
                sp.wait_ge(PL.sem, shifted[b].at(j))
                load_ctx4(b, j + 1)
        sp.wait_ge(PL.sem, shifted[0].at(T - 1))
        load_ctx4(0, 0)
    meet()
    load_expert(0)
    load_expert(1)

    meet()
    moments(x)
    with ExitStack() as tmp:
        def buffers(name, shape):
            return [sb(f"{name}_{u}", shape, tmp) for u in range(U2)]

        xs, xT, q5, k_bd = buffers("xs5", [P, D]), buffers("xT5", [P, KD, P]), buffers("q5", [P, M5, P]), \
            buffers("k_bd5", [P, M5, 2, P])
        v5, sm, smT = buffers("v5", [P, 2 * M5, S + 1]), buffers("sm5", [P, 8, P]), buffers("smT5", [P, 8, P])
        top, inv, a5, aT5 = buffers("top5", [P, 8]), buffers("inv5", [P, 8]), buffers("a5", [P, M5 * P]), \
            buffers("aT5", [P, M5, P])
        for u in range(U2):
            DVE(dve.memset(k_bd[u][:, :, :, :], 0.0))
            DVE(dve.memset(v5[u][:, :, S:S + 1], 1.0))
        wait_before(pe, d_w5)

        def body5(i, u):
            t = i * U2 + u
            A, C = banks[2 * u], banks[2 * u + 1]
            m_x = normed(xs[u][:, :], x, t)
            wait(pe, m_x)
            yield
            m_xT = transposed_tile(xs[u], xT[u], C)
            wait(pe, m_xT)
            yield
            for hf in range(2):
                for mm in range(4):
                    for k in range(KD):
                        pair = 4 * hf + mm
                        m = pe.matmul(A[:, pair * P:(pair + 1) * P], Wq5[:, k, pair * P:(pair + 1) * P], xT[u][:, k, :],
                                      start=k == 0, stop=k == KD - 1)
                m = PE(m)
                wait(act, m)
                m_q = AC(act.activation(q5[u][:, 4 * hf:4 * hf + 4, :],
                                        A[:, hf * BANK:(hf + 1) * BANK].rearrange("p (m q) -> p m q", m=4), ACT.Copy))
            yield
            for hf in range(2):
                for mm in range(4):
                    for k in range(KD):
                        pair = 4 * hf + mm
                        m = pe.matmul(C[:, pair * P:(pair + 1) * P], Wk5[:, k, pair * P:(pair + 1) * P], xT[u][:, k, :],
                                      start=k == 0, stop=k == KD - 1)
                m = PE(m)
                wait(dve, m)
                for h in range(2):
                    r = slice(h * S, (h + 1) * S)
                    m_k = DVE(dve.tensor_copy(k_bd[u][r, 4 * hf:4 * hf + 4, h, :],
                                              C[r, hf * BANK:(hf + 1) * BANK].rearrange("p (m q) -> p m q", m=4)))
            yield
            wait(pe, m_q)
            for hf in range(2):
                for k in range(KD):
                    m = pe.matmul(A[:, hf * BANK:(hf + 1) * BANK], xT[u][:, k, :],
                                  Wv5[:, k, hf * BANK:(hf + 1) * BANK], start=k == 0, stop=k == KD - 1)
                m = PE(m)
                wait(act, m)
                m_v = AC(act.activation(v5[u][:, 8 * hf:8 * hf + 8, 0:S],
                                        A[:, hf * BANK:(hf + 1) * BANK].rearrange("p (h e) -> p h e", h=8), ACT.Copy))
            yield
            m_o = None
            m_T = []
            for grp in range(2):
                wait(pe, m_k, m_o)
                for hf in range(2):
                    mask_scores(C[:, hf * BANK:(hf + 1) * BANK], 1)
                for mm in range(4):
                    pair = 4 * grp + mm
                    m = pe.matmul(C[:, mm * 2 * P:(mm + 1) * 2 * P], q5[u][:, pair, :], k_bd[u][:, pair, :, :],
                                  start=False, stop=mm % 2 == 1)
                m_E = tile_exponentials(PE(m), C, sm[u], top[u][:, :], 1.0 / 8.0)
                yield
                wait(pe, m_v, *m_T)
                m_T = tile_transposes(m_E, A, sm[u], smT[u])
                yield
                wait(pe, *m_T)
                for h in range(8):
                    at = (h // 4) * BANK + (h % 4) * (S + 1)
                    m = pe.matmul(C[:, at:at + S + 1], smT[u][:, h, :], v5[u][:, 8 * grp + h, :], start=True, stop=True)
                wait(dve, PE(m))
                parts = C[:, :].rearrange("p (b n) -> p b n", b=2)[:, :, 0:4 * (S + 1)].rearrange(
                    "p b (h e) -> p b h e", h=4)
                inv_ = inv[u][:, :].rearrange("p (b h) -> p b h", b=2)
                for b in range(2):
                    m = DVE(dve.reciprocal(inv_[:, b, :], parts[:, b, :, S]))
                wait(dve, m)
                for b in range(2):
                    at = slice((2 * grp + b) * D, (2 * grp + b + 1) * D)
                    m_o = DVE(dve.tensor_tensor(a5[u][:, at].rearrange("p (h e) -> p h e", h=4), parts[:, b, :, 0:S],
                                                inv_[:, b, :].unsqueeze(2).broadcast_to([P, 4, S]), ALU.mult))
                yield
            wait(act, m_o)
            m = AC(act.activation(a5[u][:, :], a5[u][:, :], ACT.Gelu))
            yield
            wait(pe, m, *m_T)
            m_aT = []
            for hf, (line, e) in enumerate(((DVE, dve), (AC, act))):
                for mm in range(4 * hf, 4 * hf + 4):
                    m = pe.transpose(A[:, mm * P:(mm + 1) * P], a5[u][:, mm * P:(mm + 1) * P], ident[:, :])
                wait(e, PE(m))
                dst = aT5[u][:, 4 * hf:4 * hf + 4, :]
                src = A[:, hf * BANK:(hf + 1) * BANK].rearrange("p (m q) -> p m q", m=4)
                m_aT.append(line(e.tensor_copy(dst, src) if e is dve else e.activation(dst, src, ACT.Copy)))
            yield
            wait(pe, *m_aT)
            for mm in range(M5):
                m = pe.matmul(A[:, 0:D], aT5[u][:, mm, :], Wo5[:, mm, :], start=mm == 0, stop=mm == M5 - 1)
            m = PE(m)
            wait(dve, m)
            m = DVE(dve.tensor_tensor(xs[u][:, :], xs[u][:, :], A[:, 0:D], ALU.add))
            wait(dve, m)
            xt = x[:, bass.ds(t, 1), :].rearrange("p a d -> p (a d)")
            DVE(dve.tensor_tensor(xt, xt, xs[u][:, :], ALU.add))

        with tiles(T // U2, pe=36, dve=46, act=20) as i:
            for e in (pe, dve, act):
                wait_before(e, PE, DVE, AC)
            interleave(*(body5(i, u) for u in range(U2)))

    meet()
    load_expert(2)
    load_expert(3)
    moments(x)
    with ExitStack() as tmp:
        def tb(name, shape):
            return sb(name, shape, tmp)

        xs, xT = [tb(f"xs6_{u}", [P, D]) for u in range(U2)], [tb(f"xT6_{u}", [P, KD, P]) for u in range(U2)]
        logit, hot, work, rank_in = (tb(n, [P, T, E]) for n in ("logit6", "hot6", "work6", "rank6"))
        first6, top, p_tok, rank, slot, keep = (tb(n, [P, T]) for n in
                                                ("first6", "top6", "p_tok6", "rank_tok6", "slot6", "keep6"))
        iota6, earlier6 = tb("iota6", [P, E * CAP]), tb("earlier6", [P, P])
        d_w6(sp.dma_start(iota6[:, :], everywhere("iota6")))
        d_w6(sp.dma_start(earlier6[:, :], g["earlier6"]))
        select = tb("select6", [P, T, E * CAP])
        xe = tb("xe6", [P, KD, E * CAP])
        hT = [tb(f"hT6_{n}", [P, F // P, CAP]) for n in range(2)]
        ye = tb("ye6", [P, E, D])
        slot_row = tb("slot_row6", [P, T * P])
        wait_before(pe, d_w6)
        wait_before(dve, d_w6)

        def body6(i, u):
            t = i * U2 + u
            xt = xn[:, bass.ds(t, 1), :].rearrange("p a d -> p (a d)")
            normed(xt, x, t)
            m = normed(xs[u][:, :], x, t)
            wait(pe, m)
            m = transposed_tile(xs[u], xT[u], bank(2 * u))
            wait(pe, m)
            yield
            for k in range(KD):
                m = pe.matmul(bank(2 * u + 1)[:, 0:E], xT[u][:, k, :], w_r6[:, k, :], start=k == 0, stop=k == KD - 1)
            m = PE(m)
            wait(dve, m)
            DVE(dve.tensor_copy(logit[:, bass.ds(t, 1), :].rearrange("p a e -> p (a e)"), bank(2 * u + 1)[:, 0:E]))

        with tiles(T // U2, pe=4, dve=8) as i:
            for e in (pe, dve):
                wait_before(e, PE, DVE)
            interleave(*(body6(i, u) for u in range(U2)))
        wait_before(dve, DVE)

        def over_experts(v):
            return v[:, :].unsqueeze(2).broadcast_to([P, T, E])

        def over_tiles(v):
            return v.unsqueeze(1).broadcast_to([P, T, E])

        wait(dve, DVE(dve.tensor_reduce(top[:, :], logit[:, :, :], AX.X, ALU.max)))
        m = DVE(dve.tensor_tensor(logit[:, :, :], logit[:, :, :], over_experts(top), ALU.subtract))
        wait(act, m)
        m_e = AC(act.activation(work[:, :, :], logit[:, :, :], ACT.Exp))
        wait(dve, m_e)
        m = DVE(dve.tensor_reduce(p_tok[:, :], work[:, :, :], AX.X, ALU.add))
        wait(dve, m)
        DVE(dve.reciprocal(p_tok[:, :], p_tok[:, :]))
        m = DVE(dve.tensor_scalar(hot[:, :, :], logit[:, :, :], 0.0, None, ALU.is_ge))
        wait(dve, m)
        m = DVE(dve.tensor_tensor(work[:, :, :], hot[:, :, :], over_tiles(count6[:, 0:E]), ALU.mult))
        wait(dve, m)
        m = DVE(dve.tensor_reduce(first6[:, :], work[:, :, :], AX.X, ALU.max))
        wait(dve, m)
        m = DVE(dve.tensor_tensor(hot[:, :, :], work[:, :, :], over_experts(first6), ALU.is_equal))
        wait(pe, m)
        flat = hot[:, :, :].rearrange("p t e -> p (t e)")
        pe.matmul(bank(0)[:, 0:T * E], earlier6[:, :], flat, start=True, stop=True)
        m = PE(pe.matmul(bank(1)[:, 0:T * E], ones[:, :], flat, start=True, stop=True))
        wait(dve, m)
        DVE(dve.tensor_copy(rank_in[:, :, :], bank(0)[:, 0:T * E].rearrange("p (t e) -> p t e", t=T)))
        m = DVE(dve.tensor_copy(work[:, :, :], bank(1)[:, 0:T * E].rearrange("p (t e) -> p t e", t=T)))
        for t in range(1, T):
            wait(dve, m)
            m = DVE(dve.tensor_tensor(work[:, t, :], work[:, t, :], work[:, t - 1, :], ALU.add))
        wait(dve, m)
        m = DVE(dve.tensor_tensor(rank_in[:, 1:T, :], rank_in[:, 1:T, :], work[:, 0:T - 1, :], ALU.add))
        wait(dve, m)
        m = DVE(dve.tensor_tensor(rank_in[:, :, :], rank_in[:, :, :], hot[:, :, :], ALU.mult))
        wait(dve, m)
        m = DVE(dve.tensor_reduce(rank[:, :], rank_in[:, :, :], AX.X, ALU.add))
        wait(dve, m)
        DVE(dve.tensor_scalar(keep[:, :], rank[:, :], float(CAP), None, ALU.is_lt))
        m = DVE(dve.scalar_tensor_tensor(slot[:, :], first6[:, :], -float(CAP), rank[:, :], ALU.mult, ALU.add))
        wait(dve, m)
        m = DVE(dve.scalar_tensor_tensor(slot[:, :], slot[:, :], float(CAP * E + 1), keep[:, :], ALU.add, ALU.mult))
        wait(dve, m)
        m = DVE(dve.tensor_scalar(slot[:, :], slot[:, :], -1.0, None, ALU.add))
        wait(dve, m)
        for t in range(T):
            m = DVE(dve.tensor_scalar(select[:, t, :], iota6[:, :], slot[:, t:t + 1], None, ALU.is_equal))
        wait(pe, m)
        m_xe = []
        for k in range(KD):
            for half in range(2):
                n = 2 * k + half
                cols = slice(half * BANK, (half + 1) * BANK)
                for t in range(T):
                    m = pe.matmul(bank(4 + n), xn[:, t, k * P:(k + 1) * P], select[:, t, cols],
                                  start=t == 0, stop=t == T - 1)
                m = PE(m)
                e, line = ((dve, DVE), (act, AC))[half]
                wait(e, m)
                m_xe.append(line(dve.tensor_copy(xe[:, k, cols], bank(4 + n)) if e is dve else
                                 act.activation(xe[:, k, cols], bank(4 + n), ACT.Copy)))
        m_gather = m
        wait(dve, m_gather)
        for t in range(T):
            m = DVE(dve.tensor_scalar(select[:, 0, t * P:(t + 1) * P], ident[:, :], slot[:, t:t + 1], None, ALU.mult))
        wait(pe, m)
        for half in range(2):
            m = PE(pe.matmul(bank(2 + half), ones[:, :], select[:, 0, half * BANK:(half + 1) * BANK],
                             start=True, stop=True))
        wait(dve, m)
        m = DVE(dve.tensor_copy(slot_row[:, :], banks[1][:, :]))
        wait(dve, m)
        for e_ in range(E):
            m_back = DVE(dve.tensor_scalar(select[:, e_, :], slot_row[:, :], count6[:, E + e_:E + e_ + 1], None,
                                           ALU.is_equal))

        wait(pe, *m_xe)
        wait_before(pe, DVE, AC)

        RING = 4
        with tiles(E // RING, pe=12, dve=8, act=4) as i:
            m_h, m_H, m_Y, m_y = {}, {}, {}, {}
            for e in (pe, dve, act):
                wait_before(e, PE, DVE, AC)
            pe.wait_ge(d_e.sem, (i * RING + RING) * 32)

            def up(n):
                w1 = w1_ring[n]
                for hf in range(2):
                    wait(pe, m_h.get((n - 2, hf)))
                    ps = banks[n % 2][:, hf * BANK:(hf + 1) * BANK]
                    for ff in range(4):
                        f = 4 * hf + ff
                        for k in range(KD):
                            m = pe.matmul(ps[:, ff * CAP:(ff + 1) * CAP], w1[:, k, f * P:(f + 1) * P],
                                          xe[:, k, bass.ds((i * RING + n) * CAP, CAP)],
                                          start=k == 0, stop=k == KD - 1)
                    m_H[n] = m = PE(m)
                    e, line = ((dve, DVE), (act, AC))[hf]
                    wait(e, m, m_Y.get(n - 2))
                    dst, src = hT[n % 2][:, 4 * hf:4 * hf + 4, :], ps.rearrange("p (f c) -> p f c", f=4)
                    m_h[n, hf] = line(dve.tensor_scalar(dst, src, 0.0, None, ALU.max) if e is dve else
                                      act.activation(dst, src, ACT.Relu))

            def down(n):
                wait(pe, m_h[n, 0], m_h[n, 1], m_y.get(n - 2))
                ps = bank(4 + n % 2)[:, 0:D]
                for f in range(F // P):
                    m = pe.matmul(ps, hT[n % 2][:, f, :], w2_ring[n][:, f, :], start=f == 0, stop=f == F // P - 1)
                m_Y[n] = PE(m)
                wait(dve, m_Y[n])
                dst = ye[:, bass.ds(i * RING + n, 1), :].rearrange("p a d -> p (a d)")
                m_y[n] = DVE(dve.tensor_copy(dst, ps))

            up(0)
            for n in range(RING):
                if n + 1 < RING:
                    up(n + 1)
                down(n)
            ring_read = [m_Y[n] for n in range(RING)]
        for n in range(RING):
            sp.wait_ge(PE.sem, ring_read[n].at(0))
            load_expert(RING + n)

        wait_before(pe, DVE, AC)
        m_o = {}
        for t in range(T):
            wait(pe, m_o.get(t - 4))
            for e_ in range(E):
                m = pe.matmul(bank(2 * (t % 4))[:, 0:D], select[:, e_, t * P:(t + 1) * P], ye[:, e_, :],
                              start=e_ == 0, stop=e_ == E - 1)
            m = PE(m)
            wait(dve, m)
            m_o[t] = DVE(dve.scalar_tensor_tensor(x[:, t, :], bank(2 * (t % 4))[:, 0:D], p_tok[:, t:t + 1], x[:, t, :],
                                                  ALU.mult, ALU.add))
            wait(sp, m_o[t])
            d_out(sp.dma_start(out[t * P:(t + 1) * P, :], x[:, t, :]))
        sp.wait_ge(d_out.sem, T * 16)



def constants():
    f = np.float32
    token = np.arange(P)
    same = token[:, None] // S == token[None, :] // S
    masks = np.stack([np.where(same & (token[None, :] <= token[:, None]), 0.0, MASKED),
                      np.where(same, 0.0, MASKED)]).astype(f)

    def angles(positions, width):
        inv = f(1.0) / np.power(f(10000.0), np.arange(0, width, 2, dtype=f) / f(width), dtype=f)
        a = np.arange(positions, dtype=f)[:, None] * inv[None, :]
        return np.concatenate([a, a], axis=1).T

    a2 = angles(S, P)
    sign = np.where(token < P // 2, -1.0, 1.0).astype(f)[:, None]
    rope2 = np.stack([np.tile(np.cos(a2), (1, BT)), np.tile(np.sin(a2) * sign, (1, BT))]).astype(f)
    head2 = (token[:, None] // 16 == np.arange(8)[None, :]).astype(f)
    a4 = np.tile(angles(CTX, 64), (2, 1))
    rope4 = np.stack([np.cos(a4), np.sin(a4)]).astype(f)
    turn4 = np.stack([np.ones(P), np.where(token % 64 < 32, 1.0, -1.0)], axis=1).astype(f)
    return {"masks": masks, "rope2": rope2, "head2": head2, "rope4": rope4, "turn4": turn4,
            "count6": np.concatenate([np.tile(8 - np.arange(8), (P, 1)),
                                      token[:, None] + P * np.arange(8)[None, :]], axis=1).astype(f),
            "iota6": np.arange(8 * P).astype(f), "earlier6": (token[:, None] < token[None, :]).astype(f)}


def kernel(**inputs):
    import numpy as _np
    import concourse.bacc as _bacc
    from concourse import mybir as _mybir
    from concourse.bass_utils import run_bass_kernel_spmd as _run

    a = {k: _np.asarray(v) for k, v in inputs.items()}

    def pairs(v):
        return v.reshape(-1, P).T

    lay = {
        "x": a["x"].reshape(B * S, D),
        "ctx_1024": a["ctx_1024"].reshape(B * CTX, D).reshape(B, CTX, D),
        "ctx_T": a["ctx_1024"].transpose(0, 2, 1),
        "L0_xattn_Wq": a["L0_xattn_Wq"].reshape(D, -1),
        "L0_xattn_WkT": a["L0_xattn_Wk"].reshape(D, -1).T,
        "L0_xattn_Wv": a["L0_xattn_Wv"].reshape(D, -1),
        "L0_xattn_Wo": a["L0_xattn_Wo"].reshape(-1, D),
        "L0_xattn_bq": pairs(a["L0_xattn_bq"].reshape(-1)),
        "L0_xattn_bk": pairs(a["L0_xattn_bk"].reshape(-1)),
        "L0_xattn_bv": pairs(a["L0_xattn_bv"].reshape(-1)),
        "L0_xattn_bo": a["L0_xattn_bo"],
    }
    for name in ("wq", "bq", "wqc", "bqc", "wqr", "bqr", "wkv", "bkv", "wkr", "bkr", "wkc", "bkc", "wv", "bv",
                 "wo", "bo"):
        lay["L0_attn_" + name] = a["L0_attn_" + name]
    for name in ("theta", "phi", "theta_noise", "phi_noise"):
        lay["L0_ffn_" + name] = a["L0_ffn_" + name]
    for name in ("gamma_x", "beta_x", "gamma_l", "beta_l", "Wq", "Wkv", "Wo"):
        lay["L1_xattn_" + name] = a["L1_xattn_" + name]
    lay["L1_xattn_Wq_turned"] = a["L1_xattn_Wq"].reshape(D, -1, 2, 32)[:, :, ::-1].reshape(D, -1)
    for name in ("L1_attn_Wq", "L1_attn_Wk", "L1_attn_Wv", "L1_attn_Wpost", "L1_ffn_Wr", "L1_ffn_W1", "L1_ffn_W2"):
        lay[name] = a[name]
    lay |= constants()
    nc = _bacc.Bacc("TRN2", target_bir_lowering=False, num_devices=1)
    arrays, g = {}, {}
    for name, v in lay.items():
        v = _np.ascontiguousarray(v)
        arrays[f"in_{name}"] = v
        g[name] = nc.dram_tensor(f"in_{name}", v.shape, _mybir.dt.from_np(v.dtype), kind="ExternalInput").ap()
    out = nc.dram_tensor("out", (B * S, D), F32, kind="ExternalOutput").ap()
    program(nc, g, out)
    r = _run(nc, [arrays], core_ids=[0])
    return r.results[0]["out"].reshape(B, S, D)
```
